# Optimizing a Trainium2 kernel written in Bass

```python
import numpy as np
import jax
import jax.numpy as jnp

def _softmax(x, axis=-1):
    return jax.nn.softmax(x, axis=axis)

def _gelu(x):
    return jax.nn.gelu(x, approximate=True)

def _silu(x):
    return jax.nn.silu(x)

def _sigmoid(x):
    return jax.nn.sigmoid(x)

def _layernorm(x, axis=-1, eps=1e-05):
    m = jnp.mean(x, axis=axis, keepdims=True)
    v = jnp.var(x, axis=axis, keepdims=True)
    return (x - m) / jnp.sqrt(v + eps)

def _scatter_add(tgt, idx, src, axis=0):
    return tgt.at[idx].add(src)

def _segment_sum(src, seg, n):
    return jax.ops.segment_sum(src, seg, n)
kernel_name = 'mk_decoder_postln_d1_seqx_r4_12008f'

def setup_inputs(seed: int=0):
    np.random.seed(seed)
    _w = jnp.asarray

    def _rec_inputs():
        import jax
        import jax.numpy as jnp
        _rk = jax.random.key(seed)
        x = -0.0002928 + 1 * jax.random.normal(jax.random.fold_in(_rk, 1), (16, 256, 256), jnp.float32)
        _lenS = 256 - jax.random.randint(jax.random.fold_in(_rk, 7), (16,), 0, max(1, 256 // 4) + 1, jnp.int32)
        _lenS2 = 256 - jax.random.randint(jax.random.fold_in(_rk, 8), (16,), 0, max(1, 256 // 4) + 1, jnp.int32)
        _ctx_1024P = jax.random.normal(jax.random.fold_in(_rk, 11), (16, 16, 256), jnp.float32)
        _ctx_1024c = jax.random.dirichlet(jax.random.fold_in(_rk, 511), 0.3 * jnp.ones((16,), jnp.float32), (16, 256))
        _ctx_1024t = jnp.einsum('bsk,bkd->bsd', _ctx_1024c, _ctx_1024P)
        _ctx_1024t = _ctx_1024t * jax.lax.rsqrt(jnp.mean(jnp.square(_ctx_1024t)) + 1e-12) * 0.953939
        ctx_1024 = -1.39393e-06 + 0.999914 * (_ctx_1024t + 0.3 * jax.random.normal(jax.random.fold_in(_rk, 611), (16, 256, 256), jnp.float32))
        return (x, ctx_1024)
    x, ctx_1024 = _rec_inputs()

    def _L0_attn_setup():
        import jax, jax.numpy as jnp
        import numpy as np
        B_, S_, IN_, H_, N_, K_ = (8, 512, 256, 512, 32, 4)
        key = jax.random.key(seed)
        ks = jax.random.split(key, 8)
        rn = lambda k, shape, s: jax.random.normal(k, shape, jnp.float32) * s
        return {'x': rn(ks[0], (B_, S_, IN_), 1.0), 'W_in': rn(ks[1], (2 * H_, IN_), 0.02), 'b_in': jnp.zeros((2 * H_,), jnp.float32), 'conv_w': rn(ks[2], (H_, 1, K_), 0.1), 'conv_b': jnp.zeros((H_,), jnp.float32), 'W_ssm': rn(ks[3], (N_, H_), 0.02), 'b_ssm': jnp.zeros((N_,), jnp.float32), 'A': -jnp.eye(N_, dtype=jnp.float32), 'Bv': rn(ks[4], (N_,), 0.01), 'Cv': rn(ks[5], (N_,), 0.01), 'Dv': jnp.ones((H_,), jnp.float32), 'W_out': rn(ks[6], (IN_, H_), 0.02), 'b_out': jnp.zeros((IN_,), jnp.float32)}
    _L0_attn_all = _L0_attn_setup()
    _L0_attn_in = {k: v for k, v in _L0_attn_all.items() if k in ('W_in', 'b_in', 'conv_w', 'conv_b', 'W_ssm', 'b_ssm', 'A', 'Bv', 'Cv', 'Dv', 'W_out', 'b_out')}
    del _L0_attn_all

    def _L0_xattn_setup():
        import jax, jax.numpy as jnp
        import numpy as np
        EMBED_DIM = 256
        NUM_HEADS = 16
        HEAD_DIM = EMBED_DIM // NUM_HEADS
        key = jax.random.key(seed)
        ks = jax.random.split(key, 11)
        B, N, C = (2, 512, EMBED_DIM)
        s = 1.0 / np.sqrt(C)
        return {'query': jax.random.normal(ks[0], (B, N, C), jnp.float32), 'key': jax.random.normal(ks[1], (B, N, C), jnp.float32), 'value': jax.random.normal(ks[2], (B, N, C), jnp.float32), 'Wq': jax.random.normal(ks[3], (C, C), jnp.float32) * s, 'bq': jnp.zeros((C,), jnp.float32), 'Wk': jax.random.normal(ks[4], (C, C), jnp.float32) * s, 'bk': jnp.zeros((C,), jnp.float32), 'Wv': jax.random.normal(ks[5], (C, C), jnp.float32) * s, 'bv': jnp.zeros((C,), jnp.float32), 'Wo': jax.random.normal(ks[6], (C, C), jnp.float32) * s, 'bo': jnp.zeros((C,), jnp.float32)}
    _L0_xattn_all = _L0_xattn_setup()
    _L0_xattn_in = {k: v for k, v in _L0_xattn_all.items() if k in ('Wq', 'bq', 'Wk', 'bk', 'Wv', 'bv', 'Wo', 'bo')}
    del _L0_xattn_all

    def _L0_ffn_setup():
        import jax, jax.numpy as jnp
        import numpy as np
        N_EXPERTS = 8
        CAP_FACTOR = 1.25
        BATCH, SEQ, DMODEL, DFF = (4, 512, 256, 1024)
        key = jax.random.key(seed)
        k0, k1, k2, k3 = jax.random.split(key, 4)
        x = jax.random.normal(k0, (BATCH, SEQ, DMODEL), dtype=jnp.float32)
        Wr = jax.random.normal(k1, (DMODEL, N_EXPERTS), dtype=jnp.float32) * 0.02
        W1 = jax.random.normal(k2, (N_EXPERTS, DMODEL, DFF), dtype=jnp.float32) * 0.02
        W2 = jax.random.normal(k3, (N_EXPERTS, DFF, DMODEL), dtype=jnp.float32) * 0.02
        return {'x': x, 'Wr': Wr, 'W1': W1, 'W2': W2}
    _L0_ffn_all = _L0_ffn_setup()
    _L0_ffn_in = {k: v for k, v in _L0_ffn_all.items() if k in ('Wr', 'W1', 'W2')}
    del _L0_ffn_all
    return {'x': x, 'ctx_1024': ctx_1024, 'L0_attn_W_in': _L0_attn_in['W_in'], 'L0_attn_b_in': _L0_attn_in['b_in'], 'L0_attn_conv_w': _L0_attn_in['conv_w'], 'L0_attn_conv_b': _L0_attn_in['conv_b'], 'L0_attn_W_ssm': _L0_attn_in['W_ssm'], 'L0_attn_b_ssm': _L0_attn_in['b_ssm'], 'L0_attn_A': _L0_attn_in['A'], 'L0_attn_Bv': _L0_attn_in['Bv'], 'L0_attn_Cv': _L0_attn_in['Cv'], 'L0_attn_Dv': _L0_attn_in['Dv'], 'L0_attn_W_out': _L0_attn_in['W_out'], 'L0_attn_b_out': _L0_attn_in['b_out'], 'L0_xattn_Wq': _L0_xattn_in['Wq'], 'L0_xattn_bq': _L0_xattn_in['bq'], 'L0_xattn_Wk': _L0_xattn_in['Wk'], 'L0_xattn_bk': _L0_xattn_in['bk'], 'L0_xattn_Wv': _L0_xattn_in['Wv'], 'L0_xattn_bv': _L0_xattn_in['bv'], 'L0_xattn_Wo': _L0_xattn_in['Wo'], 'L0_xattn_bo': _L0_xattn_in['bo'], 'L0_ffn_Wr': _L0_ffn_in['Wr'], 'L0_ffn_W1': _L0_ffn_in['W1'], 'L0_ffn_W2': _L0_ffn_in['W2']}

def reference(x, ctx_1024, L0_attn_W_in, L0_attn_b_in, L0_attn_conv_w, L0_attn_conv_b, L0_attn_W_ssm, L0_attn_b_ssm, L0_attn_A, L0_attn_Bv, L0_attn_Cv, L0_attn_Dv, L0_attn_W_out, L0_attn_b_out, L0_xattn_Wq, L0_xattn_bq, L0_xattn_Wk, L0_xattn_bk, L0_xattn_Wv, L0_xattn_bv, L0_xattn_Wo, L0_xattn_bo, L0_ffn_Wr, L0_ffn_W1, L0_ffn_W2):
    import jax
    import jax.numpy as jnp

    def _L0_attn_ref(x, W_in, b_in, conv_w, conv_b, W_ssm, b_ssm, A, Bv, Cv, Dv, W_out, b_out):
        import jax, jax.numpy as jnp
        import numpy as np
        B_, S_, IN_, H_, N_, K_ = (8, 512, 256, 512, 32, 4)
        resid = x
        xz = x @ W_in.T + b_in
        xh, gate = jnp.split(xz, 2, axis=-1)
        K = conv_w.shape[-1]
        xc = jnp.transpose(xh, (0, 2, 1))
        xc = jax.lax.conv_general_dilated(xc, conv_w, window_strides=(1,), padding=[(K - 1, 0)], dimension_numbers=('NCH', 'OIH', 'NCH'), feature_group_count=xc.shape[1])
        xc = xc + conv_b[None, :, None]
        xh = jax.nn.silu(jnp.transpose(xc, (0, 2, 1)))
        x_ssm = xh @ W_ssm.T + b_ssm

        def step(h, u):
            h = h @ A.T + u * Bv
            return (h, h @ Cv)
        h0 = jnp.zeros((x.shape[0], A.shape[0]), x.dtype)
        _, s = jax.lax.scan(step, h0, jnp.swapaxes(x_ssm, 0, 1))
        s = jnp.swapaxes(s, 0, 1)
        ssm_out = s[..., None] * xh + Dv * xh
        y = ssm_out * jax.nn.silu(gate)
        y = y @ W_out.T + b_out
        return y + resid

    def _L0_xattn_ref(query, key, value, Wq, bq, Wk, bk, Wv, bv, Wo, bo):
        import jax, jax.numpy as jnp
        import numpy as np
        EMBED_DIM = 256
        NUM_HEADS = 16
        HEAD_DIM = EMBED_DIM // NUM_HEADS
        B, N, C = query.shape
        H, D = (NUM_HEADS, HEAD_DIM)
        q = query @ Wq.T + bq
        k = key @ Wk.T + bk
        v = value @ Wv.T + bv
        q = q.reshape(B, N, H, D).transpose(0, 2, 1, 3)
        k = k.reshape(B, N, H, D).transpose(0, 2, 1, 3)
        v = v.reshape(B, N, H, D).transpose(0, 2, 1, 3)
        scores = jnp.einsum('bhqd,bhkd->bhqk', q, k) / jnp.sqrt(jnp.asarray(D, q.dtype))
        attn = jax.nn.softmax(scores, axis=-1)
        out = jnp.einsum('bhqk,bhkd->bhqd', attn, v)
        out = out.transpose(0, 2, 1, 3).reshape(B, N, C)
        return out @ Wo.T + bo

    def _L0_ffn_ref(x, Wr, W1, W2):
        import jax, jax.numpy as jnp
        import numpy as np
        N_EXPERTS = 8
        CAP_FACTOR = 1.25
        BATCH, SEQ, DMODEL, DFF = (4, 512, 256, 1024)
        B, S, D = x.shape
        E = W1.shape[0]
        cap = int(CAP_FACTOR * B * S / E)
        t = x.reshape(-1, D)
        probs = jax.nn.softmax(t @ Wr, axis=-1)
        idx = jnp.argmax(probs, axis=-1)
        pmax = jnp.max(probs, axis=-1)
        onehot = jax.nn.one_hot(idx, E, dtype=jnp.int32)
        pos = jnp.sum(jnp.cumsum(onehot, axis=0) * onehot, axis=-1) - 1
        kept = pos < cap
        flat = idx * cap + jnp.minimum(pos, cap - 1)
        disp = jnp.zeros((E * cap, D), t.dtype).at[flat].add(t * kept[:, None].astype(t.dtype))
        ein = disp.reshape(E, cap, D)
        h = jax.nn.relu(jnp.einsum('ecd,edf->ecf', ein, W1))
        eout = jnp.einsum('ecf,efd->ecd', h, W2).reshape(E * cap, D)
        comb = jnp.where(kept[:, None], eout[flat], t)
        factor = jnp.where(kept, pmax, jnp.ones_like(pmax))
        out = (comb * factor[:, None]).reshape(B, S, D)
        return out
    x = _layernorm(x + _L0_attn_ref(x, L0_attn_W_in, L0_attn_b_in, L0_attn_conv_w, L0_attn_conv_b, L0_attn_W_ssm, L0_attn_b_ssm, L0_attn_A, L0_attn_Bv, L0_attn_Cv, L0_attn_Dv, L0_attn_W_out, L0_attn_b_out), axis=-1)
    x = _layernorm(x + _L0_xattn_ref(x, ctx_1024, ctx_1024, L0_xattn_Wq, L0_xattn_bq, L0_xattn_Wk, L0_xattn_bk, L0_xattn_Wv, L0_xattn_bv, L0_xattn_Wo, L0_xattn_bo), axis=-1)
    x = _layernorm(x + _L0_ffn_ref(x, L0_ffn_Wr, L0_ffn_W1, L0_ffn_W2), axis=-1)
    return x

_drawn_inputs = setup_inputs


def setup_inputs(seed=0):
    import zlib

    import numpy as np

    out = dict(_drawn_inputs(seed))
    spreads = {'L0_attn_b_in': (0.0, 0.1),
     'L0_attn_conv_b': (0.0, 0.1),
     'L0_attn_b_ssm': (0.0, 0.1),
     'L0_attn_Dv': (1.0, 0.2),
     'L0_attn_b_out': (0.0, 0.1),
     'L0_xattn_bq': (0.0, 0.1),
     'L0_xattn_bk': (0.0, 0.1),
     'L0_xattn_bv': (0.0, 0.1),
     'L0_xattn_bo': (0.0, 0.1)}
    factors = {}
    for name, (base, spread) in spreads.items():
        noise = np.random.default_rng([zlib.crc32(name.encode()), seed]).standard_normal(out[name].shape)
        drawn = base * np.exp(spread * noise) if base else spread * noise
        out[name] = jnp.asarray(drawn.astype(out[name].dtype))
    for name, factor in factors.items():
        out[name] = (out[name] * factor).astype(out[name].dtype)
    return out
```

```python
from contextlib import ExitStack

import concourse.bass as bass
from concourse import mybir

F32 = mybir.dt.float32
F32R = mybir.dt.float32r
BF16 = mybir.dt.bfloat16
I32 = mybir.dt.int32
U32 = mybir.dt.uint32
ALU = mybir.AluOpType
ACT = mybir.ActivationFunctionType
AX = mybir.AxisListType

P = 128
B, S, D = 16, 256, 256
H, NS, K = 512, 32, 4
NH, HD = 16, 16
E, CAP, F = 8, 640, 1024
NT = B * S
KD = D // P
MH = H // P
EPS = 1e-5
G = 2
NG = B // G
GT = G * S
L = 16
NC = S // L
Q4 = L // 4
FAR = float(1 << 20)
ROW = D + 2


def need(eng, sem, value):
    if isinstance(value, int) and value <= 0:
        return
    eng.wait_ge(sem, value)


class Steps:

    def __init__(self, eng, sem, per_turn, turn):
        self.eng, self.sem, self.per_turn, self.turn, self.n = eng, sem, per_turn, turn, 0

    def done(self, instruction):
        self.n += 1
        instruction.then_inc(self.sem, 1)
        self.eng.wait_ge(self.sem, self.turn * self.per_turn + self.n)

    def end(self):
        assert self.n == self.per_turn, (self.n, self.per_turn)


def mixer_in(nc, T, PS, sem, c, dram):
    gated, s_all = c["gated"], c["s"]
    w_in = T("w_in", [P, KD, 2 * H], F32)
    w_ssm = T("w_ssm", [P, MH, P], F32)
    bias_in = T("bias_in", [P, 2 * MH], F32)
    bias_cv = T("bias_cv", [P, MH], F32)
    taps = T("taps", [P, MH, K], F32)
    bias_ssm = T("bias_ssm", [P, 1], F32)
    xt = T("xt", [P, 2, KD, GT], F32)
    xpad = T("xpad", [P, 2, G, S + K - 1], F32)
    conv = T("conv", [P, 2, G, S], F32)
    xh = T("xh", [P, 2, MH, GT], F32)
    sgate = T("sgate", [P, MH, GT], F32)
    u = T("u", [P, Q4, NC, B], F32)
    a_rep = T("a_rep", [NS, 2, P], F32)
    a_tr = T("a_tr", [NS, 2, NS], F32)
    b_col = T("b_col", [P, 1], F32)
    pw = T("pw", [P, L, NS], F32)
    cw = T("cw", [P, S], F32)
    gw = T("gw", [P, L], F32)
    w_end = T("w_end", [P, Q4, 4, NS], F32)
    w_loc = T("w_loc", [P, Q4, NS], F32)
    w_lag = T("w_lag", [P, 4, 4, NS], F32)
    ends = T("ends", [P, 4, B], F32)

    ps_xh = PS("ps_xh", [P, 2, 512], F32)
    ps_gate = PS("ps_gate", [P, 2, 512], F32)
    ps_u = PS("ps_u", [P, 512], F32)
    ps_pow = PS("ps_pow", [P, 512], F32)
    ps_end = PS("ps_end", [P, 512], F32)
    ps_s = PS("ps_s", [P, 512], F32)

    w_here, x_here, a_here = sem("w_here"), [sem("x_even"), sem("x_odd")], sem("a_here")
    xh_mm, gate_mm, u_mm = sem("xh_mm"), sem("gate_mm"), sem("u_mm")
    pad_ready, conv_ready, xh_ready = sem("pad_ready"), sem("conv_ready"), sem("xh_ready")
    gate_ready, gated_done, u_ready = sem("gate_ready"), sem("gated_done"), sem("u_ready")
    pads_zero, conv_step = sem("pads_zero"), sem("conv_step")
    pow_mm, pow_copied, tables, zeroed = sem("pow_mm"), sem("pow_copied"), sem("tables"), sem("zeroed")
    end_mm, ends_ready, s_mm, s_ready = sem("end_mm"), sem("ends_ready"), sem("s_mm"), sem("s_ready")

    LEVELS = 8
    n_loads = 6

    with nc.Block() as block:

        @block.sync
        def _(sp):
            sp.dma_start(a_rep[:, 0, :], dram["a_rep"]).then_inc(a_here, 16)
            sp.dma_start(a_tr[:, 0, :], dram["a_tr"]).then_inc(a_here, 16)
            sp.dma_start(cw[:, 0:1], dram["c_rep"]).then_inc(a_here, 16)
            sp.dma_start(b_col[:], dram["b_rep"]).then_inc(a_here, 16)
            sp.dma_start(pw[:, 0, :], dram["eye_rep"]).then_inc(a_here, 16)
            for g in range(2):
                sp.dma_start(xt[:, g], dram["x_t"][:, g * GT:(g + 1) * GT].rearrange("(k p) t -> p k t", p=P)
                             ).then_inc(x_here[g], 16)
            sp.dma_start(w_in[:], dram["w_in"].rearrange("(k p) n -> p k n", p=P)).then_inc(w_here, 16)
            sp.dma_start(bias_in[:], dram["b_in"]).then_inc(w_here, 16)
            sp.dma_start(bias_cv[:], dram["conv_b"]).then_inc(w_here, 16)
            sp.dma_start(taps[:], dram["conv_w"]).then_inc(w_here, 16)
            sp.dma_start(w_ssm[:], dram["w_ssm"].rearrange("(k p) n -> p k n", p=P)).then_inc(w_here, 16)
            sp.dma_start(bias_ssm[:], dram["b_ssm"]).then_inc(w_here, 16)

            def load_x(g, buf):
                sp.wait_ge(gate_mm, MH)
                sp.wait_ge(gate_mm, g * MH - MH)
                sp.dma_start(xt[:, buf], dram["x_t"][:, bass.ds(g * GT, GT)].rearrange("(k p) t -> p k t", p=P)
                             ).then_inc(x_here[buf], 16)

            with sp.Fori(1, NG // 2) as gg:
                load_x(gg * 2, 0)
                load_x(gg * 2 + 1, 1)
            for tile, source in c["loads"]:
                sp.dma_start(tile, source).then_inc(c["loaded"], 16)
            sp.wait_ge(c["blank_ready"], 2)
            sp.dma_start(dram["rows"].rearrange("(t p) r -> p t r", p=P),
                         c["blank"][:, None, :].to_broadcast([P, E * CAP // P, ROW])).then_inc(c["rows_blank"], 16)

        @block.gpsimd
        def _(pool):
            nc.gpsimd.memset(c["blank"][:, 0:D], 0.0).then_inc(c["blank_ready"], 1)
            nc.gpsimd.memset(c["blank"][:, D:ROW], FAR).then_inc(c["blank_ready"], 1)

            def gate_group(g, last):
                for m in range(MH):
                    pool.wait_ge(xh_ready, MH * g + m + 1)
                    pool.wait_ge(gate_ready, MH * g + m + 1)
                    nc.gpsimd.tensor_tensor(gated[:, m, bass.ds(g * GT, GT)], xh[:, last, m, :], sgate[:, m, :],
                                            ALU.mult).then_inc(gated_done, 1)

            with pool.Fori(0, NG // 2) as gg:
                for half in range(2):
                    gate_group(gg * 2 + half, half)

        @block.tensor
        def _(pe):
            pe.wait_ge(a_here, 80)
            for level in range(LEVELS):
                n = 1 << level
                cur, mats = level % 2, level < 4
                if level:
                    pe.wait_ge(pow_copied, level)
                pe.matmul(ps_pow[:, 0:n], a_rep[:, cur, :], cw[0:NS, 0:n], start=True, stop=True,
                          skip_group_check=True)
                if mats:
                    pe.matmul(ps_end[:, 0:n * NS], a_rep[:, cur, :],
                              pw[0:NS, 0:n, :].rearrange("p k n -> p (k n)"), start=True, stop=True,
                              skip_group_check=True)
                pe.matmul(ps_s[0:NS, 0:P], a_tr[:, cur, :], a_rep[:, cur, :], start=True, stop=True,
                          skip_group_check=True)
                pe.matmul(ps_s[0:NS, P:P + NS], a_rep[:, cur, 0:NS], a_tr[:, cur, :], start=True, stop=True,
                          skip_group_check=True).then_inc(pow_mm, 1)
            pe.wait_ge(w_here, 16 * n_loads)

            def project(g, buf):
                pe.wait_ge(x_here[buf], g * 8 + (16 if buf == 0 else 8))
                for m in range(MH):
                    need(pe, pad_ready, MH * g + m - 1)
                    for k in range(KD):
                        mm = pe.matmul(ps_xh[:, m % 2, :], w_in[:, k, m * P:(m + 1) * P], xt[:, buf, k, :],
                                       start=(k == 0), stop=(k == KD - 1))
                    mm.then_inc(xh_mm, 1)
                for m in range(MH):
                    need(pe, gate_ready, MH * g + m - 1)
                    for k in range(KD):
                        mm = pe.matmul(ps_gate[:, m % 2, :], w_in[:, k, H + m * P:H + (m + 1) * P], xt[:, buf, k, :],
                                       start=(k == 0), stop=(k == KD - 1))
                    mm.then_inc(gate_mm, 1)

            def inject(g, buf):
                need(pe, u_ready, g)
                for m in range(MH):
                    pe.wait_ge(xh_ready, MH * g + m + 1)
                    mm = pe.matmul(ps_u[:, :], w_ssm[:, m, :], xh[:, buf, m, :], start=(m == 0), stop=(m == MH - 1))
                mm.then_inc(u_mm, 1)

            project(0, 0)
            project(1, 1)
            inject(0, 0)
            with pe.Fori(1, NG // 2) as gg:
                project(gg * 2, 0)
                inject(gg * 2 - 1, 1)
                project(gg * 2 + 1, 1)
                inject(gg * 2, 0)
            inject(NG - 1, 1)

            pe.wait_ge(u_ready, NG)
            pe.wait_ge(tables, 1)
            for q in range(Q4):
                mm = pe.matmul(ps_end[:, 0:NC * B], w_end[:, q].rearrange("p r n -> p (r n)"),
                               u[:, q].rearrange("p c b -> p (c b)"), start=(q == 0), stop=(q == Q4 - 1))
            mm.then_inc(end_mm, 1)
            uc = u[:].rearrange("p q (cq c4) b -> p q c4 cq b", c4=4)
            for c4 in range(4):
                for q in range(Q4):
                    pe.matmul(ps_s[NS * c4:NS * (c4 + 1), 0:4 * B], w_loc[:, q, :], uc[:, q, c4],
                              start=(q == 0), stop=False, skip_group_check=True)
            pe.wait_ge(ends_ready, 1)
            for lag in range(4):
                mm = pe.matmul(ps_s[:, lag * B:4 * B], w_lag[:, lag].rearrange("p c n -> p (c n)"),
                               ends[:, 0:4 - lag, :].rearrange("p c b -> p (c b)"),
                               start=False, stop=(lag == 3), skip_group_check=True)
            mm.then_inc(s_mm, 1)

        @block.scalar
        def _(act):
            act.wait_ge(w_here, 16 * n_loads)
            act.wait_ge(pads_zero, 1)

            def silus(g, buf):
                for m in range(MH):
                    act.wait_ge(xh_mm, MH * g + m + 1)
                    need(act, conv_ready, MH * g + m - 1)
                    nc.scalar.activation(xpad[:, m % 2, :, K - 1:], ps_xh[:, m % 2, :].rearrange("p (b t) -> p b t", b=G),
                                         ACT.Identity, bias=bias_in[:, m:m + 1]).then_inc(pad_ready, 1)
                    if m >= 1:
                        xh_of(g, buf, m - 1)
                for m in range(MH):
                    act.wait_ge(gate_mm, MH * g + m + 1)
                    need(act, gated_done, MH * (g - 1) + m + 1)
                    nc.scalar.activation(sgate[:, m, :], ps_gate[:, m % 2, :], ACT.Silu,
                                         bias=bias_in[:, MH + m:MH + m + 1]).then_inc(gate_ready, 1)
                    if m == 0:
                        xh_of(g, buf, MH - 1)
                if not isinstance(g, int) or g >= 1:
                    inject_out(g - 1)

            def xh_of(g, buf, m):
                act.wait_ge(conv_ready, MH * g + m + 1)
                need(act, gated_done, MH * (g - 2) + m + 1)
                need(act, u_mm, g - 1)
                nc.scalar.activation(xh[:, buf, m, :], conv[:, m % 2].rearrange("p b t -> p (b t)"), ACT.Silu
                                     ).then_inc(xh_ready, 1)

            def inject_out(g):
                act.wait_ge(u_mm, g + 1)
                src = ps_u[:].rearrange("p (b c q r) -> p r q c b", b=G, c=NC, q=Q4)
                for r in range(4):
                    rows = slice(NS * r, NS * (r + 1))
                    op = nc.scalar.activation(u[rows, :, :, bass.ds(g * G, G)], src[rows, r], ACT.Identity,
                                              bias=bias_ssm[rows, :])
                op.then_inc(u_ready, 1)

            silus(0, 0)
            silus(1, 1)
            with act.Fori(1, NG // 2) as gg:
                silus(gg * 2, 0)
                silus(gg * 2 + 1, 1)
            inject_out(NG - 1)

        @block.vector
        def _(dve):
            nc.vector.memset(w_loc[:], 0.0).then_inc(zeroed, 1)
            nc.vector.memset(w_lag[:], 0.0).then_inc(zeroed, 1)
            nc.vector.memset(xpad[:, :, :, 0:K - 1], 0.0).then_inc(pads_zero, 1)
            for level in range(LEVELS):
                n = 1 << level
                nxt = (level + 1) % 2
                dve.wait_ge(pow_mm, level + 1)
                if n < S:
                    hi = min(2 * n, S)
                    last = nc.vector.tensor_copy(cw[:, n:hi], ps_pow[:, 0:hi - n])
                if level < 4:
                    last = nc.vector.tensor_copy(pw[:, n:2 * n, :].rearrange("p k n -> p (k n)"), ps_end[:, 0:n * NS])
                if level < LEVELS - 1:
                    nc.vector.tensor_copy(a_rep[:, nxt, :], ps_s[0:NS, 0:P])
                    last = nc.vector.tensor_copy(a_tr[:, nxt, :], ps_s[0:NS, P:P + NS])
                last.then_inc(pow_copied, 1)
            dve.wait_ge(pow_copied, LEVELS)
            dve.wait_ge(zeroed, 2)
            nc.vector.tensor_scalar(gw[:], cw[:, 0:L], b_col[:, 0:1], None, ALU.mult).then_inc(zeroed, 1)
            dve.wait_ge(zeroed, 3)
            for r in range(4):
                rows = slice(NS * r, NS * (r + 1))
                for q in range(Q4):
                    i = 4 * q + r
                    nc.vector.tensor_scalar(w_end[rows, q], pw[rows, L - 1 - i:L - i, :].to_broadcast([NS, 4, NS]),
                                            b_col[rows, 0:1], None, ALU.mult)
                    nc.vector.tensor_copy(w_loc[rows, q, i:L], gw[rows, 0:L - i])
                lags = w_lag[rows].rearrange("p a b n -> p (a b) n")
                last = nc.vector.tensor_copy(lags[:, r + 1:, 0:L],
                                             cw[rows, 1:1 + L * (L - 1 - r)].rearrange("p (l i) -> p l i", i=L))
            last.then_inc(tables, 1)

            def convolve(g):
                for m in range(MH):
                    b = m % 2
                    dve.wait_ge(pad_ready, MH * g + m + 1)
                    need(dve, xh_ready, MH * g + m - 1)
                    st = Steps(dve, conv_step, MH * (K - 1), g)
                    st.n = m * (K - 1)
                    st.done(nc.vector.tensor_scalar(conv[:, b], xpad[:, b, :, 0:S], taps[:, m, 0:1],
                                                    bias_cv[:, m:m + 1], ALU.mult, ALU.add))
                    for k in range(1, K):
                        op = nc.vector.scalar_tensor_tensor(conv[:, b], xpad[:, b, :, k:k + S], taps[:, m, k:k + 1],
                                                            conv[:, b], ALU.mult, ALU.add)
                        if k < K - 1:
                            st.done(op)
                    op.then_inc(conv_ready, 1)

            dve.wait_ge(w_here, 16 * n_loads)
            convolve(0)
            with dve.Fori(1, NG) as g:
                convolve(g)
            dve.wait_ge(end_mm, 1)
            for c4 in range(4):
                rows = slice(NS * c4, NS * (c4 + 1))
                last = nc.vector.tensor_copy(ends[rows], ps_end[rows, 0:NC * B].rearrange(
                    "p (cq c4 b) -> p c4 cq b", c4=4, b=B)[:, c4])
            last.then_inc(ends_ready, 1)
            dve.wait_ge(s_mm, 1)
            nc.vector.tensor_copy(s_all[:], ps_s[:, 0:4 * B].rearrange("p (c b) -> p c b", b=B)).then_inc(s_ready, 1)
            dve.wait_ge(s_ready, 1)
            dve.wait_ge(gated_done, MH * NG)


def attend(nc, T, PS, sem, c, dram):
    gated, s_all = c["gated"], c["s"]
    w, eye, ones, mask = c["w"], c["eye"], c["ones"], c["mask"]
    KT = S // P
    RM = 4 * HD
    HH = NH // 2
    VW = 2 * HD
    SCALE = HD ** -0.5

    xres = T("xres", [P, KT, D], F32)
    ctx = T("ctx", [P, 2, KD, S], F32)
    diag = T("diag", [P, 4, 64], F32)
    y = T("y", [P, MH, S], F32)
    r1 = T("r1", [P, KT, D], F32)
    x1 = T("x1", [P, 2, KT, D], F32)
    x1t = T("x1t", [P, KD, S], F32)
    half = T("half", [P, 2, KD, S], F32R)
    qst = T("qst", [P, 2, NH, S], F32R)
    kst = T("kst", [P, 2, NH, S], F32R)
    vals = T("vals", [P, 2, KT, NH, VW], F32)
    nmax = T("nmax", [P, KT, NH], F32)
    mrow = T("mrow", [NH, S], F32R)
    zrow = T("zrow", [HH, S], F32)
    pt = T("pt", [P, 2, KT, S], F32)
    oraw = T("oraw", [P, 4, S], F32)
    rec = T("rec", [P, NH], F32)
    onrm = T("onrm", [P, KT, D], F32)
    ont = T("ont", [P, KD, S], F32)
    x2t = T("x2t", [P, KD, S], F32)
    pay = T("pay", [P, 2, KT, ROW], F32)
    st1, mv1, ve1 = T("st1", [P, KT, 6], F32), T("mv1", [P, KT, 2], F32), T("ve1", [P, KT], F32)
    st2, mv2, ve2 = T("st2", [P, KT, 6], F32), T("mv2", [P, KT, 2], F32), T("ve2", [P, KT], F32)
    st3, mv3, ve3 = T("st3", [P, KT, 6], F32), T("mv3", [P, KT, 2], F32), T("ve3", [P, KT], F32)
    power = T("power", [P, KT], F32)
    lg, top, where = T("lg", [P, KT, E], F32), T("top", [P, KT, 8], F32), T("where", [P, KT, 8], U32)
    ntop, den, expert = T("ntop", [P, KT], F32), T("den", [P, KT], F32), T("expert", [P, KT], F32)
    el = T("el", [P, KT, E], F32)
    hot, carry = T("hot", [P, KT, E], BF16), T("carry", [P, E], BF16)
    tri, ones_b = T("tri", [P, P], BF16), T("ones_b", [P, P], BF16)
    sel, place = T("sel", [P, KT, E], F32), T("place", [P, KT], F32)
    over, slot0, slot = T("over", [P, KT], F32), T("slot0", [P, KT], F32), T("slot", [P, KT], F32)
    dest = T("dest", [P, 2, KT], I32)
    bq = T("bq", [P, KD], F32)

    ps_m = PS("ps_m", [P, 2, KT, S], F32)
    ps_a = PS("ps_a", [P, 2, KT, S], F32)
    ps_o = PS("ps_o", [P, 4, S], F32)
    ps_d = PS("ps_d", [P, 512], F32)
    ps_e = PS("ps_e", [P, 512], F32)
    hscr = c["hscr"]

    names = """setup_pool setup_dve setup_pe vo_row x_in0 x_in1 ctx_in0 ctx_in1 x_added
        sbc_mm k_mm v_mm wout_mm x1t_mm q_mm mt_mm diag_done y_done k_hi q_hi k_split q_split v_out r1_done var1_ready
        rstd1 x1_done x1_kept x1t_out m_out k_stored q_stored k_in00 k_in01 k_in10 k_in11 q_in00 q_in01 q_in10 q_in11 m_in
        row_zero0 row_zero1 max_mm max_done att_mm exp_done pv_mm oraw_out ot_mm on_done ont_mm ont_out oproj_mm r2_done
        var2_ready rstd2 x2_done x2t_mm x2t_out logit_mm lg_out den_done hot_ready cum_mm carry_ready
        var3_ready rstd3 dest_ready place_done pay_ready sent0 sent1 out_ready out_sent0 out_sent1
        d_step o_step p_step stats1 stats2 stats3""".split()
    s = {n: sem(n) for n in names}
    x_in, ctx_in = [s["x_in0"], s["x_in1"]], [s["ctx_in0"], s["ctx_in1"]]
    k_in, q_in = ([[s[n + str(b) + str(lo)] for lo in range(2)] for b in range(2)] for n in ("k_in", "q_in"))
    row_zero = [s["row_zero0"], s["row_zero1"]]
    sent, out_sent = [s["sent0"], s["sent1"]], [s["out_sent0"], s["out_sent1"]]

    FIRST, STEPS_N = 5, B + 3

    def run(eng, step):
        for n in range(FIRST):
            step(n, n % 2)
        with eng.Fori(0, (B - 1 - FIRST) // 2) as i:
            step(i * 2 + FIRST, FIRST % 2)
            step(i * 2 + FIRST + 1, (FIRST + 1) % 2)
        for n in range(B - 1, STEPS_N):
            step(n, n % 2)

    def on(n, lag):
        return not isinstance(n, int) or 0 <= n - lag < B

    def use(j, per, parity):
        if isinstance(j, int):
            return (j // 2 + 1) * per
        return j * (per // 2) + (per if parity == 0 else per // 2)

    def settled(eng):
        eng.wait_ge(s["setup_pe"], 1)

    with nc.Block() as block:

        @block.sync
        def _(sp):
            def load(j, p):
                if not isinstance(j, int) or j > 0:
                    settled(sp)
                need(sp, s["x_added"], j)
                sp.dma_start(xres[:], dram["x"][bass.ds(j * S, S), :].rearrange("(t p) d -> p t d", p=P)
                             ).then_inc(x_in[p], 16)
                if not isinstance(j, int) or j > 0:
                    settled(sp)
                need(sp, s["k_mm"], j - 1)
                need(sp, s["v_mm"], j - 1)
                sp.dma_start(ctx[:, p], dram["ctx_t"][:, bass.ds(j * S, S)].rearrange("(k p) t -> p k t", p=P)
                             ).then_inc(ctx_in[p], 16)

            load(0, 0)

            def step(n, p):
                if on(n, 0):
                    sp.wait_ge(s["k_split"], n + 1)
                    if not isinstance(n, int) or n >= 1:
                        for lo in range(2):
                            sp.wait_ge(k_in[1 - p][lo], use(n - 1, 64, 1 - p))
                            sp.wait_ge(q_in[1 - p][lo], use(n - 1, 64, 1 - p))
                    sp.dma_start(hscr[0].rearrange("c (m p) t -> p c m t", p=P), half[:].bitcast(F32)
                                 ).then_inc(s["k_stored"], 16)
                    sp.wait_ge(s["k_stored"], n * 16 + 16)
                if on(n, 0) and (not isinstance(n, int) or n + 1 < B):
                    load(n + 1, 1 - p)
                if on(n, 0):
                    sp.wait_ge(s["q_split"], n + 1)
                    sp.dma_start(hscr[1].rearrange("c (m p) t -> p c m t", p=P), half[:].bitcast(F32)
                                 ).then_inc(s["q_stored"], 16)
                    sp.wait_ge(s["q_stored"], n * 16 + 16)
                    for lo in range(2):
                        need(sp, s["att_mm"], (n - 2) * NH + HH * (lo + 1))
                        for buf, src, order, got in ((kst, 0, (0, 1, 0, 1), k_in), (qst, 1, (0, 0, 1, 1), q_in)):
                            if buf is qst and on(n, 2):
                                sp.dma_start(qst[RM:RM + 1, p, HH * lo:HH * (lo + 1), :].bitcast(F32), zrow[:]
                                             ).then_inc(row_zero[lo], 16)
                            for r, h in enumerate(order):
                                sp.dma_start(buf[HD * r:HD * (r + 1), p, HH * lo:HH * (lo + 1), :].bitcast(F32),
                                             hscr[src, h].rearrange("(h d) t -> d h t", d=HD)[:, HH * lo:HH * (lo + 1), :]
                                             ).then_inc(got[p][lo], 16)
                if on(n, 1):
                    sp.wait_ge(s["m_out"], n)
                    sp.dma_start(qst[RM:RM + 1, 1 - p, :, :].bitcast(F32), mrow[:].bitcast(F32)
                                 ).then_inc(s["m_in"], 16)
                if on(n, 3):
                    settled(sp)
                    sp.wait_ge(s["out_ready"], n - 2)
                    sp.dma_start(dram["out"][bass.ds((n - 3) * S, S), :].rearrange("(t p) d -> p t d", p=P),
                                 c["twice"][:, 1 - p]).then_inc(out_sent[1 - p], 16)

            run(sp, step)
            sp.wait_ge(out_sent[0], B // 2 * 16)
            sp.wait_ge(out_sent[1], B // 2 * 16)

        @block.gpsimd
        def _(pool):
            nc.gpsimd.memset(power[:], -0.5).then_inc(s["setup_pool"], 1)
            nc.gpsimd.memset(zrow[:], 0.0).then_inc(s["setup_pool"], 1)
            pool.wait_ge(s["setup_pool"], 2)
            nc.gpsimd.memset(qst[RM:P, :, :, :].bitcast(F32), 0.0).then_inc(s["setup_pool"], 1)
            nc.gpsimd.memset(kst[RM:P, :, :, :].bitcast(F32), 0.0).then_inc(s["setup_pool"], 1)
            pool.wait_ge(s["setup_pool"], 4)
            nc.gpsimd.memset(kst[RM:RM + 1, :, :, :].bitcast(F32), 1.0).then_inc(s["setup_pool"], 1)
            pool.wait_ge(s["setup_pool"], 5)
            pool.wait_ge(c["rows_blank"], 16)

            def step(n, p):
                if on(n, 0):
                    pool.wait_ge(x_in[p], use(n, 16, p))
                    own = Steps(pool, s["p_step"], 1, n)
                    need(pool, s["r1_done"], n)
                    own.done(nc.gpsimd.tensor_tensor(c["x2b"][:], xres[:],
                                                    c["b_out"][:, None, :].to_broadcast([P, KT, D]), ALU.add))
                    nc.gpsimd.tensor_tensor(c["x2b"][:], c["x2b"][:], xres[:], ALU.add).then_inc(s["x_added"], 1)
                    pool.wait_ge(s["var1_ready"], n + 1)
                    nc.gpsimd.tensor_tensor(ve1[:], ve1[:], power[:], ALU.pow).then_inc(s["rstd1"], 1)
                if on(n, 3):
                    pool.wait_ge(s["var2_ready"], n - 2)
                    nc.gpsimd.tensor_tensor(ve2[:], ve2[:], power[:], ALU.pow).then_inc(s["rstd2"], 1)
                if on(n, 0):
                    pool.wait_ge(s["x1_done"], n + 1)
                    if isinstance(n, int) and n == 0:
                        pool.wait_ge(s["vo_row"], 1)
                    nc.gpsimd.tensor_tensor(gated[:, 0:KT, bass.ds(n * S, S)], x1[:, p],
                                            c["b_o"][:, None, :].to_broadcast([P, KT, D]), ALU.add
                                            ).then_inc(s["x1_kept"], 1)
                if on(n, 3):
                    pool.wait_ge(s["var3_ready"], n - 2)
                    nc.gpsimd.tensor_tensor(ve3[:], ve3[:], power[:], ALU.pow).then_inc(s["rstd3"], 1)
                if on(n, 3):
                    j, jp = n - 3, 1 - p
                    settled(pool)
                    pool.wait_ge(s["dest_ready"], j + 1)
                    pool.wait_ge(s["pay_ready"], j + 1)
                    for t in range(KT):
                        nc.gpsimd.indirect_dma_start(
                            out=dram["rows"], out_offset=bass.IndirectOffsetOnAxis(ap=dest[:, jp, t:t + 1], axis=0),
                            in_=pay[:, jp, t, :], in_offset=None, bounds_check=E * CAP - 1, oob_is_err=False,
                        ).then_inc(sent[jp], 16)

            run(pool, step)
            pool.wait_ge(sent[0], B // 2 * KT * 16)
            pool.wait_ge(sent[1], B // 2 * KT * 16)

        @block.tensor
        def _(pe):
            pe.wait_ge(c["loaded"], 16 * len(c["loads"]))
            for k in range(KD):
                mm = pe.matmul(ps_d[:, 0:D], c["bv_rep"][:, k, :], w["o"][:, k, :], start=(k == 0), stop=(k == KD - 1))
            mm.then_inc(s["setup_pe"], 1)
            pe.wait_ge(s["setup_dve"], 6)
            pe.wait_ge(s["setup_pool"], 5)

            def spread_s(j, p):
                pe.wait_ge(s["diag_done"], j + 1)
                need(pe, s["m_out"], j - 1)
                pe.matmul(ps_d[:, 0:S], ones[:], diag[:].rearrange("p c i -> p (c i)"), start=True, stop=True
                          ).then_inc(s["sbc_mm"], 1)

            def keys(j, p):
                pe.wait_ge(ctx_in[p], use(j, 16, p))
                pe.wait_ge(s["y_done"], j + 1)
                for m in range(KD):
                    for k in range(KD):
                        mm = pe.matmul(ps_d[:, m * S:(m + 1) * S], w["k"][:, k, m * P:(m + 1) * P], ctx[:, p, k, :],
                                       start=(k == 0), stop=(k == KD - 1), skip_group_check=True)
                mm.then_inc(s["k_mm"], 1)

            def values(j, p, dense):
                if dense is not None:
                    pe.wait_ge(s["k_split"], dense + 1)
                for t in range(KT):
                    for k in range(KD):
                        mm = pe.matmul(ps_d[:, t * D:(t + 1) * D], ctx[:, p, k, t * P:(t + 1) * P], w["v"][:, k, :],
                                       start=(k == 0), stop=(k == KD - 1), skip_group_check=True)
                mm.then_inc(s["v_mm"], 1)

            def mixer_out(j, p):
                need(pe, s["v_out"], j)
                pe.wait_ge(s["k_split"], j + 1)
                for t in range(KT):
                    for m in range(MH):
                        mm = pe.matmul(ps_d[:, t * D:(t + 1) * D], y[:, m, t * P:(t + 1) * P], w["out"][:, m, :],
                                       start=(m == 0), stop=(m == MH - 1), skip_group_check=True)
                mm.then_inc(s["wout_mm"], 1)

            def turn(ps, src, done):
                for t in range(KT):
                    for k in range(KD):
                        mm = pe.transpose(ps[:, k * S + t * P:k * S + (t + 1) * P], src[:, t, k * P:(k + 1) * P], eye[:])
                mm.then_inc(done, 1)

            def queries(j, p):
                pe.wait_ge(s["x1t_out"], j + 1)
                for m in range(KD):
                    for k in range(KD):
                        mm = pe.matmul(ps_d[:, m * S:(m + 1) * S], w["q"][:, k, m * P:(m + 1) * P], x1t[:, k, :],
                                       start=(k == 0), stop=(k == KD - 1), skip_group_check=True)
                mm.then_inc(s["q_mm"], 1)

            def maxima_rows(j, dense):
                pe.wait_ge(s["max_done"], NH * j + NH)
                if dense is not None:
                    pe.wait_ge(s["q_split"], dense + 1)
                for t in range(KT):
                    mm = pe.transpose(ps_d[0:NH, t * P:(t + 1) * P], nmax[:, t, :], eye[:])
                mm.then_inc(s["mt_mm"], 1)

            def scores(j, p, h):
                if h % HH == 0:
                    pe.wait_ge(q_in[p][h // HH], use(j, 64, p))
                    pe.wait_ge(k_in[p][h // HH], use(j, 64, p))
                    need(pe, row_zero[h // HH], 16 * (j - 1))
                need(pe, s["max_done"], NH * j + h - 1)
                for t in range(KT):
                    mm = pe.matmul(ps_m[:, h % 2, t, :], qst[:, p, h, t * P:(t + 1) * P], kst[:, p, h, :],
                                   start=True, stop=True, skip_group_check=True)
                mm.then_inc(s["max_mm"], 1)

            def scores_t(j, p, h):
                if h == 0:
                    pe.wait_ge(s["m_in"], j * 16 + 16)
                need(pe, s["exp_done"], NH * j + h - 1)
                for t in range(KT):
                    mm = pe.matmul(ps_a[:, h % 2, t, :], kst[:, p, h, t * P:(t + 1) * P], qst[:, p, h, :],
                                   start=True, stop=True, skip_group_check=True)
                mm.then_inc(s["att_mm"], 1)

            def weigh(j, p, h):
                pe.wait_ge(s["exp_done"], NH * j + h + 1)
                if h == 0:
                    pe.wait_ge(s["v_out"], j + 1)
                    need(pe, s["oraw_out"], j)
                for t in range(KT):
                    mm = pe.matmul(ps_o[VW * (h % 4):VW * (h % 4 + 1), h // 4, :], vals[:, p, t, h, :],
                                   pt[:, h % 2, t, :],
                                   start=(t == 0), stop=(t == KT - 1), skip_group_check=True)
                mm.then_inc(s["pv_mm"], 1)

            def sums_by_query(j, t):
                if t == 0:
                    pe.wait_ge(s["oraw_out"], j + 1)
                    need(pe, s["place_done"], j)
                else:
                    pe.wait_ge(s["on_done"], 2 * j + 1)
                for g in range(4):
                    mm = pe.transpose(ps_e[:, g * P:(g + 1) * P], oraw[:, g, t * P:(t + 1) * P], eye[:])
                mm.then_inc(s["ot_mm"], 1)

            def project_out(j):
                pe.wait_ge(s["ont_out"], j + 1)
                for t in range(KT):
                    for k in range(KD):
                        mm = pe.matmul(ps_e[:, t * D:(t + 1) * D], ont[:, k, t * P:(t + 1) * P], w["o"][:, k, :],
                                       start=(k == 0), stop=(k == KD - 1), skip_group_check=True)
                mm.then_inc(s["oproj_mm"], 1)

            def router(j):
                pe.wait_ge(s["x2t_out"], j + 1)
                for t in range(KT):
                    for k in range(KD):
                        mm = pe.matmul(ps_e[:, t * E:(t + 1) * E], x2t[:, k, t * P:(t + 1) * P], w["r"][:, k, :],
                                       start=(k == 0), stop=(k == KD - 1), skip_group_check=True)
                mm.then_inc(s["logit_mm"], 1)

            def count(j):
                pe.wait_ge(s["hot_ready"], j + 1)
                need(pe, s["carry_ready"], j)
                for t in range(KT):
                    here = ps_e[:, t * E:(t + 1) * E]
                    pe.matmul(here, tri[:], hot[:, t, :], start=True, stop=False, skip_group_check=True)
                    if t:
                        pe.matmul(here, ones_b[:], hot[:, 0, :], start=False, stop=False, skip_group_check=True)
                    mm = pe.matmul(here, ones_b[:], carry[:], start=False, stop=True, skip_group_check=True)
                mm.then_inc(s["cum_mm"], 1)

            def step(n, p):
                q = 1 - p
                for h in range(NH + 2):
                    if h < NH and on(n, 1):
                        scores(n - 1, q, h)
                    if h < NH and on(n, 2):
                        scores_t(n - 2, p, h)
                    if h == 0 and on(n, 0):
                        spread_s(n, p)
                    if h == 1 and on(n, 0):
                        keys(n, p)
                    if h == 3 and on(n, 1):
                        values(n - 1, q, n if on(n, 0) else None)
                    if h == 4 and on(n, 0):
                        mixer_out(n, p)
                    if h == 8 and on(n, 0):
                        pe.wait_ge(s["x1_done"], n + 1)
                        turn(ps_d, x1[:, p], s["x1t_mm"])
                    if h == 9 and on(n, 0):
                        queries(n, p)
                    if on(n, 3):
                        if h == 1:
                            sums_by_query(n - 3, 0)
                        if h == 2:
                            sums_by_query(n - 3, 1)
                        if h == 4:
                            pe.wait_ge(s["on_done"], 2 * (n - 3) + 2)
                            turn(ps_e, onrm, s["ont_mm"])
                        if h == 5:
                            project_out(n - 3)
                        if h == 9:
                            pe.wait_ge(s["x2_done"], n - 2)
                            turn(ps_e, pay[:, q], s["x2t_mm"])
                        if h == 10:
                            router(n - 3)
                        if h == 14:
                            count(n - 3)
                    if h >= 2 and on(n, 2):
                        weigh(n - 2, p, h - 2)
                if on(n, 1):
                    maxima_rows(n - 1, n if on(n, 0) else None)

            run(pe, step)

        @block.scalar
        def _(act):
            act.wait_ge(c["loaded"], 16 * len(c["loads"]))

            def split_hi(bias, out):
                for m in range(KD):
                    op = nc.scalar.activation(half[:, 0, m, :], ps_d[:, m * S:(m + 1) * S], ACT.Identity,
                                              bias=bias[:, m:m + 1])
                op.then_inc(out, 1)

            def step(n, p):
                q = 1 - p
                for h in range(NH + 2):
                    if h == 0 and on(n, 3):
                        j = n - 3
                        act.wait_ge(s["pv_mm"], NH * j + NH)
                        need(act, s["ot_mm"], 2 * j)
                        nc.scalar.copy(oraw[:].rearrange("p g t -> p (g t)"), ps_o[:].rearrange("p g t -> p (g t)")
                                       ).then_inc(s["oraw_out"], 1)
                    if h == 2 and on(n, 0):
                        act.wait_ge(s["k_mm"], n + 1)
                        need(act, s["q_stored"], 16 * n)
                        split_hi(c["b_k"], s["k_hi"])
                    if h == 4 and on(n, 1):
                        act.wait_ge(s["v_mm"], n)
                        need(act, s["pv_mm"], NH * (n - 2))
                        nc.scalar.copy(vals[:, q, :, :, 0:HD], ps_d[:].rearrange("p (t h d) -> p t h d", t=KT, h=NH)
                                       ).then_inc(s["v_out"], 1)
                    if h == 5 and on(n, 3):
                        act.wait_ge(s["ont_mm"], n - 2)
                        nc.scalar.copy(ont[:].rearrange("p k t -> p (k t)"), ps_e[:]).then_inc(s["ont_out"], 1)
                    if h == 9 and on(n, 0):
                        act.wait_ge(s["x1t_mm"], n + 1)
                        nc.scalar.copy(x1t[:].rearrange("p k t -> p (k t)"), ps_d[:]).then_inc(s["x1t_out"], 1)
                    if h == 10 and on(n, 3):
                        act.wait_ge(s["x2t_mm"], n - 2)
                        nc.scalar.copy(x2t[:].rearrange("p k t -> p (k t)"), ps_e[:]).then_inc(s["x2t_out"], 1)
                    if h == 10 and on(n, 0):
                        act.wait_ge(s["q_mm"], n + 1)
                        act.wait_ge(s["k_stored"], 16 * n + 16)
                        if isinstance(n, int) and n == 0:
                            act.wait_ge(s["setup_dve"], 6)
                        split_hi(bq, s["q_hi"])
                    if h == 13 and on(n, 3):
                        j = n - 3
                        act.wait_ge(s["lg_out"], 2 * j + 2)
                        need(act, s["pay_ready"], j)
                        for t in range(KT):
                            op = nc.scalar.activation(el[:, t, :], lg[:, t, :], ACT.Exp, bias=ntop[:, t:t + 1],
                                                      accum_out=den[:, t:t + 1])
                        op.then_inc(s["den_done"], 1)
                    if h < NH and on(n, 2):
                        j = n - 2
                        act.wait_ge(s["att_mm"], NH * j + h + 1)
                        need(act, s["pv_mm"], NH * j + h - 1)
                        nc.scalar.activation(pt[:, h % 2].rearrange("p t q -> p (t q)"),
                                             ps_a[:, h % 2].rearrange("p t q -> p (t q)"), ACT.Exp
                                             ).then_inc(s["exp_done"], 1)
                if on(n, 1):
                    act.wait_ge(s["mt_mm"], n)
                    need(act, s["m_in"], 16 * (n - 1))
                    nc.scalar.copy(mrow[:], ps_d[0:NH, 0:S]).then_inc(s["m_out"], 1)

            run(act, step)

        @block.vector
        def _(dve):
            nc.vector.memset(vals[:, :, :, :, HD:VW], 1.0).then_inc(s["setup_dve"], 1)
            nc.vector.memset(carry[:], 0.0).then_inc(s["setup_dve"], 1)
            dve.wait_ge(c["loaded"], 16 * len(c["loads"]))
            nc.vector.tensor_scalar(w["q"][:], w["q"][:], SCALE, None, ALU.mult).then_inc(s["setup_dve"], 1)
            nc.vector.tensor_scalar(bq[:], c["b_q"][:], SCALE, None, ALU.mult).then_inc(s["setup_dve"], 1)
            nc.vector.tensor_copy(tri[:], c["tri"][:]).then_inc(s["setup_dve"], 1)
            nc.vector.tensor_copy(ones_b[:], ones[:]).then_inc(s["setup_dve"], 1)
            dve.wait_ge(s["setup_pe"], 1)
            nc.vector.tensor_tensor(c["b_o"][:], c["b_o"][:], ps_d[:, 0:D], ALU.add).then_inc(s["vo_row"], 1)
            dve.wait_ge(s["setup_dve"], 6)
            dve.wait_ge(s["setup_pool"], 5)
            dve.wait_ge(s["vo_row"], 1)

            def lo_half(bias, hi, out, j):
                dve.wait_ge(hi, j + 1)
                for m in range(KD):
                    op = nc.vector.scalar_tensor_tensor(half[:, 1, m, :], ps_d[:, m * S:(m + 1) * S], bias[:, m:m + 1],
                                                        half[:, 0, m, :].bitcast(F32), ALU.add, ALU.subtract)
                op.then_inc(out, 1)

            def stats(chain, st, mv, src, stats_done, batch):
                for t in range(KT):
                    op = nc.vector.bn_stats(st[:, t, :], src[:, t, 0:D])
                op.then_inc(stats_done, 1)
                dve.wait_ge(s["vo_row"], 1)
                dve.wait_ge(stats_done, batch + 1)
                for t in range(KT):
                    op = nc.vector.bn_aggr(mv[:, t, :], st[:, t, :])
                chain.done(op)

            def step(n, p):
                q = 1 - p
                j = n - 3
                dc = Steps(dve, s["d_step"], 1, n)
                oc = Steps(dve, s["o_step"], 13, j)
                for h in range(NH + 2):
                    if h == 0 and on(n, 0):
                        need(dve, s["sbc_mm"], n)
                        nc.vector.tensor_tensor(diag[:], s_all[:, :, bass.ds(n, 1)].to_broadcast([P, 4, 64]),
                                                mask[:, None, :].to_broadcast([P, 4, 64]), ALU.mult
                                                ).then_inc(s["diag_done"], 1)
                    if h < NH and on(n, 1):
                        dve.wait_ge(s["max_mm"], NH * (n - 1) + h + 1)
                        if h == 0:
                            need(dve, s["mt_mm"], n - 1)
                        nc.vector.tensor_reduce(nmax[:, :, h], ps_m[:, h % 2], AX.X, ALU.max, negate=True
                                                ).then_inc(s["max_done"], 1)
                    if h == 0 and on(n, 0):
                        dve.wait_ge(s["sbc_mm"], n + 1)
                        need(dve, s["wout_mm"], n)
                        for m in range(MH):
                            op = nc.vector.scalar_tensor_tensor(y[:, m, :], ps_d[:, 0:S], c["d_col"][:, m:m + 1],
                                                                gated[:, m, bass.ds(n * S, S)], ALU.add, ALU.mult)
                        op.then_inc(s["y_done"], 1)
                    if h in (2, 3) and on(n, 3):
                        t = h - 2
                        dve.wait_ge(s["ot_mm"], 2 * j + t + 1)
                        if t == 0:
                            need(dve, s["ont_mm"], j)
                        o4 = ps_e[:].rearrange("p (h w) -> p h w", w=VW)
                        oc.done(nc.vector.reciprocal(rec[:], o4[:, :, HD]))
                        nc.vector.tensor_tensor(onrm[:, t].rearrange("p (h d) -> p h d", d=HD), o4[:, :, 0:HD],
                                                rec[:, :, None].to_broadcast([P, NH, HD]), ALU.mult
                                                ).then_inc(s["on_done"], 1)
                    if h == 2 and on(n, 0):
                        lo_half(c["b_k"], s["k_hi"], s["k_split"], n)
                    if h == 5 and on(n, 0):
                        dve.wait_ge(s["wout_mm"], n + 1)
                        dve.wait_ge(s["x_added"], n + 1)
                        nc.vector.tensor_tensor(r1[:].rearrange("p t d -> p (t d)"), ps_d[:],
                                                c["x2b"][:].rearrange("p t d -> p (t d)"), ALU.add
                                                ).then_inc(s["r1_done"], 1)
                        dve.wait_ge(s["r1_done"], n + 1)
                        stats(dc, st1, mv1, r1, s["stats1"], n)
                        nc.vector.tensor_scalar(ve1[:], mv1[:, :, 1], EPS, None, ALU.add).then_inc(s["var1_ready"], 1)
                    if h == 7 and on(n, 0):
                        dve.wait_ge(s["rstd1"], n + 1)
                        need(dve, s["x1_kept"], n - 1)
                        for t in range(KT):
                            op = nc.vector.tensor_scalar(x1[:, p, t, :], r1[:, t, :], mv1[:, t, 0:1], ve1[:, t:t + 1],
                                                         ALU.subtract, ALU.mult)
                        op.then_inc(s["x1_done"], 1)
                    if h == 6 and on(n, 3):
                        dve.wait_ge(s["oproj_mm"], j + 1)
                        dve.wait_ge(s["x1_kept"], j + 1)
                        nc.vector.tensor_tensor(c["r2"][:], ps_e[:].rearrange("p (t d) -> p t d", t=KT),
                                                gated[:, 0:KT, bass.ds(j * S, S)], ALU.add).then_inc(s["r2_done"], 1)
                        dve.wait_ge(s["r2_done"], j + 1)
                        stats(oc, st2, mv2, c["r2"], s["stats2"], j)
                        nc.vector.tensor_scalar(ve2[:], mv2[:, :, 1], EPS, None, ALU.add).then_inc(s["var2_ready"], 1)
                    if h == 8 and on(n, 3):
                        dve.wait_ge(s["rstd2"], j + 1)
                        need(dve, sent[q], use(j, 32, q) - 32)
                        for t in range(KT):
                            op = nc.vector.tensor_scalar(pay[:, q, t, 0:D], c["r2"][:, t, :], mv2[:, t, 0:1],
                                                         ve2[:, t:t + 1], ALU.subtract, ALU.mult)
                        op.then_inc(s["x2_done"], 1)
                        nc.vector.tensor_copy(pay[:, q, :, D], c["tokens"][:, bass.ds(j * KT, KT)])
                    if h == 10 and on(n, 3):
                        dve.wait_ge(s["x2_done"], j + 1)
                        stats(oc, st3, mv3, pay[:, q], s["stats3"], j)
                        nc.vector.tensor_scalar(ve3[:], mv3[:, :, 1], 4.0, EPS, ALU.mult, ALU.add
                                                ).then_inc(s["var3_ready"], 1)
                    if h == 11 and on(n, 0):
                        lo_half(bq, s["q_hi"], s["q_split"], n)
                    if h == 12 and on(n, 3):
                        dve.wait_ge(s["logit_mm"], j + 1)
                        nc.vector.tensor_copy(lg[:].rearrange("p t e -> p (t e)"), ps_e[:, 0:KT * E]).then_inc(s["lg_out"], 1)
                        dve.wait_ge(s["vo_row"], 1)
                        dve.wait_ge(s["lg_out"], 2 * j + 1)
                        for t in range(KT):
                            op = nc.vector.max(top[:, t, :], lg[:, t, :])
                        oc.done(op)
                        nc.vector.tensor_scalar(ntop[:], top[:, :, 0], -1.0, None, ALU.mult).then_inc(s["lg_out"], 1)
                        for t in range(KT):
                            op = nc.vector.max_index(where[:, t, :], top[:, t, :], lg[:, t, :])
                        oc.done(op)
                        oc.done(nc.vector.tensor_copy(expert[:], where[:, :, 0]))
                        for t in range(KT):
                            op = nc.vector.tensor_scalar(hot[:, t, :], c["kinds"][:], expert[:, t:t + 1], None, ALU.is_equal)
                        op.then_inc(s["hot_ready"], 1)
                        dve.wait_ge(s["rstd3"], j + 1)
                        need(dve, out_sent[q], use(j, 16, q) - 16)
                        oc.done(nc.vector.tensor_scalar(ve3[:], ve3[:], 2.0, None, ALU.mult))
                        for t in range(KT):
                            op = nc.vector.tensor_scalar(c["twice"][:, q, t, :], pay[:, q, t, 0:D], mv3[:, t, 0:1],
                                                         ve3[:, t:t + 1], ALU.subtract, ALU.mult)
                        op.then_inc(s["out_ready"], 1)
                        oc.done(nc.vector.tensor_scalar(slot0[:], expert[:], float(CAP), -1.0, ALU.mult, ALU.add))
                    if h == 15 and on(n, 3):
                        dve.wait_ge(s["cum_mm"], j + 1)
                        oc.done(nc.vector.tensor_tensor(sel[:].rearrange("p t e -> p (t e)"), ps_e[:, 0:KT * E],
                                                        hot[:].rearrange("p t e -> p (t e)"), ALU.mult))
                        nc.vector.tensor_tensor(carry[:], carry[:], hot[:, 0, :], ALU.add).then_inc(s["place_done"], 1)
                        oc.done(nc.vector.tensor_reduce(place[:], sel[:], AX.X, ALU.add))
                        nc.vector.tensor_tensor(carry[:], carry[:], hot[:, 1, :], ALU.add).then_inc(s["carry_ready"], 1)
                        oc.done(nc.vector.tensor_scalar(over[:], place[:], float(CAP), FAR, ALU.is_gt, ALU.mult))
                        oc.done(nc.vector.tensor_tensor(slot[:], slot0[:], place[:], ALU.add))
                        nc.vector.tensor_tensor(dest[:, q, :], slot[:], over[:], ALU.add).then_inc(s["dest_ready"], 1)
                        dve.wait_ge(s["den_done"], j + 1)
                        nc.vector.reciprocal(pay[:, q, :, D + 1], den[:]).then_inc(s["pay_ready"], 1)

            run(dve, step)
            dve.wait_ge(s["carry_ready"], B)


def experts(nc, T, PS, sem, c, dram):
    w, eye = c["w"], c["eye"]
    TS = CAP // P
    FT = F // P
    HC = CAP // 2

    rows = T("rows", [P, 2, TS, ROW], F32)
    w1 = T("w1", [P, 2, KD, F], F32)
    w2 = T("w2", [P, 2, FT, D], F32)
    xt = T("xt3", [P, 2, KD, CAP], F32)
    hid = T("hid", [P, FT, CAP], F32)
    res = T("res", [P, TS, D], F32)
    new = T("new", [P, 2, TS, D], F32)
    st, mv, ve = T("st4", [P, TS, 6], F32), T("mv4", [P, TS, 2], F32), T("ve4", [P, TS], F32)
    power = T("power4", [P, TS], F32)
    token = T("token", [P, 2, TS], I32)

    ps_t = PS("ps_t", [P, 2, 512], F32)
    ps_h = PS("ps_h", [P, 2, 2, 512], F32)
    ps_y = PS("ps_y", [P, 2, 512], F32)

    names = """rows_in0 rows_in1 w1_in0 w1_in1 w2_in0 w2_in1 turn_mm turn_out hid_mm hid_act hid_dve out_mm res_done
        var_ready rstd new_done sent0 sent1 step3 token_done setup3 stats_done""".split()
    s = {n: sem("e_" + n) for n in names}
    rows_in, w1_in, w2_in, sent = ([s[n + str(i)] for i in range(2)] for n in ("rows_in", "w1_in", "w2_in", "sent"))
    TURNS = (TS + 1) // 2

    def use(e, per, parity):
        if isinstance(e, int):
            return (e // 2 + 1) * per
        return e * (per // 2) + (per if parity == 0 else per // 2)

    def run(eng, step):
        step(0, 0)
        step(1, 1)
        with eng.Fori(1, E // 2) as i:
            step(i * 2, 0)
            step(i * 2 + 1, 1)

    with nc.Block() as block:

        @block.sync
        def _(sp):
            def step(e, p):
                need(sp, s["hid_mm"], (e - 1) * FT)
                sp.dma_start(w1[:, p], dram["w1"][bass.ds(e * D, D), :].rearrange("(k p) f -> p k f", p=P)
                             ).then_inc(w1_in[p], 16)
                need(sp, s["res_done"], (e - 1) * TS)
                need(sp, s["token_done"], e - 1)
                sp.dma_start(rows[:, p], dram["rows"][bass.ds(e * CAP, CAP), :].rearrange("(t p) r -> p t r", p=P)
                             ).then_inc(rows_in[p], 16)
                sp.dma_start(w2[:, p], dram["w2"][bass.ds(e * F, F), :].rearrange("(k p) d -> p k d", p=P)
                             ).then_inc(w2_in[p], 16)

            run(sp, step)

        @block.tensor
        def _(pe):
            def turn_rows(e, p):
                pe.wait_ge(rows_in[p], use(e, 16, p))
                for i in range(TURNS):
                    need(pe, s["turn_out"], e * TURNS + i - 1)
                    for t in range(2 * i, min(2 * i + 2, TS)):
                        for k in range(KD):
                            mm = pe.transpose(ps_t[:, (p * TURNS + i) % 2, (t % 2) * D + k * P:(t % 2) * D + (k + 1) * P],
                                              rows[:, p, t, k * P:(k + 1) * P], eye[:])
                    mm.then_inc(s["turn_mm"], 1)

            def hidden(e, p):
                pe.wait_ge(w1_in[p], use(e, 16, p))
                pe.wait_ge(s["turn_out"], (e + 1) * TURNS)
                for f in range(FT):
                    need(pe, s["hid_act"], e * FT + f - 1)
                    need(pe, s["hid_dve"], e * FT + f - 1)
                    for c2 in range(2):
                        for k in range(KD):
                            mm = pe.matmul(ps_h[:, f % 2, c2, 0:HC], w1[:, p, k, f * P:(f + 1) * P],
                                           xt[:, p, k, c2 * HC:(c2 + 1) * HC], start=(k == 0), stop=(k == KD - 1))
                    mm.then_inc(s["hid_mm"], 1)

            def down(e, p):
                pe.wait_ge(w2_in[p], use(e, 16, p))
                pe.wait_ge(s["hid_act"], (e + 1) * FT)
                pe.wait_ge(s["hid_dve"], (e + 1) * FT)
                for t in range(TS):
                    need(pe, s["res_done"], e * TS + t - 1)
                    for f in range(FT):
                        mm = pe.matmul(ps_y[:, (p + t) % 2, 0:D], hid[:, f, t * P:(t + 1) * P], w2[:, p, f, :],
                                       start=(f == 0), stop=(f == FT - 1))
                    mm.then_inc(s["out_mm"], 1)

            turn_rows(0, 0)

            def step(e, p, last=False):
                hidden(e, p)
                if not last:
                    turn_rows(e + 1, 1 - p)
                down(e, p)

            step(0, 0)
            step(1, 1)
            with pe.Fori(1, E // 2 - 1) as i:
                step(i * 2, 0)
                step(i * 2 + 1, 1)
            step(E - 2, 0)
            step(E - 1, 1, last=True)

        @block.scalar
        def _(act):
            def turned(e, p):
                for i in range(TURNS):
                    act.wait_ge(s["turn_mm"], e * TURNS + i + 1)
                    need(act, s["hid_mm"], (e - 1) * FT)
                    n = min(2, TS - 2 * i)
                    src = ps_t[:, (p * TURNS + i) % 2, 0:n * D].rearrange("p (t k c) -> p t k c", t=n, k=KD)
                    dst = xt[:, p, :, 2 * i * P:(2 * i + n) * P].rearrange("p k (t c) -> p t k c", t=n)
                    nc.scalar.copy(dst, src).then_inc(s["turn_out"], 1)

            def relus(e, p):
                for f in range(FT):
                    act.wait_ge(s["hid_mm"], e * FT + f + 1)
                    need(act, s["out_mm"], e * TS)
                    nc.scalar.activation(hid[:, f, 0:HC], ps_h[:, f % 2, 0, 0:HC], ACT.Relu).then_inc(s["hid_act"], 1)

            turned(0, 0)

            def step(e, p, last=False):
                relus(e, p)
                if not last:
                    turned(e + 1, 1 - p)

            step(0, 0)
            step(1, 1)
            with act.Fori(1, E // 2 - 1) as i:
                step(i * 2, 0)
                step(i * 2 + 1, 1)
            step(E - 2, 0)
            step(E - 1, 1, last=True)

        @block.vector
        def _(dve):
            def step(e, p):
                for f in range(FT):
                    dve.wait_ge(s["hid_mm"], e * FT + f + 1)
                    need(dve, s["out_mm"], e * TS)
                    nc.vector.tensor_scalar(hid[:, f, HC:CAP], ps_h[:, f % 2, 1, 0:HC], 0.0, None, ALU.max
                                            ).then_inc(s["hid_dve"], 1)
                for t in range(TS):
                    dve.wait_ge(s["out_mm"], e * TS + t + 1)
                    nc.vector.scalar_tensor_tensor(res[:, t, :], ps_y[:, (p + t) % 2, 0:D], rows[:, p, t, D + 1:D + 2],
                                                   rows[:, p, t, 0:D], ALU.mult, ALU.add).then_inc(s["res_done"], 1)
                    dve.wait_ge(s["res_done"], e * TS + t + 1)
                    nc.vector.bn_stats(st[:, t, :], res[:, t, :]).then_inc(s["stats_done"], 1)
                chain = Steps(dve, s["step3"], 1, e)
                dve.wait_ge(s["res_done"], 1)
                dve.wait_ge(s["stats_done"], e * TS + TS)
                for t in range(TS):
                    op = nc.vector.bn_aggr(mv[:, t, :], st[:, t, :])
                chain.done(op)
                need(dve, sent[p], use(e, 16 * TS, p) - 16 * TS)
                nc.vector.tensor_copy(token[:, p, :], rows[:, p, :, D]).then_inc(s["token_done"], 1)
                nc.vector.tensor_scalar(ve[:], mv[:, :, 1], EPS, None, ALU.add).then_inc(s["var_ready"], 1)
                dve.wait_ge(s["rstd"], e + 1)
                for t in range(TS):
                    op = nc.vector.tensor_scalar(new[:, p, t, :], res[:, t, :], mv[:, t, 0:1], ve[:, t:t + 1],
                                                 ALU.subtract, ALU.mult)
                op.then_inc(s["new_done"], 1)

            run(dve, step)

        @block.gpsimd
        def _(pool):
            nc.gpsimd.memset(power[:], -0.5).then_inc(s["setup3"], 1)
            pool.wait_ge(s["setup3"], 1)

            def step(e, p):
                pool.wait_ge(s["var_ready"], e + 1)
                nc.gpsimd.tensor_tensor(ve[:], ve[:], power[:], ALU.pow).then_inc(s["rstd"], 1)
                pool.wait_ge(s["var_ready"], 1)
                pool.wait_ge(s["new_done"], e + 1)
                pool.wait_ge(s["token_done"], e + 1)
                for t in range(TS):
                    nc.gpsimd.indirect_dma_start(
                        out=dram["out"], out_offset=bass.IndirectOffsetOnAxis(ap=token[:, p, t:t + 1], axis=0),
                        in_=new[:, p, t, :], in_offset=None, bounds_check=NT - 1, oob_is_err=False,
                    ).then_inc(sent[p], 16)

            run(pool, step)
            pool.wait_ge(sent[0], E // 2 * TS * 16)
            pool.wait_ge(sent[1], E // 2 * TS * 16)


def decoder(nc, dram):
    with ExitStack() as whole:
        def keep(name, shape, dt):
            return whole.enter_context(nc.sbuf_tensor(name, shape, dt))

        def sem(name):
            return whole.enter_context(nc.semaphore(name))

        dram["rows"] = nc.dram_tensor("rows_dram", (E * CAP, ROW), F32, kind="Internal").ap()
        c = {"eye": keep("eye", [P, P], F32), "w": {}}
        c["loads"] = [(c["eye"][:], dram["eye"])]
        with ExitStack() as first_two:
            def hold(name, shape, dt=F32):
                return first_two.enter_context(nc.sbuf_tensor(name, shape, dt))

            def load(name, shape, pattern=None, **kw):
                tile = hold(name + "_sb", shape)
                source = dram[name] if pattern is None else dram[name].rearrange(pattern, **kw)
                c["loads"].append((tile[:], source))
                return tile

            c["gated"] = hold("gated", [P, MH, NT])
            c["s"] = hold("s_all", [P, 4, B])
            c["blank"] = hold("blank", [P, ROW])
            c["hscr"] = nc.dram_tensor("halves_dram", (2, 2, D, S), F32, kind="Internal").ap()
            for n in "qkvo":
                c["w"][n] = load("w_" + n, [P, KD, D], "(k p) n -> p k n", p=P)
            c["w"]["out"] = load("w_out", [P, MH, D], "(k p) n -> p k n", p=P)
            c["w"]["r"] = load("w_r", [P, KD, E], "(k p) n -> p k n", p=P)
            c["bv_rep"] = load("bv_rep", [P, KD, P], "(k p) n -> p k n", p=P)
            for n, width in (("ones", P), ("mask", 64), ("tri", P), ("kinds", E), ("tokens", NT // P),
                             ("b_out", D), ("b_o", D), ("d_col", MH), ("b_k", KD), ("b_q", KD)):
                c[n] = load(n, [P, width])
            for n in ("loaded", "blank_ready", "rows_blank"):
                c[n] = sem(n)
            for part, before in ((mixer_in, {}), (attend, {"x2b": [P, S // P, D], "r2": [P, S // P, D],
                                                          "twice": [P, 2, S // P, D]})):
                with ExitStack() as own:
                    def tile(name, shape, dt):
                        return own.enter_context(nc.sbuf_tensor(name, shape, dt))

                    def bank(name, shape, dt):
                        return own.enter_context(nc.psum_tensor(name, shape, dt))

                    def flag(name):
                        return own.enter_context(nc.semaphore(name))

                    for name, shape in before.items():
                        c[name] = tile(name, shape, F32)
                    part(nc, tile, bank, flag, c, dram)
        with ExitStack() as own:
            def tile(name, shape, dt):
                return own.enter_context(nc.sbuf_tensor(name, shape, dt))

            def bank(name, shape, dt):
                return own.enter_context(nc.psum_tensor(name, shape, dt))

            def flag(name):
                return own.enter_context(nc.semaphore(name))

            experts(nc, tile, bank, flag, c, dram)


def laid_out(inputs):
    import numpy as np

    def a(name):
        return np.ascontiguousarray(inputs[name])

    def column(v):
        return v.reshape(-1, P).T

    mix, att, ffn = "L0_attn_", "L0_xattn_", "L0_ffn_"
    arrays = {
        "x": a("x").reshape(NT, D), "x_t": a("x").reshape(NT, D).T, "ctx_t": a("ctx_1024").reshape(NT, D).T,
        "w_in": a(mix + "W_in").T, "b_in": column(a(mix + "b_in")),
        "conv_w": a(mix + "conv_w").reshape(MH, P, K).transpose(1, 0, 2), "conv_b": column(a(mix + "conv_b")),
        "w_ssm": np.tile(a(mix + "W_ssm").T, (1, 4)), "b_ssm": np.tile(a(mix + "b_ssm"), 4)[:, None],
        "a_rep": np.tile(a(mix + "A"), (1, 4)), "a_tr": a(mix + "A").T,
        "c_rep": np.tile(a(mix + "Cv"), 4)[:, None], "b_rep": np.tile(a(mix + "Bv"), 4)[:, None],
        "d_col": column(a(mix + "Dv")), "w_out": a(mix + "W_out").T,
        "b_out": np.broadcast_to(a(mix + "b_out"), (P, D)), "b_o": np.broadcast_to(a(att + "bo"), (P, D)),
        "bv_rep": np.broadcast_to(a(att + "bv")[:, None], (D, P)),
        "b_q": column(a(att + "bq")), "b_k": column(a(att + "bk")),
        "w_r": a(ffn + "Wr"), "w1": a(ffn + "W1").reshape(E * D, F), "w2": a(ffn + "W2").reshape(E * F, D),
    }
    for n in "qkvo":
        arrays["w_" + n] = a(att + "W" + n).T
    one = np.float32
    arrays["eye_rep"] = np.tile(np.eye(NS, dtype=one), (4, 1))
    arrays["eye"] = np.eye(P, dtype=one)
    arrays["ones"] = np.ones((P, P), one)
    arrays["tri"] = np.triu(np.ones((P, P), one))
    arrays["kinds"] = np.tile(np.arange(E, dtype=one), (P, 1))
    arrays["tokens"] = np.arange(NT, dtype=one).reshape(NT // P, P).T
    mask = np.zeros((4, NS, 4, L), one)
    for c4 in range(4):
        mask[c4, :L, c4, :] = np.eye(L, dtype=one)
    arrays["mask"] = mask.reshape(P, 4 * L)
    return {n: np.ascontiguousarray(v) for n, v in arrays.items()}


def kernel(**inputs):
    import numpy as _np
    import concourse.bacc as _bacc
    from concourse import mybir as _mybir
    from concourse.bass_utils import run_bass_kernel_spmd as _run

    nc = _bacc.Bacc("TRN2", target_bir_lowering=False, num_devices=1)
    arrays, dram = {}, {}
    for name, v in laid_out(inputs).items():
        arrays["in_" + name] = v
        dram[name] = nc.dram_tensor("in_" + name, v.shape, _mybir.dt.from_np(v.dtype), kind="ExternalInput").ap()
    dram["out"] = nc.dram_tensor("out_rows", (NT, D), _mybir.dt.from_np(_np.dtype("float32")), kind="ExternalOutput").ap()
    decoder(nc, dram)
    r = _run(nc, [arrays], core_ids=[0])
    return r.results[0]["out_rows"].reshape(B, S, D)
```

```python
from contextlib import ExitStack

import concourse.bass as bass
from concourse import mybir

F32 = mybir.dt.float32
F32R = mybir.dt.float32r
BF16 = mybir.dt.bfloat16
I32 = mybir.dt.int32
U32 = mybir.dt.uint32
ALU = mybir.AluOpType
ACT = mybir.ActivationFunctionType
AX = mybir.AxisListType

P = 128
B, S, D = 16, 256, 256
H, NS, K = 512, 32, 4
NH, HD = 16, 16
E, CAP, F = 8, 640, 1024
NT = B * S
KD = D // P
MH = H // P
EPS = 1e-5
G = 2
NG = B // G
GT = G * S
L = 16
NC = S // L
Q4 = L // 4
FAR = float(1 << 20)
ROW = D + 2


def need(eng, sem, value):
    if isinstance(value, int) and value <= 0:
        return
    eng.wait_ge(sem, value)


class Steps:

    def __init__(self, eng, sem, per_turn, turn):
        self.eng, self.sem, self.per_turn, self.turn, self.n = eng, sem, per_turn, turn, 0

    def done(self, instruction):
        self.n += 1
        instruction.then_inc(self.sem, 1)
        self.eng.wait_ge(self.sem, self.turn * self.per_turn + self.n)

    def end(self):
        assert self.n == self.per_turn, (self.n, self.per_turn)


def mixer_in(nc, T, PS, sem, c, dram):
    gated, s_all = c["gated"], c["s"]
    w_in = T("w_in", [P, KD, 2 * H], F32)
    w_ssm = T("w_ssm", [P, MH, P], F32)
    bias_in = T("bias_in", [P, 2 * MH], F32)
    bias_cv = T("bias_cv", [P, MH], F32)
    taps = T("taps", [P, MH, K], F32)
    bias_ssm = T("bias_ssm", [P, 1], F32)
    xt = T("xt", [P, 2, KD, GT], F32)
    xpad = T("xpad", [P, 2, G, S + K - 1], F32)
    conv = T("conv", [P, 2, G, S], F32)
    xh = T("xh", [P, 2, MH, GT], F32)
    sgate = T("sgate", [P, MH, GT], F32)
    u = T("u", [P, Q4, NC, B], F32)
    a_rep = T("a_rep", [NS, 2, P], F32)
    a_tr = T("a_tr", [NS, 2, NS], F32)
    b_col = T("b_col", [P, 1], F32)
    pw = T("pw", [P, L, NS], F32)
    cw = T("cw", [P, S], F32)
    gw = T("gw", [P, L], F32)
    w_end = T("w_end", [P, Q4, 4, NS], F32)
    w_loc = T("w_loc", [P, Q4, NS], F32)
    w_lag = T("w_lag", [P, 4, 4, NS], F32)
    ends = T("ends", [P, 4, B], F32)

    ps_xh = PS("ps_xh", [P, 2, 512], F32)
    ps_gate = PS("ps_gate", [P, 2, 512], F32)
    ps_u = PS("ps_u", [P, 512], F32)
    ps_pow = PS("ps_pow", [P, 512], F32)
    ps_end = PS("ps_end", [P, 512], F32)
    ps_s = PS("ps_s", [P, 512], F32)

    w_here, x_here, a_here = sem("w_here"), [sem("x_even"), sem("x_odd")], sem("a_here")
    xh_mm, gate_mm, u_mm = sem("xh_mm"), sem("gate_mm"), sem("u_mm")
    pad_ready, conv_ready, xh_ready = sem("pad_ready"), sem("conv_ready"), sem("xh_ready")
    gate_ready, gated_done, u_ready = sem("gate_ready"), sem("gated_done"), sem("u_ready")
    pads_zero, conv_step = sem("pads_zero"), sem("conv_step")
    pow_mm, pow_copied, tables, zeroed = sem("pow_mm"), sem("pow_copied"), sem("tables"), sem("zeroed")
    end_mm, ends_ready, s_mm, s_ready = sem("end_mm"), sem("ends_ready"), sem("s_mm"), sem("s_ready")

    LEVELS = 8
    n_loads = 6

    with nc.Block() as block:

        @block.sync
        def _(sp):
            sp.dma_start(a_rep[:, 0, :], dram["a_rep"]).then_inc(a_here, 16)
            sp.dma_start(a_tr[:, 0, :], dram["a_tr"]).then_inc(a_here, 16)
            sp.dma_start(cw[:, 0:1], dram["c_rep"]).then_inc(a_here, 16)
            sp.dma_start(b_col[:], dram["b_rep"]).then_inc(a_here, 16)
            sp.dma_start(pw[:, 0, :], dram["eye_rep"]).then_inc(a_here, 16)
            for g in range(2):
                sp.dma_start(xt[:, g], dram["x_t"][:, g * GT:(g + 1) * GT].rearrange("(k p) t -> p k t", p=P)
                             ).then_inc(x_here[g], 16)
            sp.dma_start(w_in[:], dram["w_in"].rearrange("(k p) n -> p k n", p=P)).then_inc(w_here, 16)
            sp.dma_start(bias_in[:], dram["b_in"]).then_inc(w_here, 16)
            sp.dma_start(bias_cv[:], dram["conv_b"]).then_inc(w_here, 16)
            sp.dma_start(taps[:], dram["conv_w"]).then_inc(w_here, 16)
            sp.dma_start(w_ssm[:], dram["w_ssm"].rearrange("(k p) n -> p k n", p=P)).then_inc(w_here, 16)
            sp.dma_start(bias_ssm[:], dram["b_ssm"]).then_inc(w_here, 16)

            def load_x(g, buf):
                sp.wait_ge(gate_mm, MH)
                sp.wait_ge(gate_mm, g * MH - MH)
                sp.dma_start(xt[:, buf], dram["x_t"][:, bass.ds(g * GT, GT)].rearrange("(k p) t -> p k t", p=P)
                             ).then_inc(x_here[buf], 16)

            with sp.Fori(1, NG // 2) as gg:
                load_x(gg * 2, 0)
                load_x(gg * 2 + 1, 1)
            for tile, source in c["loads"]:
                sp.dma_start(tile, source).then_inc(c["loaded"], 16)
            sp.wait_ge(c["blank_ready"], 2)
            sp.dma_start(dram["rows"].rearrange("(t p) r -> p t r", p=P),
                         c["blank"][:, None, :].to_broadcast([P, E * CAP // P, ROW])).then_inc(c["rows_blank"], 16)

        @block.gpsimd
        def _(pool):
            nc.gpsimd.memset(c["blank"][:, 0:D], 0.0).then_inc(c["blank_ready"], 1)
            nc.gpsimd.memset(c["blank"][:, D:ROW], FAR).then_inc(c["blank_ready"], 1)

            def gate_group(g, last):
                for m in range(MH):
                    pool.wait_ge(xh_ready, MH * g + m + 1)
                    pool.wait_ge(gate_ready, MH * g + m + 1)
                    nc.gpsimd.tensor_tensor(gated[:, m, bass.ds(g * GT, GT)], xh[:, last, m, :], sgate[:, m, :],
                                            ALU.mult).then_inc(gated_done, 1)

            with pool.Fori(0, NG // 2) as gg:
                for half in range(2):
                    gate_group(gg * 2 + half, half)

        @block.tensor
        def _(pe):
            pe.wait_ge(a_here, 80)
            for level in range(LEVELS):
                n = 1 << level
                cur, mats = level % 2, level < 4
                if level:
                    pe.wait_ge(pow_copied, level)
                pe.matmul(ps_pow[:, 0:n], a_rep[:, cur, :], cw[0:NS, 0:n], start=True, stop=True,
                          skip_group_check=True)
                if mats:
                    pe.matmul(ps_end[:, 0:n * NS], a_rep[:, cur, :],
                              pw[0:NS, 0:n, :].rearrange("p k n -> p (k n)"), start=True, stop=True,
                              skip_group_check=True)
                pe.matmul(ps_s[0:NS, 0:P], a_tr[:, cur, :], a_rep[:, cur, :], start=True, stop=True,
                          skip_group_check=True)
                pe.matmul(ps_s[0:NS, P:P + NS], a_rep[:, cur, 0:NS], a_tr[:, cur, :], start=True, stop=True,
                          skip_group_check=True).then_inc(pow_mm, 1)
            pe.wait_ge(w_here, 16 * n_loads)

            def project(g, buf):
                pe.wait_ge(x_here[buf], g * 8 + (16 if buf == 0 else 8))
                for m in range(MH):
                    need(pe, pad_ready, MH * g + m - 1)
                    for k in range(KD):
                        mm = pe.matmul(ps_xh[:, m % 2, :], w_in[:, k, m * P:(m + 1) * P], xt[:, buf, k, :],
                                       start=(k == 0), stop=(k == KD - 1))
                    mm.then_inc(xh_mm, 1)
                for m in range(MH):
                    need(pe, gate_ready, MH * g + m - 1)
                    for k in range(KD):
                        mm = pe.matmul(ps_gate[:, m % 2, :], w_in[:, k, H + m * P:H + (m + 1) * P], xt[:, buf, k, :],
                                       start=(k == 0), stop=(k == KD - 1))
                    mm.then_inc(gate_mm, 1)

            def inject(g, buf):
                need(pe, u_ready, g)
                for m in range(MH):
                    pe.wait_ge(xh_ready, MH * g + m + 1)
                    mm = pe.matmul(ps_u[:, :], w_ssm[:, m, :], xh[:, buf, m, :], start=(m == 0), stop=(m == MH - 1))
                mm.then_inc(u_mm, 1)

            project(0, 0)
            project(1, 1)
            inject(0, 0)
            with pe.Fori(1, NG // 2) as gg:
                project(gg * 2, 0)
                inject(gg * 2 - 1, 1)
                project(gg * 2 + 1, 1)
                inject(gg * 2, 0)
            inject(NG - 1, 1)

            pe.wait_ge(u_ready, NG)
            pe.wait_ge(tables, 1)
            for q in range(Q4):
                mm = pe.matmul(ps_end[:, 0:NC * B], w_end[:, q].rearrange("p r n -> p (r n)"),
                               u[:, q].rearrange("p c b -> p (c b)"), start=(q == 0), stop=(q == Q4 - 1))
            mm.then_inc(end_mm, 1)
            uc = u[:].rearrange("p q (cq c4) b -> p q c4 cq b", c4=4)
            for c4 in range(4):
                for q in range(Q4):
                    pe.matmul(ps_s[NS * c4:NS * (c4 + 1), 0:4 * B], w_loc[:, q, :], uc[:, q, c4],
                              start=(q == 0), stop=False, skip_group_check=True)
            pe.wait_ge(ends_ready, 1)
            for lag in range(4):
                mm = pe.matmul(ps_s[:, lag * B:4 * B], w_lag[:, lag].rearrange("p c n -> p (c n)"),
                               ends[:, 0:4 - lag, :].rearrange("p c b -> p (c b)"),
                               start=False, stop=(lag == 3), skip_group_check=True)
            mm.then_inc(s_mm, 1)

        @block.scalar
        def _(act):
            act.wait_ge(w_here, 16 * n_loads)
            act.wait_ge(pads_zero, 1)

            def silus(g, buf):
                for m in range(MH):
                    act.wait_ge(xh_mm, MH * g + m + 1)
                    need(act, conv_ready, MH * g + m - 1)
                    nc.scalar.activation(xpad[:, m % 2, :, K - 1:], ps_xh[:, m % 2, :].rearrange("p (b t) -> p b t", b=G),
                                         ACT.Identity, bias=bias_in[:, m:m + 1]).then_inc(pad_ready, 1)
                    if m >= 1:
                        xh_of(g, buf, m - 1)
                for m in range(MH):
                    act.wait_ge(gate_mm, MH * g + m + 1)
                    need(act, gated_done, MH * (g - 1) + m + 1)
                    nc.scalar.activation(sgate[:, m, :], ps_gate[:, m % 2, :], ACT.Silu,
                                         bias=bias_in[:, MH + m:MH + m + 1]).then_inc(gate_ready, 1)
                    if m == 0:
                        xh_of(g, buf, MH - 1)
                if not isinstance(g, int) or g >= 1:
                    inject_out(g - 1)

            def xh_of(g, buf, m):
                act.wait_ge(conv_ready, MH * g + m + 1)
                need(act, gated_done, MH * (g - 2) + m + 1)
                need(act, u_mm, g - 1)
                nc.scalar.activation(xh[:, buf, m, :], conv[:, m % 2].rearrange("p b t -> p (b t)"), ACT.Silu
                                     ).then_inc(xh_ready, 1)

            def inject_out(g):
                act.wait_ge(u_mm, g + 1)
                src = ps_u[:].rearrange("p (b c q r) -> p r q c b", b=G, c=NC, q=Q4)
                for r in range(4):
                    rows = slice(NS * r, NS * (r + 1))
                    op = nc.scalar.activation(u[rows, :, :, bass.ds(g * G, G)], src[rows, r], ACT.Identity,
                                              bias=bias_ssm[rows, :])
                op.then_inc(u_ready, 1)

            silus(0, 0)
            silus(1, 1)
            with act.Fori(1, NG // 2) as gg:
                silus(gg * 2, 0)
                silus(gg * 2 + 1, 1)
            inject_out(NG - 1)

        @block.vector
        def _(dve):
            nc.vector.memset(w_loc[:], 0.0).then_inc(zeroed, 1)
            nc.vector.memset(w_lag[:], 0.0).then_inc(zeroed, 1)
            nc.vector.memset(xpad[:, :, :, 0:K - 1], 0.0).then_inc(pads_zero, 1)
            for level in range(LEVELS):
                n = 1 << level
                nxt = (level + 1) % 2
                dve.wait_ge(pow_mm, level + 1)
                if n < S:
                    hi = min(2 * n, S)
                    last = nc.vector.tensor_copy(cw[:, n:hi], ps_pow[:, 0:hi - n])
                if level < 4:
                    last = nc.vector.tensor_copy(pw[:, n:2 * n, :].rearrange("p k n -> p (k n)"), ps_end[:, 0:n * NS])
                if level < LEVELS - 1:
                    nc.vector.tensor_copy(a_rep[:, nxt, :], ps_s[0:NS, 0:P])
                    last = nc.vector.tensor_copy(a_tr[:, nxt, :], ps_s[0:NS, P:P + NS])
                last.then_inc(pow_copied, 1)
            dve.wait_ge(pow_copied, LEVELS)
            dve.wait_ge(zeroed, 2)
            nc.vector.tensor_scalar(gw[:], cw[:, 0:L], b_col[:, 0:1], None, ALU.mult).then_inc(zeroed, 1)
            dve.wait_ge(zeroed, 3)
            for r in range(4):
                rows = slice(NS * r, NS * (r + 1))
                for q in range(Q4):
                    i = 4 * q + r
                    nc.vector.tensor_scalar(w_end[rows, q], pw[rows, L - 1 - i:L - i, :].to_broadcast([NS, 4, NS]),
                                            b_col[rows, 0:1], None, ALU.mult)
                    nc.vector.tensor_copy(w_loc[rows, q, i:L], gw[rows, 0:L - i])
                lags = w_lag[rows].rearrange("p a b n -> p (a b) n")
                last = nc.vector.tensor_copy(lags[:, r + 1:, 0:L],
                                             cw[rows, 1:1 + L * (L - 1 - r)].rearrange("p (l i) -> p l i", i=L))
            last.then_inc(tables, 1)

            def convolve(g):
                for m in range(MH):
                    b = m % 2
                    dve.wait_ge(pad_ready, MH * g + m + 1)
                    need(dve, xh_ready, MH * g + m - 1)
                    st = Steps(dve, conv_step, MH * (K - 1), g)
                    st.n = m * (K - 1)
                    st.done(nc.vector.tensor_scalar(conv[:, b], xpad[:, b, :, 0:S], taps[:, m, 0:1],
                                                    bias_cv[:, m:m + 1], ALU.mult, ALU.add))
                    for k in range(1, K):
                        op = nc.vector.scalar_tensor_tensor(conv[:, b], xpad[:, b, :, k:k + S], taps[:, m, k:k + 1],
                                                            conv[:, b], ALU.mult, ALU.add)
                        if k < K - 1:
                            st.done(op)
                    op.then_inc(conv_ready, 1)

            dve.wait_ge(w_here, 16 * n_loads)
            convolve(0)
            with dve.Fori(1, NG) as g:
                convolve(g)
            dve.wait_ge(end_mm, 1)
            for c4 in range(4):
                rows = slice(NS * c4, NS * (c4 + 1))
                last = nc.vector.tensor_copy(ends[rows], ps_end[rows, 0:NC * B].rearrange(
                    "p (cq c4 b) -> p c4 cq b", c4=4, b=B)[:, c4])
            last.then_inc(ends_ready, 1)
            dve.wait_ge(s_mm, 1)
            nc.vector.tensor_copy(s_all[:], ps_s[:, 0:4 * B].rearrange("p (c b) -> p c b", b=B)).then_inc(s_ready, 1)
            dve.wait_ge(s_ready, 1)
            dve.wait_ge(gated_done, MH * NG)


def attend(nc, T, PS, sem, c, dram):
    gated, s_all = c["gated"], c["s"]
    w, eye, ones, mask = c["w"], c["eye"], c["ones"], c["mask"]
    KT = S // P
    MR = 96
    HH = NH // 2
    VW = 2 * HD
    AL, WL = 3, 5
    SCALE = HD ** -0.5

    xres = T("xres", [P, KT, D], F32)
    ctx = T("ctx", [P, 2, KD, S], F32)
    diag = T("diag", [P, 4, 64], F32)
    y = T("y", [P, MH, S], F32)
    r1 = T("r1", [P, KT, D], F32)
    x1 = T("x1", [P, 2, KT, D], F32)
    x1t = T("x1t", [P, KD, S], F32)
    half = T("half", [P, 2, KD, S], F32R)
    qst = T("qst", [P, 2, NH, S], F32R)
    kst = T("kst", [P, 2, NH, S], F32R)
    vals = T("vals", [P, 2, KT, NH, VW], F32)
    nmax = T("nmax", [P, 2, KT, NH], F32)
    mrow = T("mrow", [NH, S], F32R)
    pt = T("pt", [P, 2, KT, S], F32)
    oraw = T("oraw", [P, 4, S], F32)
    rec = T("rec", [P, NH], F32)
    onrm = T("onrm", [P, KT, D], F32)
    ont = T("ont", [P, KD, S], F32)
    x2t = T("x2t", [P, KD, S], F32)
    pay = T("pay", [P, 2, KT, ROW], F32)
    st1, mv1, ve1 = T("st1", [P, KT, 6], F32), T("mv1", [P, KT, 2], F32), T("ve1", [P, KT], F32)
    st2, mv2, ve2 = T("st2", [P, KT, 6], F32), T("mv2", [P, KT, 2], F32), T("ve2", [P, KT], F32)
    st3, mv3, ve3 = T("st3", [P, KT, 6], F32), T("mv3", [P, KT, 2], F32), T("ve3", [P, KT], F32)
    power = T("power", [P, KT], F32)
    lg, top, where = T("lg", [P, KT, E], F32), T("top", [P, KT, 8], F32), T("where", [P, KT, 8], U32)
    ntop, den, expert = T("ntop", [P, KT], F32), T("den", [P, KT], F32), T("expert", [P, KT], F32)
    el = T("el", [P, KT, E], F32)
    hot, carry = T("hot", [P, KT, E], BF16), T("carry", [P, E], BF16)
    tri, ones_b = T("tri", [P, P], BF16), T("ones_b", [P, P], BF16)
    sel, place = T("sel", [P, KT, E], F32), T("place", [P, KT], F32)
    over, slot0, slot = T("over", [P, KT], F32), T("slot0", [P, KT], F32), T("slot", [P, KT], F32)
    dest = T("dest", [P, 2, KT], I32)
    bq = T("bq", [P, KD], F32)

    ps_m = PS("ps_m", [P, 2, KT, S], F32)
    ps_a = PS("ps_a", [P, 2, KT, S], F32)
    ps_o = PS("ps_o", [P, 4, S], F32)
    ps_d = PS("ps_d", [P, 512], F32)
    ps_e = PS("ps_e", [P, 512], F32)
    hscr = c["hscr"]

    names = """setup_pool setup_dve setup_pe vo_row x_in0 x_in1 ctx_in0 ctx_in1 x_added
        sbc_mm k_mm v_mm wout_mm x1t_mm q_mm mt_mm diag_done y_done k_hi q_hi k_split q_split v_out r1_done var1_ready
        rstd1 x1_done x1_kept x1t_out m_out k_stored q_stored k_in00 k_in01 k_in10 k_in11 q_in00 q_in01 q_in10 q_in11
        m_in max_mm max_done att_mm exp_done pv_mm oraw_lo oraw_hi ot_mm on_done ont_mm ont_out oproj_mm r2_done
        var2_ready rstd2 x2_done x2t_mm x2t_out logit_mm lg_out den_done hot_ready cum_mm carry_ready
        var3_ready rstd3 dest_ready place_done pay_ready sent0 sent1 out_ready out_sent0 out_sent1
        d_step o_step r_step p_step stats1 stats2 stats3""".split()
    s = {n: sem(n) for n in names}
    x_in, ctx_in = [s["x_in0"], s["x_in1"]], [s["ctx_in0"], s["ctx_in1"]]
    k_in, q_in = ([[s[n + str(b) + str(lo)] for lo in range(2)] for b in range(2)] for n in ("k_in", "q_in"))
    sent, out_sent = [s["sent0"], s["sent1"]], [s["out_sent0"], s["out_sent1"]]
    KIN, QIN = 3 * 16, 2 * 16

    FIRST, LAST = 5, B - 2

    def run(eng, step):
        for n in range(-1, FIRST):
            step(n, n % 2)
        with eng.Fori(0, (LAST + 1 - FIRST) // 2) as i:
            step(i * 2 + FIRST, FIRST % 2)
            step(i * 2 + FIRST + 1, (FIRST + 1) % 2)
        for n in range(LAST + 1, B + 4):
            step(n, n % 2)

    def on(n, lag):
        return not isinstance(n, int) or 0 <= n - lag < B

    def use(j, per, parity):
        if isinstance(j, int):
            return (j // 2 + 1) * per
        return j * (per // 2) + (per if parity == 0 else per // 2)

    def settled(eng):
        eng.wait_ge(s["setup_pe"], 1)

    def behind(n, h, slots):
        return (n - 2, h - slots, 2) if h >= slots else (n - 3, h - slots + NH, 3)

    with nc.Block() as block:

        @block.sync
        def _(sp):
            def load_x(j, p):
                settled(sp)
                need(sp, s["x_added"], j)
                sp.dma_start(xres[:], dram["x"][bass.ds(j * S, S), :].rearrange("(t p) d -> p t d", p=P)
                             ).then_inc(x_in[p], 16)

            def load_ctx(j, p):
                settled(sp)
                need(sp, s["k_mm"], j - 1)
                need(sp, s["v_mm"], j - 1)
                sp.dma_start(ctx[:, p], dram["ctx_t"][:, bass.ds(j * S, S)].rearrange("(k p) t -> p k t", p=P)
                             ).then_inc(ctx_in[p], 16)

            def stack(j, p, lo):
                need(sp, s["att_mm"], (j - 2) * NH + HH * (lo + 1))
                heads = slice(HH * lo, HH * (lo + 1))
                for rows, src in ((slice(0, 32), slice(0, 32)), (slice(32, 48), slice(16, 32)),
                                  (slice(48, 64), slice(0, 16))):
                    sp.dma_start(kst[rows, p, heads, :].bitcast(F32), hscr[p, 0, lo][src]).then_inc(k_in[p][lo], 16)
                for rows in (slice(0, 32), slice(32, 64)):
                    sp.dma_start(qst[rows, p, heads, :].bitcast(F32), hscr[p, 1, lo]).then_inc(q_in[p][lo], 16)

            def store(j, p, which, split, stored):
                sp.wait_ge(split, j + 1)
                for m in range(KD):
                    sp.dma_start(hscr[p, which, m].rearrange("(c d) h t -> (d h) c t", c=2),
                                 half[:, :, m, :].bitcast(F32)).then_inc(stored, 16)
                settled(sp)
                sp.wait_ge(stored, j * 32 + 32)

            load_x(0, 0)
            load_ctx(0, 0)

            def step(n, p):
                if on(n, 4):
                    settled(sp)
                    sp.wait_ge(s["out_ready"], n - 3)
                    sp.dma_start(dram["out"][bass.ds((n - 4) * S, S), :].rearrange("(t p) d -> p t d", p=P),
                                 c["twice"][:, p]).then_inc(out_sent[p], 16)
                if on(n, 0) and on(n, -1):
                    load_x(n + 1, 1 - p)
                if on(n, 2):
                    sp.wait_ge(s["m_out"], n - 1)
                    sp.dma_start(qst[MR:MR + 1, p, :, :].bitcast(F32), mrow[:].bitcast(F32)).then_inc(s["m_in"], 16)
                if on(n, 1):
                    stack(n - 1, 1 - p, 1)
                if on(n, 0):
                    if on(n, 2):
                        for lo in range(2):
                            sp.wait_ge(k_in[p][lo], use(n - 2, KIN, p))
                            sp.wait_ge(q_in[p][lo], use(n - 2, QIN, p))
                    store(n, p, 0, s["k_split"], s["k_stored"])
                    store(n, p, 1, s["q_split"], s["q_stored"])
                    stack(n, p, 0)
                if on(n, 0) and on(n, -1):
                    load_ctx(n + 1, 1 - p)

            run(sp, step)
            sp.wait_ge(out_sent[0], B // 2 * 16)
            sp.wait_ge(out_sent[1], B // 2 * 16)

        @block.gpsimd
        def _(pool):
            nc.gpsimd.memset(power[:], -0.5).then_inc(s["setup_pool"], 1)
            pool.wait_ge(s["setup_pool"], 1)
            nc.gpsimd.memset(qst[64:P, :, :, :].bitcast(F32), 0.0).then_inc(s["setup_pool"], 1)
            nc.gpsimd.memset(kst[64:P, :, :, :].bitcast(F32), 0.0).then_inc(s["setup_pool"], 1)
            pool.wait_ge(s["setup_pool"], 3)
            nc.gpsimd.memset(kst[MR:MR + 1, :, :, :].bitcast(F32), 1.0).then_inc(s["setup_pool"], 1)
            pool.wait_ge(s["setup_pool"], 4)
            pool.wait_ge(c["rows_blank"], 16)

            def residual(j, p):
                pool.wait_ge(x_in[p], use(j, 16, p))
                own = Steps(pool, s["p_step"], 1, j)
                need(pool, s["r1_done"], j)
                own.done(nc.gpsimd.tensor_tensor(c["x2b"][:], xres[:],
                                                c["b_out"][:, None, :].to_broadcast([P, KT, D]), ALU.add))
                nc.gpsimd.tensor_tensor(c["x2b"][:], c["x2b"][:], xres[:], ALU.add).then_inc(s["x_added"], 1)

            residual(0, 0)

            def step(n, p):
                q = 1 - p
                if on(n, 0):
                    pool.wait_ge(s["var1_ready"], n + 1)
                    nc.gpsimd.tensor_tensor(ve1[:], ve1[:], power[:], ALU.pow).then_inc(s["rstd1"], 1)
                if on(n, 4):
                    pool.wait_ge(s["dest_ready"], n - 3)
                if on(n, 0):
                    pool.wait_ge(s["x1_done"], n + 1)
                    if isinstance(n, int) and n == 0:
                        pool.wait_ge(s["vo_row"], 1)
                    nc.gpsimd.tensor_tensor(gated[:, 0:KT, bass.ds(n * S, S)], x1[:, p],
                                            c["b_o"][:, None, :].to_broadcast([P, KT, D]), ALU.add
                                            ).then_inc(s["x1_kept"], 1)
                if on(n, 4):
                    settled(pool)
                    pool.wait_ge(s["pay_ready"], n - 3)
                    for t in range(KT):
                        nc.gpsimd.indirect_dma_start(
                            out=dram["rows"], out_offset=bass.IndirectOffsetOnAxis(ap=dest[:, p, t:t + 1], axis=0),
                            in_=pay[:, p, t, :], in_offset=None, bounds_check=E * CAP - 1, oob_is_err=False,
                        ).then_inc(sent[p], 16)
                if on(n, 0) and on(n, -1):
                    residual(n + 1, q)
                if on(n, 3):
                    j = n - 3
                    pool.wait_ge(s["var2_ready"], j + 1)
                    nc.gpsimd.tensor_tensor(ve2[:], ve2[:], power[:], ALU.pow).then_inc(s["rstd2"], 1)
                    pool.wait_ge(s["var3_ready"], j + 1)
                    need(pool, out_sent[q], use(j, 16, q) - 16)
                    nc.gpsimd.tensor_tensor(ve3[:], ve3[:], power[:], ALU.pow).then_inc(s["rstd3"], 1)
                    settled(pool)
                    pool.wait_ge(s["rstd3"], j + 1)
                    for t in range(KT):
                        op = nc.gpsimd.tensor_scalar(c["twice"][:, q, t, :], pay[:, q, t, 0:D], mv3[:, t, 0:1],
                                                     ve3[:, t:t + 1], ALU.subtract, ALU.mult)
                    op.then_inc(s["out_ready"], 1)

            run(pool, step)
            pool.wait_ge(sent[0], B // 2 * KT * 16)
            pool.wait_ge(sent[1], B // 2 * KT * 16)

        @block.tensor
        def _(pe):
            pe.wait_ge(c["loaded"], 16 * len(c["loads"]))
            for k in range(KD):
                mm = pe.matmul(ps_d[:, 0:D], c["bv_rep"][:, k, :], w["o"][:, k, :], start=(k == 0), stop=(k == KD - 1))
            mm.then_inc(s["setup_pe"], 1)
            pe.wait_ge(s["setup_dve"], 6)
            pe.wait_ge(s["setup_pool"], 4)

            def spread_s(j):
                pe.wait_ge(s["diag_done"], j + 1)
                need(pe, s["v_out"], j - 1)
                pe.matmul(ps_d[:, 0:S], ones[:], diag[:].rearrange("p c i -> p (c i)"), start=True, stop=True
                          ).then_inc(s["sbc_mm"], 1)

            def keys(j, p, m):
                if m == 0:
                    pe.wait_ge(ctx_in[p], use(j, 16, p))
                    pe.wait_ge(s["r1_done"], j + 1)
                for k in range(KD):
                    mm = pe.matmul(ps_d[:, m * S:(m + 1) * S], w["k"][:, k, m * P:(m + 1) * P], ctx[:, p, k, :],
                                   start=(k == 0), stop=(k == KD - 1), skip_group_check=True)
                if m == KD - 1:
                    mm.then_inc(s["k_mm"], 1)

            def values(j, p, t, dense):
                if t == 0 and dense is not None:
                    pe.wait_ge(s["q_split"], dense + 1)
                for k in range(KD):
                    mm = pe.matmul(ps_d[:, t * D:(t + 1) * D], ctx[:, p, k, t * P:(t + 1) * P], w["v"][:, k, :],
                                   start=(k == 0), stop=(k == KD - 1), skip_group_check=True)
                if t == KT - 1:
                    mm.then_inc(s["v_mm"], 1)

            def mixer_out(j, t):
                if t == 0:
                    pe.wait_ge(s["y_done"], j + 1)
                for m in range(MH):
                    mm = pe.matmul(ps_d[:, t * D:(t + 1) * D], y[:, m, t * P:(t + 1) * P], w["out"][:, m, :],
                                   start=(m == 0), stop=(m == MH - 1), skip_group_check=True)
                if t == KT - 1:
                    mm.then_inc(s["wout_mm"], 1)

            def turn(ps, src, done):
                for t in range(KT):
                    for k in range(KD):
                        mm = pe.transpose(ps[:, k * S + t * P:k * S + (t + 1) * P], src[:, t, k * P:(k + 1) * P], eye[:])
                mm.then_inc(done, 1)

            def queries(j, m):
                if m == 0:
                    pe.wait_ge(s["x1t_out"], j + 1)
                for k in range(KD):
                    mm = pe.matmul(ps_d[:, m * S:(m + 1) * S], w["q"][:, k, m * P:(m + 1) * P], x1t[:, k, :],
                                   start=(k == 0), stop=(k == KD - 1), skip_group_check=True)
                if m == KD - 1:
                    mm.then_inc(s["q_mm"], 1)

            def maxima_rows(j, p):
                pe.wait_ge(s["max_done"], NH * j + NH)
                for t in range(KT):
                    mm = pe.transpose(ps_m[0:NH, p, 0, t * P:(t + 1) * P], nmax[:, p, t, :], eye[:])
                mm.then_inc(s["mt_mm"], 1)

            def scores(j, p, h):
                if h % HH == 0:
                    pe.wait_ge(q_in[p][h // HH], use(j, QIN, p))
                    pe.wait_ge(k_in[p][h // HH], use(j, KIN, p))
                if h == 2:
                    need(pe, s["m_out"], j)
                else:
                    need(pe, s["max_done"], NH * j + (h if h == 1 else h - 1))
                for t in range(KT):
                    mm = pe.matmul(ps_m[:, (h + (h > 0) + p) % 2, t, :], qst[0:MR, p, h, t * P:(t + 1) * P],
                                   kst[0:MR, p, h, :], start=True, stop=True, skip_group_check=True)
                mm.then_inc(s["max_mm"], 1)

            def scores_t(j, p, h):
                if h == 0:
                    pe.wait_ge(s["m_in"], j * 16 + 16)
                need(pe, s["exp_done"], NH * j + h - 1)
                for t in range(KT):
                    mm = pe.matmul(ps_a[:, h % 2, t, :], kst[:, p, h, t * P:(t + 1) * P], qst[:, p, h, :],
                                   start=True, stop=True, skip_group_check=True)
                mm.then_inc(s["att_mm"], 1)

            def weigh(j, p, h):
                pe.wait_ge(s["exp_done"], NH * j + h + 1)
                if h == 0:
                    pe.wait_ge(s["v_out"], j + 1)
                    need(pe, s["oraw_lo"], j)
                if h == HH:
                    need(pe, s["oraw_hi"], j)
                for t in range(KT):
                    mm = pe.matmul(ps_o[VW * (h % 4):VW * (h % 4 + 1), h // 4, :], vals[:, p, t, h, :],
                                   pt[:, h % 2, t, :],
                                   start=(t == 0), stop=(t == KT - 1), skip_group_check=True)
                mm.then_inc(s["pv_mm"], 1)

            def sums_by_query(j, t):
                if t == 0:
                    pe.wait_ge(s["oraw_hi"], j + 1)
                    need(pe, s["place_done"], j)
                else:
                    pe.wait_ge(s["on_done"], 2 * j + 1)
                for g in range(4):
                    mm = pe.transpose(ps_e[:, g * P:(g + 1) * P], oraw[:, g, t * P:(t + 1) * P], eye[:])
                mm.then_inc(s["ot_mm"], 1)

            def project_out(j, t):
                if t == 0:
                    pe.wait_ge(s["ont_out"], j + 1)
                for k in range(KD):
                    mm = pe.matmul(ps_e[:, t * D:(t + 1) * D], ont[:, k, t * P:(t + 1) * P], w["o"][:, k, :],
                                   start=(k == 0), stop=(k == KD - 1), skip_group_check=True)
                if t == KT - 1:
                    mm.then_inc(s["oproj_mm"], 1)

            def router(j):
                pe.wait_ge(s["x2t_out"], j + 1)
                for t in range(KT):
                    for k in range(KD):
                        mm = pe.matmul(ps_e[:, t * E:(t + 1) * E], x2t[:, k, t * P:(t + 1) * P], w["r"][:, k, :],
                                       start=(k == 0), stop=(k == KD - 1), skip_group_check=True)
                mm.then_inc(s["logit_mm"], 1)

            def count(j):
                pe.wait_ge(s["hot_ready"], j + 1)
                need(pe, s["carry_ready"], j)
                for t in range(KT):
                    here = ps_e[:, t * E:(t + 1) * E]
                    pe.matmul(here, tri[:], hot[:, t, :], start=True, stop=False, skip_group_check=True)
                    if t:
                        pe.matmul(here, ones_b[:], hot[:, 0, :], start=False, stop=False, skip_group_check=True)
                    mm = pe.matmul(here, ones_b[:], carry[:], start=False, stop=True, skip_group_check=True)
                mm.then_inc(s["cum_mm"], 1)

            def step(n, p):
                q = 1 - p
                for h in range(NH):
                    if on(n, 1):
                        scores(n - 1, q, h)
                    if h == 0 and on(n, 2):
                        maxima_rows(n - 2, p)
                    j, head, lag = behind(n, h, AL)
                    if on(n, lag):
                        scores_t(j, p if lag == 2 else q, head)
                    if h == 12 and on(n, -1):
                        spread_s(n + 1)
                    if h in (14, 15) and on(n, -1):
                        mixer_out(n + 1, h - 14)
                    if h in (1, 2) and on(n, 0):
                        keys(n, p, h - 1)
                    if h == 4 and on(n, 0):
                        pe.wait_ge(s["k_split"], n + 1)
                        pe.wait_ge(s["x1_done"], n + 1)
                        turn(ps_d, x1[:, p], s["x1t_mm"])
                    if h in (6, 7) and on(n, 0):
                        queries(n, h - 6)
                    if h in (9, 10) and on(n, 1):
                        values(n - 1, q, h - 9, n if on(n, 0) else None)
                    if h == 0 and on(n, 4):
                        count(n - 4)
                    if h in (6, 7) and on(n, 3):
                        sums_by_query(n - 3, h - 6)
                    if h == 8 and on(n, 3):
                        pe.wait_ge(s["on_done"], 2 * (n - 3) + 2)
                        turn(ps_e, onrm, s["ont_mm"])
                    if h in (9, 10) and on(n, 3):
                        project_out(n - 3, h - 9)
                    if h == 13 and on(n, 3):
                        pe.wait_ge(s["x2_done"], n - 2)
                        turn(ps_e, pay[:, q], s["x2t_mm"])
                    if h == 14 and on(n, 3):
                        router(n - 3)
                    j, head, lag = behind(n, h, WL)
                    if on(n, lag):
                        weigh(j, p if lag == 2 else q, head)

            run(pe, step)

        @block.scalar
        def _(act):
            act.wait_ge(c["loaded"], 16 * len(c["loads"]))

            def split_hi(bias, out):
                for m in range(KD):
                    op = nc.scalar.activation(half[:, 0, m, :], ps_d[:, m * S:(m + 1) * S], ACT.Identity,
                                              bias=bias[:, m:m + 1])
                op.then_inc(out, 1)

            def sums_out(j, half_of, done):
                act.wait_ge(s["pv_mm"], NH * j + HH * (half_of + 1))
                need(act, s["ot_mm"], 2 * j)
                two = slice(2 * half_of, 2 * half_of + 2)
                nc.scalar.copy(oraw[:, two].rearrange("p g t -> p (g t)"), ps_o[:, two].rearrange("p g t -> p (g t)")
                               ).then_inc(done, 1)

            def step(n, p):
                q = 1 - p
                for h in range(NH):
                    if h == 1 and on(n, 2):
                        act.wait_ge(s["mt_mm"], n - 1)
                        need(act, s["m_in"], 16 * (n - 2))
                        nc.scalar.copy(mrow[:], ps_m[0:NH, p, 0, :]).then_inc(s["m_out"], 1)
                    if h == 0 and on(n, 4):
                        j = n - 4
                        act.wait_ge(s["lg_out"], 2 * j + 2)
                        need(act, s["pay_ready"], j)
                        for t in range(KT):
                            op = nc.scalar.activation(el[:, t, :], lg[:, t, :], ACT.Exp, bias=ntop[:, t:t + 1],
                                                      accum_out=den[:, t:t + 1])
                        op.then_inc(s["den_done"], 1)
                    if h == 3 and on(n, 0):
                        act.wait_ge(s["k_mm"], n + 1)
                        need(act, s["q_stored"], 32 * n)
                        split_hi(c["b_k"], s["k_hi"])
                    if h == 5 and on(n, 0):
                        act.wait_ge(s["x1t_mm"], n + 1)
                        nc.scalar.copy(x1t[:].rearrange("p k t -> p (k t)"), ps_d[:]).then_inc(s["x1t_out"], 1)
                    if h == WL and on(n, 3):
                        sums_out(n - 3, 1, s["oraw_hi"])
                    if h == 8 and on(n, 0):
                        act.wait_ge(s["q_mm"], n + 1)
                        act.wait_ge(s["k_stored"], 32 * n + 32)
                        if isinstance(n, int) and n == 0:
                            act.wait_ge(s["setup_dve"], 6)
                        split_hi(bq, s["q_hi"])
                    if h == 9 and on(n, 3):
                        act.wait_ge(s["ont_mm"], n - 2)
                        nc.scalar.copy(ont[:].rearrange("p k t -> p (k t)"), ps_e[:]).then_inc(s["ont_out"], 1)
                    if h == 11 and on(n, 1):
                        act.wait_ge(s["v_mm"], n)
                        need(act, s["pv_mm"], NH * (n - 2))
                        nc.scalar.copy(vals[:, q, :, :, 0:HD], ps_d[:].rearrange("p (t h d) -> p t h d", t=KT, h=NH)
                                       ).then_inc(s["v_out"], 1)
                    if h == WL + HH and on(n, 2):
                        sums_out(n - 2, 0, s["oraw_lo"])
                    if h == 14 and on(n, 3):
                        act.wait_ge(s["x2t_mm"], n - 2)
                        nc.scalar.copy(x2t[:].rearrange("p k t -> p (k t)"), ps_e[:]).then_inc(s["x2t_out"], 1)
                    j, head, lag = behind(n, h, AL)
                    if on(n, lag):
                        act.wait_ge(s["att_mm"], NH * j + head + 1)
                        need(act, s["pv_mm"], NH * j + head - 1)
                        nc.scalar.activation(pt[:, head % 2].rearrange("p t q -> p (t q)"),
                                             ps_a[:, head % 2].rearrange("p t q -> p (t q)"), ACT.Exp
                                             ).then_inc(s["exp_done"], 1)

            run(act, step)

        @block.vector
        def _(dve):
            nc.vector.memset(vals[:, :, :, :, HD:VW], 1.0).then_inc(s["setup_dve"], 1)
            nc.vector.memset(carry[:], 0.0).then_inc(s["setup_dve"], 1)
            dve.wait_ge(c["loaded"], 16 * len(c["loads"]))
            nc.vector.tensor_scalar(w["q"][:], w["q"][:], SCALE, None, ALU.mult).then_inc(s["setup_dve"], 1)
            nc.vector.tensor_scalar(bq[:], c["b_q"][:], SCALE, None, ALU.mult).then_inc(s["setup_dve"], 1)
            nc.vector.tensor_copy(tri[:], c["tri"][:]).then_inc(s["setup_dve"], 1)
            nc.vector.tensor_copy(ones_b[:], ones[:]).then_inc(s["setup_dve"], 1)
            dve.wait_ge(s["setup_pe"], 1)
            nc.vector.tensor_tensor(c["b_o"][:], c["b_o"][:], ps_d[:, 0:D], ALU.add).then_inc(s["vo_row"], 1)
            dve.wait_ge(s["setup_dve"], 6)
            dve.wait_ge(s["setup_pool"], 4)
            dve.wait_ge(s["vo_row"], 1)

            def lo_half(bias, hi, out, j):
                dve.wait_ge(hi, j + 1)
                for m in range(KD):
                    op = nc.vector.scalar_tensor_tensor(half[:, 1, m, :], ps_d[:, m * S:(m + 1) * S], bias[:, m:m + 1],
                                                        half[:, 0, m, :].bitcast(F32), ALU.add, ALU.subtract)
                op.then_inc(out, 1)

            def stats(chain, st, mv, src, stats_done, batch):
                for t in range(KT):
                    op = nc.vector.bn_stats(st[:, t, :], src[:, t, 0:D])
                op.then_inc(stats_done, 1)
                dve.wait_ge(s["vo_row"], 1)
                dve.wait_ge(stats_done, batch + 1)
                for t in range(KT):
                    op = nc.vector.bn_aggr(mv[:, t, :], st[:, t, :])
                chain.done(op)

            def step(n, p):
                q = 1 - p
                j = n - 3
                dc = Steps(dve, s["d_step"], 1, n)
                oc = Steps(dve, s["o_step"], 8, j)
                rc = Steps(dve, s["r_step"], 4, n - 4)
                for h in range(NH):
                    if on(n, 1):
                        dve.wait_ge(s["max_mm"], NH * (n - 1) + h + 1)
                        nc.vector.tensor_reduce(nmax[:, q, :, h], ps_m[:, (h + (h > 0) + q) % 2], AX.X, ALU.max,
                                                negate=True).then_inc(s["max_done"], 1)
                    if h == 0 and on(n, 0):
                        dve.wait_ge(s["wout_mm"], n + 1)
                        dve.wait_ge(s["x_added"], n + 1)
                        nc.vector.tensor_tensor(r1[:].rearrange("p t d -> p (t d)"), ps_d[:],
                                                c["x2b"][:].rearrange("p t d -> p (t d)"), ALU.add
                                                ).then_inc(s["r1_done"], 1)
                        dve.wait_ge(s["r1_done"], n + 1)
                        stats(dc, st1, mv1, r1, s["stats1"], n)
                        nc.vector.tensor_scalar(ve1[:], mv1[:, :, 1], EPS, None, ALU.add).then_inc(s["var1_ready"], 1)
                    if h == 1 and on(n, 4):
                        dve.wait_ge(s["cum_mm"], n - 3)
                        rc.done(nc.vector.tensor_tensor(sel[:].rearrange("p t e -> p (t e)"), ps_e[:, 0:KT * E],
                                                        hot[:].rearrange("p t e -> p (t e)"), ALU.mult))
                        nc.vector.tensor_tensor(carry[:], carry[:], hot[:, 0, :], ALU.add).then_inc(s["place_done"], 1)
                        rc.done(nc.vector.tensor_reduce(place[:], sel[:], AX.X, ALU.add))
                        nc.vector.tensor_tensor(carry[:], carry[:], hot[:, 1, :], ALU.add).then_inc(s["carry_ready"], 1)
                        rc.done(nc.vector.tensor_scalar(over[:], place[:], float(CAP), FAR, ALU.is_gt, ALU.mult))
                        rc.done(nc.vector.tensor_tensor(slot[:], slot0[:], place[:], ALU.add))
                        nc.vector.tensor_tensor(dest[:, p, :], slot[:], over[:], ALU.add).then_inc(s["dest_ready"], 1)
                        dve.wait_ge(s["den_done"], n - 3)
                        nc.vector.reciprocal(pay[:, p, :, D + 1], den[:]).then_inc(s["pay_ready"], 1)
                    if h == 3 and on(n, 0):
                        dve.wait_ge(s["rstd1"], n + 1)
                        need(dve, s["x1_kept"], n - 1)
                        for t in range(KT):
                            op = nc.vector.tensor_scalar(x1[:, p, t, :], r1[:, t, :], mv1[:, t, 0:1], ve1[:, t:t + 1],
                                                         ALU.subtract, ALU.mult)
                        op.then_inc(s["x1_done"], 1)
                        lo_half(c["b_k"], s["k_hi"], s["k_split"], n)
                    if h in (6, 7) and on(n, 3):
                        t = h - 6
                        dve.wait_ge(s["ot_mm"], 2 * j + t + 1)
                        if t == 0:
                            need(dve, s["ont_mm"], j)
                        o4 = ps_e[:].rearrange("p (h w) -> p h w", w=VW)
                        oc.done(nc.vector.reciprocal(rec[:], o4[:, :, HD]))
                        nc.vector.tensor_tensor(onrm[:, t].rearrange("p (h d) -> p h d", d=HD), o4[:, :, 0:HD],
                                                rec[:, :, None].to_broadcast([P, NH, HD]), ALU.mult
                                                ).then_inc(s["on_done"], 1)
                    if h == 8 and on(n, 0):
                        lo_half(bq, s["q_hi"], s["q_split"], n)
                    if h == 10 and on(n, 3):
                        dve.wait_ge(s["oproj_mm"], j + 1)
                        dve.wait_ge(s["x1_kept"], j + 1)
                        nc.vector.tensor_tensor(c["r2"][:], ps_e[:].rearrange("p (t d) -> p t d", t=KT),
                                                gated[:, 0:KT, bass.ds(j * S, S)], ALU.add).then_inc(s["r2_done"], 1)
                        dve.wait_ge(s["r2_done"], j + 1)
                        stats(oc, st2, mv2, c["r2"], s["stats2"], j)
                        nc.vector.tensor_scalar(ve2[:], mv2[:, :, 1], EPS, None, ALU.add).then_inc(s["var2_ready"], 1)
                    if h == 11 and on(n, -1):
                        need(dve, s["sbc_mm"], n + 1)
                        nc.vector.tensor_tensor(diag[:], s_all[:, :, bass.ds(n + 1, 1)].to_broadcast([P, 4, 64]),
                                                mask[:, None, :].to_broadcast([P, 4, 64]), ALU.mult
                                                ).then_inc(s["diag_done"], 1)
                    if h == 12 and on(n, 3):
                        dve.wait_ge(s["rstd2"], j + 1)
                        need(dve, sent[q], use(j, 32, q) - 32)
                        need(dve, s["out_ready"], j - 1)
                        for t in range(KT):
                            op = nc.vector.tensor_scalar(pay[:, q, t, 0:D], c["r2"][:, t, :], mv2[:, t, 0:1],
                                                         ve2[:, t:t + 1], ALU.subtract, ALU.mult)
                        op.then_inc(s["x2_done"], 1)
                        nc.vector.tensor_copy(pay[:, q, :, D], c["tokens"][:, bass.ds(j * KT, KT)])
                    if h == 12 and on(n, -1):
                        dve.wait_ge(s["sbc_mm"], n + 2)
                        for m in range(MH):
                            op = nc.vector.scalar_tensor_tensor(y[:, m, :], ps_d[:, 0:S], c["d_col"][:, m:m + 1],
                                                                gated[:, m, bass.ds((n + 1) * S, S)], ALU.add, ALU.mult)
                        op.then_inc(s["y_done"], 1)
                    if h == 13 and on(n, 3):
                        dve.wait_ge(s["x2_done"], j + 1)
                        need(dve, s["out_ready"], j)
                        stats(oc, st3, mv3, pay[:, q], s["stats3"], j)
                        nc.vector.tensor_scalar(ve3[:], mv3[:, :, 1], EPS / 4, None, ALU.add
                                                ).then_inc(s["var3_ready"], 1)
                    if h == 15 and on(n, 3):
                        dve.wait_ge(s["logit_mm"], j + 1)
                        nc.vector.tensor_copy(lg[:].rearrange("p t e -> p (t e)"), ps_e[:, 0:KT * E]).then_inc(s["lg_out"], 1)
                        dve.wait_ge(s["vo_row"], 1)
                        dve.wait_ge(s["lg_out"], 2 * j + 1)
                        for t in range(KT):
                            op = nc.vector.max(top[:, t, :], lg[:, t, :])
                        oc.done(op)
                        nc.vector.tensor_scalar(ntop[:], top[:, :, 0], -1.0, None, ALU.mult).then_inc(s["lg_out"], 1)
                        for t in range(KT):
                            op = nc.vector.max_index(where[:, t, :], top[:, t, :], lg[:, t, :])
                        oc.done(op)
                        oc.done(nc.vector.tensor_copy(expert[:], where[:, :, 0]))
                        for t in range(KT):
                            op = nc.vector.tensor_scalar(hot[:, t, :], c["kinds"][:], expert[:, t:t + 1], None, ALU.is_equal)
                        op.then_inc(s["hot_ready"], 1)
                        oc.done(nc.vector.tensor_scalar(slot0[:], expert[:], float(CAP), -1.0, ALU.mult, ALU.add))

            run(dve, step)
            dve.wait_ge(s["carry_ready"], B)


def experts(nc, T, PS, sem, c, dram):
    w, eye = c["w"], c["eye"]
    TS = CAP // P
    FT = F // P
    HC = CAP // 2

    rows = T("rows", [P, 2, TS, ROW], F32)
    w1 = T("w1", [P, 2, KD, F], F32)
    w2 = T("w2", [P, 2, FT, D], F32)
    xt = T("xt3", [P, 2, KD, CAP], F32)
    hid = T("hid", [P, FT, CAP], F32)
    res = T("res", [P, TS, D], F32)
    new = T("new", [P, 2, TS, D], F32)
    st, mv, ve = T("st4", [P, TS, 6], F32), T("mv4", [P, TS, 2], F32), T("ve4", [P, TS], F32)
    power = T("power4", [P, TS], F32)
    token = T("token", [P, 2, TS], I32)

    ps_t = PS("ps_t", [P, 2, 512], F32)
    ps_h = PS("ps_h", [P, 2, 2, 512], F32)
    ps_y = PS("ps_y", [P, 2, 512], F32)

    names = """rows_in0 rows_in1 w1_in0 w1_in1 w2_in0 w2_in1 turn_mm turn_out hid_mm hid_act hid_dve out_mm res_done
        var_ready rstd new_done sent0 sent1 step3 token_done setup3 stats_done""".split()
    s = {n: sem("e_" + n) for n in names}
    rows_in, w1_in, w2_in, sent = ([s[n + str(i)] for i in range(2)] for n in ("rows_in", "w1_in", "w2_in", "sent"))
    TURNS = (TS + 1) // 2

    def use(e, per, parity):
        if isinstance(e, int):
            return (e // 2 + 1) * per
        return e * (per // 2) + (per if parity == 0 else per // 2)

    def run(eng, step):
        step(0, 0)
        step(1, 1)
        with eng.Fori(1, E // 2) as i:
            step(i * 2, 0)
            step(i * 2 + 1, 1)

    with nc.Block() as block:

        @block.sync
        def _(sp):
            def step(e, p):
                need(sp, s["hid_mm"], (e - 1) * FT)
                sp.dma_start(w1[:, p], dram["w1"][bass.ds(e * D, D), :].rearrange("(k p) f -> p k f", p=P)
                             ).then_inc(w1_in[p], 16)
                need(sp, s["res_done"], (e - 1) * TS)
                need(sp, s["token_done"], e - 1)
                sp.dma_start(rows[:, p], dram["rows"][bass.ds(e * CAP, CAP), :].rearrange("(t p) r -> p t r", p=P)
                             ).then_inc(rows_in[p], 16)
                sp.dma_start(w2[:, p], dram["w2"][bass.ds(e * F, F), :].rearrange("(k p) d -> p k d", p=P)
                             ).then_inc(w2_in[p], 16)

            run(sp, step)

        @block.tensor
        def _(pe):
            def turn_rows(e, p):
                pe.wait_ge(rows_in[p], use(e, 16, p))
                for i in range(TURNS):
                    need(pe, s["turn_out"], e * TURNS + i - 1)
                    for t in range(2 * i, min(2 * i + 2, TS)):
                        for k in range(KD):
                            mm = pe.transpose(ps_t[:, (p * TURNS + i) % 2, (t % 2) * D + k * P:(t % 2) * D + (k + 1) * P],
                                              rows[:, p, t, k * P:(k + 1) * P], eye[:])
                    mm.then_inc(s["turn_mm"], 1)

            def hidden(e, p):
                pe.wait_ge(w1_in[p], use(e, 16, p))
                pe.wait_ge(s["turn_out"], (e + 1) * TURNS)
                for f in range(FT):
                    need(pe, s["hid_act"], e * FT + f - 1)
                    need(pe, s["hid_dve"], e * FT + f - 1)
                    for c2 in range(2):
                        for k in range(KD):
                            mm = pe.matmul(ps_h[:, f % 2, c2, 0:HC], w1[:, p, k, f * P:(f + 1) * P],
                                           xt[:, p, k, c2 * HC:(c2 + 1) * HC], start=(k == 0), stop=(k == KD - 1))
                    mm.then_inc(s["hid_mm"], 1)

            def down(e, p):
                pe.wait_ge(w2_in[p], use(e, 16, p))
                pe.wait_ge(s["hid_act"], (e + 1) * FT)
                pe.wait_ge(s["hid_dve"], (e + 1) * FT)
                for t in range(TS):
                    need(pe, s["res_done"], e * TS + t - 1)
                    for f in range(FT):
                        mm = pe.matmul(ps_y[:, (p + t) % 2, 0:D], hid[:, f, t * P:(t + 1) * P], w2[:, p, f, :],
                                       start=(f == 0), stop=(f == FT - 1))
                    mm.then_inc(s["out_mm"], 1)

            turn_rows(0, 0)

            def step(e, p, last=False):
                hidden(e, p)
                if not last:
                    turn_rows(e + 1, 1 - p)
                down(e, p)

            step(0, 0)
            step(1, 1)
            with pe.Fori(1, E // 2 - 1) as i:
                step(i * 2, 0)
                step(i * 2 + 1, 1)
            step(E - 2, 0)
            step(E - 1, 1, last=True)

        @block.scalar
        def _(act):
            def turned(e, p):
                for i in range(TURNS):
                    act.wait_ge(s["turn_mm"], e * TURNS + i + 1)
                    need(act, s["hid_mm"], (e - 1) * FT)
                    n = min(2, TS - 2 * i)
                    src = ps_t[:, (p * TURNS + i) % 2, 0:n * D].rearrange("p (t k c) -> p t k c", t=n, k=KD)
                    dst = xt[:, p, :, 2 * i * P:(2 * i + n) * P].rearrange("p k (t c) -> p t k c", t=n)
                    nc.scalar.copy(dst, src).then_inc(s["turn_out"], 1)

            def relus(e, p):
                for f in range(FT):
                    act.wait_ge(s["hid_mm"], e * FT + f + 1)
                    need(act, s["out_mm"], e * TS)
                    nc.scalar.activation(hid[:, f, 0:HC], ps_h[:, f % 2, 0, 0:HC], ACT.Relu).then_inc(s["hid_act"], 1)

            turned(0, 0)

            def step(e, p, last=False):
                relus(e, p)
                if not last:
                    turned(e + 1, 1 - p)

            step(0, 0)
            step(1, 1)
            with act.Fori(1, E // 2 - 1) as i:
                step(i * 2, 0)
                step(i * 2 + 1, 1)
            step(E - 2, 0)
            step(E - 1, 1, last=True)

        @block.vector
        def _(dve):
            def step(e, p):
                for f in range(FT):
                    dve.wait_ge(s["hid_mm"], e * FT + f + 1)
                    need(dve, s["out_mm"], e * TS)
                    nc.vector.tensor_scalar(hid[:, f, HC:CAP], ps_h[:, f % 2, 1, 0:HC], 0.0, None, ALU.max
                                            ).then_inc(s["hid_dve"], 1)
                for t in range(TS):
                    dve.wait_ge(s["out_mm"], e * TS + t + 1)
                    nc.vector.scalar_tensor_tensor(res[:, t, :], ps_y[:, (p + t) % 2, 0:D], rows[:, p, t, D + 1:D + 2],
                                                   rows[:, p, t, 0:D], ALU.mult, ALU.add).then_inc(s["res_done"], 1)
                    dve.wait_ge(s["res_done"], e * TS + t + 1)
                    nc.vector.bn_stats(st[:, t, :], res[:, t, :]).then_inc(s["stats_done"], 1)
                chain = Steps(dve, s["step3"], 1, e)
                dve.wait_ge(s["res_done"], 1)
                dve.wait_ge(s["stats_done"], e * TS + TS)
                for t in range(TS):
                    op = nc.vector.bn_aggr(mv[:, t, :], st[:, t, :])
                chain.done(op)
                need(dve, sent[p], use(e, 16 * TS, p) - 16 * TS)
                nc.vector.tensor_copy(token[:, p, :], rows[:, p, :, D]).then_inc(s["token_done"], 1)
                nc.vector.tensor_scalar(ve[:], mv[:, :, 1], EPS, None, ALU.add).then_inc(s["var_ready"], 1)
                dve.wait_ge(s["rstd"], e + 1)
                for t in range(TS):
                    op = nc.vector.tensor_scalar(new[:, p, t, :], res[:, t, :], mv[:, t, 0:1], ve[:, t:t + 1],
                                                 ALU.subtract, ALU.mult)
                op.then_inc(s["new_done"], 1)

            run(dve, step)

        @block.gpsimd
        def _(pool):
            nc.gpsimd.memset(power[:], -0.5).then_inc(s["setup3"], 1)
            pool.wait_ge(s["setup3"], 1)

            def step(e, p):
                pool.wait_ge(s["var_ready"], e + 1)
                nc.gpsimd.tensor_tensor(ve[:], ve[:], power[:], ALU.pow).then_inc(s["rstd"], 1)
                pool.wait_ge(s["var_ready"], 1)
                pool.wait_ge(s["new_done"], e + 1)
                pool.wait_ge(s["token_done"], e + 1)
                for t in range(TS):
                    nc.gpsimd.indirect_dma_start(
                        out=dram["out"], out_offset=bass.IndirectOffsetOnAxis(ap=token[:, p, t:t + 1], axis=0),
                        in_=new[:, p, t, :], in_offset=None, bounds_check=NT - 1, oob_is_err=False,
                    ).then_inc(sent[p], 16)

            run(pool, step)
            pool.wait_ge(sent[0], E // 2 * TS * 16)
            pool.wait_ge(sent[1], E // 2 * TS * 16)


def decoder(nc, dram):
    with ExitStack() as whole:
        def keep(name, shape, dt):
            return whole.enter_context(nc.sbuf_tensor(name, shape, dt))

        def sem(name):
            return whole.enter_context(nc.semaphore(name))

        dram["rows"] = nc.dram_tensor("rows_dram", (E * CAP, ROW), F32, kind="Internal").ap()
        c = {"eye": keep("eye", [P, P], F32), "w": {}}
        c["loads"] = [(c["eye"][:], dram["eye"])]
        with ExitStack() as first_two:
            def hold(name, shape, dt=F32):
                return first_two.enter_context(nc.sbuf_tensor(name, shape, dt))

            def load(name, shape, pattern=None, **kw):
                tile = hold(name + "_sb", shape)
                source = dram[name] if pattern is None else dram[name].rearrange(pattern, **kw)
                c["loads"].append((tile[:], source))
                return tile

            c["gated"] = hold("gated", [P, MH, NT])
            c["s"] = hold("s_all", [P, 4, B])
            c["blank"] = hold("blank", [P, ROW])
            c["hscr"] = nc.dram_tensor("halves_dram", (2, 2, KD, 2 * HD, P // HD, S), F32, kind="Internal").ap()
            for n in "qkvo":
                c["w"][n] = load("w_" + n, [P, KD, D], "(k p) n -> p k n", p=P)
            c["w"]["out"] = load("w_out", [P, MH, D], "(k p) n -> p k n", p=P)
            c["w"]["r"] = load("w_r", [P, KD, E], "(k p) n -> p k n", p=P)
            c["bv_rep"] = load("bv_rep", [P, KD, P], "(k p) n -> p k n", p=P)
            for n, width in (("ones", P), ("mask", 64), ("tri", P), ("kinds", E), ("tokens", NT // P),
                             ("b_out", D), ("b_o", D), ("d_col", MH), ("b_k", KD), ("b_q", KD)):
                c[n] = load(n, [P, width])
            for n in ("loaded", "blank_ready", "rows_blank"):
                c[n] = sem(n)
            for part, before in ((mixer_in, {}), (attend, {"x2b": [P, S // P, D], "r2": [P, S // P, D],
                                                          "twice": [P, 2, S // P, D]})):
                with ExitStack() as own:
                    def tile(name, shape, dt):
                        return own.enter_context(nc.sbuf_tensor(name, shape, dt))

                    def bank(name, shape, dt):
                        return own.enter_context(nc.psum_tensor(name, shape, dt))

                    def flag(name):
                        return own.enter_context(nc.semaphore(name))

                    for name, shape in before.items():
                        c[name] = tile(name, shape, F32)
                    part(nc, tile, bank, flag, c, dram)
        with ExitStack() as own:
            def tile(name, shape, dt):
                return own.enter_context(nc.sbuf_tensor(name, shape, dt))

            def bank(name, shape, dt):
                return own.enter_context(nc.psum_tensor(name, shape, dt))

            def flag(name):
                return own.enter_context(nc.semaphore(name))

            experts(nc, tile, bank, flag, c, dram)


def laid_out(inputs):
    import numpy as np

    def a(name):
        return np.ascontiguousarray(inputs[name])

    def column(v):
        return v.reshape(-1, P).T

    def by_dim(v):
        return v.reshape(v.shape[:-1] + (KD, P // HD, HD)).swapaxes(-1, -2).reshape(v.shape)

    mix, att, ffn = "L0_attn_", "L0_xattn_", "L0_ffn_"
    arrays = {
        "x": a("x").reshape(NT, D), "x_t": a("x").reshape(NT, D).T, "ctx_t": a("ctx_1024").reshape(NT, D).T,
        "w_in": a(mix + "W_in").T, "b_in": column(a(mix + "b_in")),
        "conv_w": a(mix + "conv_w").reshape(MH, P, K).transpose(1, 0, 2), "conv_b": column(a(mix + "conv_b")),
        "w_ssm": np.tile(a(mix + "W_ssm").T, (1, 4)), "b_ssm": np.tile(a(mix + "b_ssm"), 4)[:, None],
        "a_rep": np.tile(a(mix + "A"), (1, 4)), "a_tr": a(mix + "A").T,
        "c_rep": np.tile(a(mix + "Cv"), 4)[:, None], "b_rep": np.tile(a(mix + "Bv"), 4)[:, None],
        "d_col": column(a(mix + "Dv")), "w_out": a(mix + "W_out").T,
        "b_out": np.broadcast_to(a(mix + "b_out"), (P, D)), "b_o": np.broadcast_to(a(att + "bo"), (P, D)),
        "bv_rep": np.broadcast_to(a(att + "bv")[:, None], (D, P)),
        "b_q": column(by_dim(a(att + "bq"))), "b_k": column(by_dim(a(att + "bk"))),
        "w_r": a(ffn + "Wr"), "w1": a(ffn + "W1").reshape(E * D, F), "w2": a(ffn + "W2").reshape(E * F, D),
    }
    for n in "vo":
        arrays["w_" + n] = a(att + "W" + n).T
    for n in "qk":
        arrays["w_" + n] = by_dim(a(att + "W" + n).T)
    one = np.float32
    arrays["eye_rep"] = np.tile(np.eye(NS, dtype=one), (4, 1))
    arrays["eye"] = np.eye(P, dtype=one)
    arrays["ones"] = np.ones((P, P), one)
    arrays["tri"] = np.triu(np.ones((P, P), one))
    arrays["kinds"] = np.tile(np.arange(E, dtype=one), (P, 1))
    arrays["tokens"] = np.arange(NT, dtype=one).reshape(NT // P, P).T
    mask = np.zeros((4, NS, 4, L), one)
    for c4 in range(4):
        mask[c4, :L, c4, :] = np.eye(L, dtype=one)
    arrays["mask"] = mask.reshape(P, 4 * L)
    return {n: np.ascontiguousarray(v) for n, v in arrays.items()}


def kernel(**inputs):
    import numpy as _np
    import concourse.bacc as _bacc
    from concourse import mybir as _mybir
    from concourse.bass_utils import run_bass_kernel_spmd as _run

    nc = _bacc.Bacc("TRN2", target_bir_lowering=False, num_devices=1)
    arrays, dram = {}, {}
    for name, v in laid_out(inputs).items():
        arrays["in_" + name] = v
        dram[name] = nc.dram_tensor("in_" + name, v.shape, _mybir.dt.from_np(v.dtype), kind="ExternalInput").ap()
    dram["out"] = nc.dram_tensor("out_rows", (NT, D), _mybir.dt.from_np(_np.dtype("float32")), kind="ExternalOutput").ap()
    decoder(nc, dram)
    r = _run(nc, [arrays], core_ids=[0])
    return r.results[0]["out_rows"].reshape(B, S, D)
```

```python
from contextlib import ExitStack

import concourse.bass as bass
from concourse import mybir

F32 = mybir.dt.float32
F32R = mybir.dt.float32r
BF16 = mybir.dt.bfloat16
I32 = mybir.dt.int32
U32 = mybir.dt.uint32
ALU = mybir.AluOpType
ACT = mybir.ActivationFunctionType
AX = mybir.AxisListType

P = 128
B, S, D = 16, 256, 256
H, NS, K = 512, 32, 4
NH, HD = 16, 16
E, CAP, F = 8, 640, 1024
NT = B * S
KD = D // P
MH = H // P
EPS = 1e-5
G = 2
NG = B // G
GT = G * S
L = 16
NC = S // L
Q4 = L // 4
FAR = float(1 << 20)
ROW = D + 2


def need(eng, sem, value):
    if isinstance(value, int) and value <= 0:
        return
    eng.wait_ge(sem, value)


class Steps:

    def __init__(self, eng, sem, per_turn, turn):
        self.eng, self.sem, self.per_turn, self.turn, self.n = eng, sem, per_turn, turn, 0

    def done(self, instruction):
        self.n += 1
        instruction.then_inc(self.sem, 1)
        self.eng.wait_ge(self.sem, self.turn * self.per_turn + self.n)

    def end(self):
        assert self.n == self.per_turn, (self.n, self.per_turn)


def mixer_in(nc, T, PS, sem, c, dram):
    gated, s_all = c["gated"], c["s"]
    w_in = T("w_in", [P, KD, 2 * H], F32)
    w_ssm = T("w_ssm", [P, MH, P], F32)
    bias_in = T("bias_in", [P, 2 * MH], F32)
    bias_cv = T("bias_cv", [P, MH], F32)
    taps = T("taps", [P, MH, K], F32)
    bias_ssm = T("bias_ssm", [P, 1], F32)
    xt = T("xt", [P, 2, KD, GT], F32)
    xpad = T("xpad", [P, 2, G, S + K - 1], F32)
    conv = T("conv", [P, 2, G, S], F32)
    xh = T("xh", [P, 2, MH, GT], F32)
    sgate = T("sgate", [P, MH, GT], F32)
    u = T("u", [P, Q4, NC, B], F32)
    a_rep = T("a_rep", [NS, 2, P], F32)
    a_tr = T("a_tr", [NS, 2, NS], F32)
    b_col = T("b_col", [P, 1], F32)
    pw = T("pw", [P, L, NS], F32)
    cw = T("cw", [P, S], F32)
    gw = T("gw", [P, L], F32)
    w_end = T("w_end", [P, Q4, 4, NS], F32)
    w_loc = T("w_loc", [P, Q4, NS], F32)
    w_lag = T("w_lag", [P, 4, 4, NS], F32)
    ends = T("ends", [P, 4, B], F32)

    ps_xh = PS("ps_xh", [P, 2, 512], F32)
    ps_gate = PS("ps_gate", [P, 2, 512], F32)
    ps_u = PS("ps_u", [P, 512], F32)
    ps_pow = PS("ps_pow", [P, 512], F32)
    ps_end = PS("ps_end", [P, 512], F32)
    ps_s = PS("ps_s", [P, 512], F32)

    w_here, x_here, a_here = sem("w_here"), [sem("x_even"), sem("x_odd")], sem("a_here")
    xh_mm, gate_mm, u_mm = sem("xh_mm"), sem("gate_mm"), sem("u_mm")
    pad_ready, conv_ready, xh_ready = sem("pad_ready"), sem("conv_ready"), sem("xh_ready")
    gate_ready, gated_done, u_ready = sem("gate_ready"), sem("gated_done"), sem("u_ready")
    pads_zero, conv_step = sem("pads_zero"), sem("conv_step")
    pow_mm, pow_copied, tables, zeroed = sem("pow_mm"), sem("pow_copied"), sem("tables"), sem("zeroed")
    end_mm, ends_ready, s_mm, s_ready = sem("end_mm"), sem("ends_ready"), sem("s_mm"), sem("s_ready")

    LEVELS = 8
    n_loads = 6

    with nc.Block() as block:

        @block.sync
        def _(sp):
            sp.dma_start(a_rep[:, 0, :], dram["a_rep"]).then_inc(a_here, 16)
            sp.dma_start(a_tr[:, 0, :], dram["a_tr"]).then_inc(a_here, 16)
            sp.dma_start(cw[:, 0:1], dram["c_rep"]).then_inc(a_here, 16)
            sp.dma_start(b_col[:], dram["b_rep"]).then_inc(a_here, 16)
            sp.dma_start(pw[:, 0, :], dram["eye_rep"]).then_inc(a_here, 16)
            for g in range(2):
                sp.dma_start(xt[:, g], dram["x_t"][:, g * GT:(g + 1) * GT].rearrange("(k p) t -> p k t", p=P)
                             ).then_inc(x_here[g], 16)
            sp.dma_start(w_in[:], dram["w_in"].rearrange("(k p) n -> p k n", p=P)).then_inc(w_here, 16)
            sp.dma_start(bias_in[:], dram["b_in"]).then_inc(w_here, 16)
            sp.dma_start(bias_cv[:], dram["conv_b"]).then_inc(w_here, 16)
            sp.dma_start(taps[:], dram["conv_w"]).then_inc(w_here, 16)
            sp.dma_start(w_ssm[:], dram["w_ssm"].rearrange("(k p) n -> p k n", p=P)).then_inc(w_here, 16)
            sp.dma_start(bias_ssm[:], dram["b_ssm"]).then_inc(w_here, 16)

            def load_x(g, buf):
                sp.wait_ge(gate_mm, MH)
                sp.wait_ge(gate_mm, g * MH - MH)
                sp.dma_start(xt[:, buf], dram["x_t"][:, bass.ds(g * GT, GT)].rearrange("(k p) t -> p k t", p=P)
                             ).then_inc(x_here[buf], 16)

            with sp.Fori(1, NG // 2) as gg:
                load_x(gg * 2, 0)
                load_x(gg * 2 + 1, 1)
            for tile, source in c["loads"]:
                sp.dma_start(tile, source).then_inc(c["loaded"], 16)
            sp.wait_ge(c["blank_ready"], 2)
            sp.dma_start(dram["rows"].rearrange("(t p) r -> p t r", p=P),
                         c["blank"][:, None, :].to_broadcast([P, E * CAP // P, ROW])).then_inc(c["rows_blank"], 16)

        @block.gpsimd
        def _(pool):
            nc.gpsimd.memset(c["blank"][:, 0:D], 0.0).then_inc(c["blank_ready"], 1)
            nc.gpsimd.memset(c["blank"][:, D:ROW], FAR).then_inc(c["blank_ready"], 1)

            def gate_group(g, last):
                for m in range(MH):
                    pool.wait_ge(xh_ready, MH * g + m + 1)
                    pool.wait_ge(gate_ready, MH * g + m + 1)
                    nc.gpsimd.tensor_tensor(gated[:, m, bass.ds(g * GT, GT)], xh[:, last, m, :], sgate[:, m, :],
                                            ALU.mult).then_inc(gated_done, 1)

            with pool.Fori(0, NG // 2) as gg:
                for half in range(2):
                    gate_group(gg * 2 + half, half)

        @block.tensor
        def _(pe):
            pe.wait_ge(a_here, 80)
            for level in range(LEVELS):
                n = 1 << level
                cur, mats = level % 2, level < 4
                if level:
                    pe.wait_ge(pow_copied, level)
                pe.matmul(ps_pow[:, 0:n], a_rep[:, cur, :], cw[0:NS, 0:n], start=True, stop=True,
                          skip_group_check=True)
                if mats:
                    pe.matmul(ps_end[:, 0:n * NS], a_rep[:, cur, :],
                              pw[0:NS, 0:n, :].rearrange("p k n -> p (k n)"), start=True, stop=True,
                              skip_group_check=True)
                pe.matmul(ps_s[0:NS, 0:P], a_tr[:, cur, :], a_rep[:, cur, :], start=True, stop=True,
                          skip_group_check=True)
                pe.matmul(ps_s[0:NS, P:P + NS], a_rep[:, cur, 0:NS], a_tr[:, cur, :], start=True, stop=True,
                          skip_group_check=True).then_inc(pow_mm, 1)
            pe.wait_ge(w_here, 16 * n_loads)

            def project(g, buf):
                pe.wait_ge(x_here[buf], g * 8 + (16 if buf == 0 else 8))
                for m in range(MH):
                    need(pe, pad_ready, MH * g + m - 1)
                    for k in range(KD):
                        mm = pe.matmul(ps_xh[:, m % 2, :], w_in[:, k, m * P:(m + 1) * P], xt[:, buf, k, :],
                                       start=(k == 0), stop=(k == KD - 1))
                    mm.then_inc(xh_mm, 1)
                for m in range(MH):
                    need(pe, gate_ready, MH * g + m - 1)
                    for k in range(KD):
                        mm = pe.matmul(ps_gate[:, m % 2, :], w_in[:, k, H + m * P:H + (m + 1) * P], xt[:, buf, k, :],
                                       start=(k == 0), stop=(k == KD - 1))
                    mm.then_inc(gate_mm, 1)

            def inject(g, buf):
                need(pe, u_ready, g)
                for m in range(MH):
                    pe.wait_ge(xh_ready, MH * g + m + 1)
                    mm = pe.matmul(ps_u[:, :], w_ssm[:, m, :], xh[:, buf, m, :], start=(m == 0), stop=(m == MH - 1))
                mm.then_inc(u_mm, 1)

            project(0, 0)
            project(1, 1)
            inject(0, 0)
            with pe.Fori(1, NG // 2) as gg:
                project(gg * 2, 0)
                inject(gg * 2 - 1, 1)
                project(gg * 2 + 1, 1)
                inject(gg * 2, 0)
            inject(NG - 1, 1)

            pe.wait_ge(u_ready, NG)
            pe.wait_ge(tables, 1)
            for q in range(Q4):
                mm = pe.matmul(ps_end[:, 0:NC * B], w_end[:, q].rearrange("p r n -> p (r n)"),
                               u[:, q].rearrange("p c b -> p (c b)"), start=(q == 0), stop=(q == Q4 - 1))
            mm.then_inc(end_mm, 1)
            uc = u[:].rearrange("p q (cq c4) b -> p q c4 cq b", c4=4)
            for c4 in range(4):
                for q in range(Q4):
                    pe.matmul(ps_s[NS * c4:NS * (c4 + 1), 0:4 * B], w_loc[:, q, :], uc[:, q, c4],
                              start=(q == 0), stop=False, skip_group_check=True)
            pe.wait_ge(ends_ready, 1)
            for lag in range(4):
                mm = pe.matmul(ps_s[:, lag * B:4 * B], w_lag[:, lag].rearrange("p c n -> p (c n)"),
                               ends[:, 0:4 - lag, :].rearrange("p c b -> p (c b)"),
                               start=False, stop=(lag == 3), skip_group_check=True)
            mm.then_inc(s_mm, 1)

        @block.scalar
        def _(act):
            act.wait_ge(w_here, 16 * n_loads)
            act.wait_ge(pads_zero, 1)

            def silus(g, buf):
                for m in range(MH):
                    act.wait_ge(xh_mm, MH * g + m + 1)
                    need(act, conv_ready, MH * g + m - 1)
                    nc.scalar.activation(xpad[:, m % 2, :, K - 1:], ps_xh[:, m % 2, :].rearrange("p (b t) -> p b t", b=G),
                                         ACT.Identity, bias=bias_in[:, m:m + 1]).then_inc(pad_ready, 1)
                    if m >= 1:
                        xh_of(g, buf, m - 1)
                for m in range(MH):
                    act.wait_ge(gate_mm, MH * g + m + 1)
                    need(act, gated_done, MH * (g - 1) + m + 1)
                    nc.scalar.activation(sgate[:, m, :], ps_gate[:, m % 2, :], ACT.Silu,
                                         bias=bias_in[:, MH + m:MH + m + 1]).then_inc(gate_ready, 1)
                    if m == 0:
                        xh_of(g, buf, MH - 1)
                if not isinstance(g, int) or g >= 1:
                    inject_out(g - 1)

            def xh_of(g, buf, m):
                act.wait_ge(conv_ready, MH * g + m + 1)
                need(act, gated_done, MH * (g - 2) + m + 1)
                need(act, u_mm, g - 1)
                nc.scalar.activation(xh[:, buf, m, :], conv[:, m % 2].rearrange("p b t -> p (b t)"), ACT.Silu
                                     ).then_inc(xh_ready, 1)

            def inject_out(g):
                act.wait_ge(u_mm, g + 1)
                src = ps_u[:].rearrange("p (b c q r) -> p r q c b", b=G, c=NC, q=Q4)
                for r in range(4):
                    rows = slice(NS * r, NS * (r + 1))
                    op = nc.scalar.activation(u[rows, :, :, bass.ds(g * G, G)], src[rows, r], ACT.Identity,
                                              bias=bias_ssm[rows, :])
                op.then_inc(u_ready, 1)

            silus(0, 0)
            silus(1, 1)
            with act.Fori(1, NG // 2) as gg:
                silus(gg * 2, 0)
                silus(gg * 2 + 1, 1)
            inject_out(NG - 1)

        @block.vector
        def _(dve):
            nc.vector.memset(w_loc[:], 0.0).then_inc(zeroed, 1)
            nc.vector.memset(w_lag[:], 0.0).then_inc(zeroed, 1)
            nc.vector.memset(xpad[:, :, :, 0:K - 1], 0.0).then_inc(pads_zero, 1)
            for level in range(LEVELS):
                n = 1 << level
                nxt = (level + 1) % 2
                dve.wait_ge(pow_mm, level + 1)
                if n < S:
                    hi = min(2 * n, S)
                    last = nc.vector.tensor_copy(cw[:, n:hi], ps_pow[:, 0:hi - n])
                if level < 4:
                    last = nc.vector.tensor_copy(pw[:, n:2 * n, :].rearrange("p k n -> p (k n)"), ps_end[:, 0:n * NS])
                if level < LEVELS - 1:
                    nc.vector.tensor_copy(a_rep[:, nxt, :], ps_s[0:NS, 0:P])
                    last = nc.vector.tensor_copy(a_tr[:, nxt, :], ps_s[0:NS, P:P + NS])
                last.then_inc(pow_copied, 1)
            dve.wait_ge(pow_copied, LEVELS)
            dve.wait_ge(zeroed, 2)
            nc.vector.tensor_scalar(gw[:], cw[:, 0:L], b_col[:, 0:1], None, ALU.mult).then_inc(zeroed, 1)
            dve.wait_ge(zeroed, 3)
            for r in range(4):
                rows = slice(NS * r, NS * (r + 1))
                for q in range(Q4):
                    i = 4 * q + r
                    nc.vector.tensor_scalar(w_end[rows, q], pw[rows, L - 1 - i:L - i, :].to_broadcast([NS, 4, NS]),
                                            b_col[rows, 0:1], None, ALU.mult)
                    nc.vector.tensor_copy(w_loc[rows, q, i:L], gw[rows, 0:L - i])
                lags = w_lag[rows].rearrange("p a b n -> p (a b) n")
                last = nc.vector.tensor_copy(lags[:, r + 1:, 0:L],
                                             cw[rows, 1:1 + L * (L - 1 - r)].rearrange("p (l i) -> p l i", i=L))
            last.then_inc(tables, 1)

            def convolve(g):
                for m in range(MH):
                    b = m % 2
                    dve.wait_ge(pad_ready, MH * g + m + 1)
                    need(dve, xh_ready, MH * g + m - 1)
                    st = Steps(dve, conv_step, MH * (K - 1), g)
                    st.n = m * (K - 1)
                    st.done(nc.vector.tensor_scalar(conv[:, b], xpad[:, b, :, 0:S], taps[:, m, 0:1],
                                                    bias_cv[:, m:m + 1], ALU.mult, ALU.add))
                    for k in range(1, K):
                        op = nc.vector.scalar_tensor_tensor(conv[:, b], xpad[:, b, :, k:k + S], taps[:, m, k:k + 1],
                                                            conv[:, b], ALU.mult, ALU.add)
                        if k < K - 1:
                            st.done(op)
                    op.then_inc(conv_ready, 1)

            dve.wait_ge(w_here, 16 * n_loads)
            convolve(0)
            with dve.Fori(1, NG) as g:
                convolve(g)
            dve.wait_ge(end_mm, 1)
            for c4 in range(4):
                rows = slice(NS * c4, NS * (c4 + 1))
                last = nc.vector.tensor_copy(ends[rows], ps_end[rows, 0:NC * B].rearrange(
                    "p (cq c4 b) -> p c4 cq b", c4=4, b=B)[:, c4])
            last.then_inc(ends_ready, 1)
            dve.wait_ge(s_mm, 1)
            nc.vector.tensor_copy(s_all[:], ps_s[:, 0:4 * B].rearrange("p (c b) -> p c b", b=B)).then_inc(s_ready, 1)
            dve.wait_ge(s_ready, 1)
            dve.wait_ge(gated_done, MH * NG)


def attend(nc, T, PS, sem, c, dram):
    gated, s_all = c["gated"], c["s"]
    w, eye, ones, mask = c["w"], c["eye"], c["ones"], c["mask"]
    KT = S // P
    MR = 96
    HH = NH // 2
    VW = 2 * HD
    AL, WL = 3, 5
    SCALE = HD ** -0.5

    xres = T("xres", [P, KT, D], F32)
    ctx = T("ctx", [P, 2, KD, S], F32)
    diag = T("diag", [P, 4, 64], F32)
    y = T("y", [P, MH, S], F32)
    r1 = T("r1", [P, KT, D], F32)
    x1 = T("x1", [P, KT, D], F32)
    x1t = T("x1t", [P, KD, S], F32)
    kq = T("kq", [P, KD, S], F32)
    half = T("half", [P, 2, KD, S], F32R)
    qst = T("qst", [P, 2, NH, S], F32R)
    kst = T("kst", [P, 2, NH, S], F32R)
    vals = T("vals", [P, 2, KT, NH, VW], F32)
    nmax = T("nmax", [P, 2, KT, NH], F32)
    mrow = T("mrow", [NH, S], F32R)
    pt = T("pt", [P, 2, KT, S], F32)
    oraw = T("oraw", [P, 4, S], F32)
    rec = T("rec", [P, NH], F32)
    onrm = T("onrm", [P, KT, D], F32)
    ont = T("ont", [P, KD, S], F32)
    x2t = T("x2t", [P, KD, S], F32)
    pay = T("pay", [P, 2, KT, ROW], F32)
    st1, mv1, ve1 = T("st1", [P, KT, 6], F32), T("mv1", [P, KT, 2], F32), T("ve1", [P, KT], F32)
    st2, mv2, ve2 = T("st2", [P, KT, 6], F32), T("mv2", [P, KT, 2], F32), T("ve2", [P, KT], F32)
    st3, mv3, ve3 = T("st3", [P, KT, 6], F32), T("mv3", [P, KT, 2], F32), T("ve3", [P, KT], F32)
    power = T("power", [P, KT], F32)
    lg, top, where = T("lg", [P, KT, E], F32), T("top", [P, KT, 8], F32), T("where", [P, KT, 8], U32)
    ntop, den, expert = T("ntop", [P, KT], F32), T("den", [P, KT], F32), T("expert", [P, KT], F32)
    el = T("el", [P, KT, E], F32)
    hot, carry = T("hot", [P, KT, E], BF16), T("carry", [P, E], BF16)
    tri, ones_b = T("tri", [P, P], BF16), T("ones_b", [P, P], BF16)
    sel, place = T("sel", [P, KT, E], F32), T("place", [P, KT], F32)
    over, slot0, slot = T("over", [P, KT], F32), T("slot0", [P, KT], F32), T("slot", [P, KT], F32)
    dest = T("dest", [P, 2, KT], I32)
    bq = T("bq", [P, KD], F32)

    ps_m = PS("ps_m", [P, 2, KT, S], F32)
    ps_a = PS("ps_a", [P, 2, KT, S], F32)
    ps_o = PS("ps_o", [P, 4, S], F32)
    ps_d = PS("ps_d", [P, 512], F32)
    ps_e = PS("ps_e", [P, 512], F32)
    hscr = c["hscr"]

    names = """setup_pool setup_dve setup_pe vo_row x_in0 x_in1 ctx_in0 ctx_in1 x_added
        sbc_mm k_mm v_mm wout_mm x1t_mm q_mm mt_mm diag_done y_done k_out q_out k_hi q_hi k_split q_split v_out r1_done var1_ready
        rstd1 x1_done x1_kept x1t_out m_out k_stored q_stored k_in00 k_in01 k_in10 k_in11 q_in00 q_in01 q_in10 q_in11
        m_in max_mm max_done att_mm exp_done pv_mm oraw_lo oraw_hi ot_mm on_done ont_mm ont_out oproj_mm r2_done
        var2_ready rstd2 x2_done x2t_mm x2t_out logit_mm lg_out top_out ntop_out sel_out place_out over_out den_done hot_ready cum_mm carry_ready
        var3_ready rstd3 dest_ready place_done pay_ready sent0 sent1 out_ready out_sent0 out_sent1
        d_step o_step r_step p_step stats1 stats2 stats3""".split()
    s = {n: sem(n) for n in names}
    x_in, ctx_in = [s["x_in0"], s["x_in1"]], [s["ctx_in0"], s["ctx_in1"]]
    k_in, q_in = ([[s[n + str(b) + str(lo)] for lo in range(2)] for b in range(2)] for n in ("k_in", "q_in"))
    sent, out_sent = [s["sent0"], s["sent1"]], [s["out_sent0"], s["out_sent1"]]
    KIN, QIN = 3 * 16, 2 * 16

    FIRST, LAST = 6, B - 3

    def run(eng, step):
        for n in range(-1, FIRST):
            step(n, n % 2)
        with eng.Fori(0, (LAST + 1 - FIRST) // 2) as i:
            step(i * 2 + FIRST, FIRST % 2)
            step(i * 2 + FIRST + 1, (FIRST + 1) % 2)
        for n in range(LAST + 1, B + 4):
            step(n, n % 2)

    def on(n, lag):
        return not isinstance(n, int) or 0 <= n - lag < B

    def use(j, per, parity):
        if isinstance(j, int):
            return (j // 2 + 1) * per
        return j * (per // 2) + (per if parity == 0 else per // 2)

    def settled(eng):
        eng.wait_ge(s["setup_pe"], 1)

    def behind(n, h, slots):
        return (n - 2, h - slots, 2) if h >= slots else (n - 3, h - slots + NH, 3)

    with nc.Block() as block:

        @block.sync
        def _(sp):
            def load_x(j, p):
                settled(sp)
                need(sp, s["x_added"], j)
                sp.dma_start(xres[:], dram["x"][bass.ds(j * S, S), :].rearrange("(t p) d -> p t d", p=P)
                             ).then_inc(x_in[p], 16)

            def load_ctx(j, p):
                settled(sp)
                need(sp, s["k_mm"], j - 1)
                need(sp, s["v_mm"], j - 1)
                sp.dma_start(ctx[:, p], dram["ctx_t"][:, bass.ds(j * S, S)].rearrange("(k p) t -> p k t", p=P)
                             ).then_inc(ctx_in[p], 16)

            def stack(j, p, lo):
                need(sp, s["att_mm"], (j - 2) * NH + HH * (lo + 1))
                heads = slice(HH * lo, HH * (lo + 1))
                for rows, src in ((slice(0, 32), slice(0, 32)), (slice(32, 48), slice(16, 32)),
                                  (slice(48, 64), slice(0, 16))):
                    sp.dma_start(kst[rows, p, heads, :].bitcast(F32), hscr[p, 0, lo][src]).then_inc(k_in[p][lo], 16)
                for rows in (slice(0, 32), slice(32, 64)):
                    sp.dma_start(qst[rows, p, heads, :].bitcast(F32), hscr[p, 1, lo]).then_inc(q_in[p][lo], 16)

            def store(j, p, which, split, stored):
                sp.wait_ge(split, j + 1)
                for m in range(KD):
                    sp.dma_start(hscr[p, which, m].rearrange("(c d) h t -> (d h) c t", c=2),
                                 half[:, :, m, :].bitcast(F32)).then_inc(stored, 16)
                settled(sp)
                sp.wait_ge(stored, j * 32 + 32)

            load_x(0, 0)
            load_ctx(0, 0)

            def step(n, p):
                if on(n, 0) and on(n, -1):
                    load_x(n + 1, 1 - p)
                if on(n, 2):
                    sp.wait_ge(s["m_out"], n - 1)
                    sp.dma_start(qst[MR:MR + 1, p, :, :].bitcast(F32), mrow[:].bitcast(F32)).then_inc(s["m_in"], 16)
                if on(n, 1):
                    stack(n - 1, 1 - p, 1)
                if on(n, 0):
                    if on(n, 2):
                        for lo in range(2):
                            sp.wait_ge(k_in[p][lo], use(n - 2, KIN, p))
                            sp.wait_ge(q_in[p][lo], use(n - 2, QIN, p))
                    store(n, p, 0, s["k_split"], s["k_stored"])
                    store(n, p, 1, s["q_split"], s["q_stored"])
                    stack(n, p, 0)
                if on(n, 0) and on(n, -1):
                    load_ctx(n + 1, 1 - p)
                if on(n, 4):
                    settled(sp)
                    sp.wait_ge(s["out_ready"], n - 3)
                    sp.dma_start(dram["out"][bass.ds((n - 4) * S, S), :].rearrange("(t p) d -> p t d", p=P),
                                 c["twice"][:, p]).then_inc(out_sent[p], 16)

            run(sp, step)
            sp.wait_ge(s["y_done"], B)
            sp.dma_start(c["w1_raw"], dram["w1"][0:D, :].rearrange("(k p) f -> p k f", p=P)).then_inc(c["w1_in"], 16)
            sp.dma_start(c["w2_raw"], dram["w2"][0:F, :].rearrange("(k p) d -> p k d", p=P)).then_inc(c["w2_in"], 16)
            sp.wait_ge(out_sent[0], B // 2 * 16)
            sp.wait_ge(out_sent[1], B // 2 * 16)

        @block.gpsimd
        def _(pool):
            nc.gpsimd.memset(power[:], -0.5).then_inc(s["setup_pool"], 1)
            pool.wait_ge(s["setup_pool"], 1)
            nc.gpsimd.memset(kst[64:P, :, :, :].bitcast(F32), 1.0).then_inc(s["setup_pool"], 1)
            pool.wait_ge(s["setup_pool"], 2)
            pool.wait_ge(c["rows_blank"], 16)

            def residual(j, p):
                pool.wait_ge(x_in[p], use(j, 16, p))
                own = Steps(pool, s["p_step"], 1, j)
                need(pool, s["r1_done"], j)
                own.done(nc.gpsimd.tensor_tensor(c["x2b"][:], xres[:],
                                                c["b_out"][:, None, :].to_broadcast([P, KT, D]), ALU.add))
                nc.gpsimd.tensor_tensor(c["x2b"][:], c["x2b"][:], xres[:], ALU.add).then_inc(s["x_added"], 1)

            def split_lo(j, hi, done):
                pool.wait_ge(hi, j + 1)
                nc.gpsimd.tensor_tensor(half[:, 1], kq[:], half[:, 0].bitcast(F32), ALU.subtract).then_inc(done, 1)

            residual(0, 0)

            def step(n, p):
                q = 1 - p
                if on(n, 0):
                    pool.wait_ge(s["var1_ready"], n + 1)
                    nc.gpsimd.tensor_tensor(ve1[:], ve1[:], power[:], ALU.pow).then_inc(s["rstd1"], 1)
                if on(n, 0):
                    pool.wait_ge(s["x1_done"], n + 1)
                    if isinstance(n, int) and n == 0:
                        pool.wait_ge(s["vo_row"], 1)
                    nc.gpsimd.tensor_tensor(gated[:, 0:KT, bass.ds(n * S, S)], x1[:],
                                            c["b_o"][:, None, :].to_broadcast([P, KT, D]), ALU.add
                                            ).then_inc(s["x1_kept"], 1)
                    split_lo(n, s["k_hi"], s["k_split"])
                if on(n, 4):
                    pool.wait_ge(s["var3_ready"], n - 3)
                    need(pool, out_sent[p], use(n - 4, 16, p) - 16)
                    nc.gpsimd.tensor_tensor(ve3[:], ve3[:], power[:], ALU.pow).then_inc(s["rstd3"], 1)
                    settled(pool)
                    pool.wait_ge(s["rstd3"], n - 3)
                    for t in range(KT):
                        op = nc.gpsimd.tensor_scalar(c["twice"][:, p, t, :], pay[:, p, t, 0:D], mv3[:, t, 0:1],
                                                     ve3[:, t:t + 1], ALU.subtract, ALU.mult)
                    op.then_inc(s["out_ready"], 1)
                if on(n, 0):
                    split_lo(n, s["q_hi"], s["q_split"])
                if on(n, 4):
                    settled(pool)
                    pool.wait_ge(s["dest_ready"], n - 3)
                    pool.wait_ge(s["pay_ready"], n - 3)
                    for t in range(KT):
                        nc.gpsimd.indirect_dma_start(
                            out=dram["rows"], out_offset=bass.IndirectOffsetOnAxis(ap=dest[:, p, t:t + 1], axis=0),
                            in_=pay[:, p, t, :], in_offset=None, bounds_check=E * CAP - 1, oob_is_err=False,
                        ).then_inc(sent[p], 16)
                if on(n, 0) and on(n, -1):
                    residual(n + 1, q)
                if on(n, 3):
                    j = n - 3
                    pool.wait_ge(s["var2_ready"], j + 1)
                    nc.gpsimd.tensor_tensor(ve2[:], ve2[:], power[:], ALU.pow).then_inc(s["rstd2"], 1)

            run(pool, step)
            pool.wait_ge(sent[0], B // 2 * KT * 16)
            pool.wait_ge(sent[1], B // 2 * KT * 16)

        @block.tensor
        def _(pe):
            pe.wait_ge(c["loaded"], 16 * len(c["loads"]))
            for k in range(KD):
                mm = pe.matmul(ps_d[:, 0:D], c["bv_rep"][:, k, :], w["o"][:, k, :], start=(k == 0), stop=(k == KD - 1))
            mm.then_inc(s["setup_pe"], 1)
            pe.wait_ge(s["setup_dve"], 7)
            pe.wait_ge(s["setup_pool"], 2)

            def spread_s(j):
                pe.wait_ge(s["diag_done"], j + 1)
                need(pe, s["v_out"], j - 1)
                need(pe, s["q_out"], j)
                pe.matmul(ps_d[:, 0:S], ones[:], diag[:].rearrange("p c i -> p (c i)"), start=True, stop=True
                          ).then_inc(s["sbc_mm"], 1)

            def keys(j, p, m):
                if m == 0:
                    pe.wait_ge(ctx_in[p], use(j, 16, p))
                    pe.wait_ge(s["r1_done"], j + 1)
                for k in range(KD):
                    mm = pe.matmul(ps_d[:, m * S:(m + 1) * S], w["k"][:, k, m * P:(m + 1) * P], ctx[:, p, k, :],
                                   start=(k == 0), stop=(k == KD - 1), skip_group_check=True)
                if m == KD - 1:
                    mm.then_inc(s["k_mm"], 1)

            def values(j, p, t, dense):
                if t == 0 and dense is not None:
                    pe.wait_ge(s["q_out"], dense + 1)
                for k in range(KD):
                    mm = pe.matmul(ps_d[:, t * D:(t + 1) * D], ctx[:, p, k, t * P:(t + 1) * P], w["v"][:, k, :],
                                   start=(k == 0), stop=(k == KD - 1), skip_group_check=True)
                if t == KT - 1:
                    mm.then_inc(s["v_mm"], 1)

            def mixer_out(j, t):
                if t == 0:
                    pe.wait_ge(s["y_done"], j + 1)
                for m in range(MH):
                    mm = pe.matmul(ps_d[:, t * D:(t + 1) * D], y[:, m, t * P:(t + 1) * P], w["out"][:, m, :],
                                   start=(m == 0), stop=(m == MH - 1), skip_group_check=True)
                if t == KT - 1:
                    mm.then_inc(s["wout_mm"], 1)

            def turn(ps, src, done):
                for t in range(KT):
                    for k in range(KD):
                        mm = pe.transpose(ps[:, k * S + t * P:k * S + (t + 1) * P], src[:, t, k * P:(k + 1) * P], eye[:])
                mm.then_inc(done, 1)

            def queries(j, m):
                if m == 0:
                    pe.wait_ge(s["x1t_out"], j + 1)
                for k in range(KD):
                    mm = pe.matmul(ps_d[:, m * S:(m + 1) * S], w["q"][:, k, m * P:(m + 1) * P], x1t[:, k, :],
                                   start=(k == 0), stop=(k == KD - 1), skip_group_check=True)
                if m == KD - 1:
                    mm.then_inc(s["q_mm"], 1)

            def maxima_rows(j, p):
                pe.wait_ge(s["max_done"], NH * j + NH)
                for t in range(KT):
                    mm = pe.transpose(ps_m[0:NH, p, 0, t * P:(t + 1) * P], nmax[:, p, t, :], eye[:])
                mm.then_inc(s["mt_mm"], 1)

            def scores(j, p, h):
                if h % HH == 0:
                    pe.wait_ge(q_in[p][h // HH], use(j, QIN, p))
                    pe.wait_ge(k_in[p][h // HH], use(j, KIN, p))
                if h == 2:
                    need(pe, s["m_out"], j)
                else:
                    need(pe, s["max_done"], NH * j + (h if h == 1 else h - 1))
                for t in range(KT):
                    mm = pe.matmul(ps_m[:, (h + (h > 0) + p) % 2, t, :], qst[0:MR, p, h, t * P:(t + 1) * P],
                                   kst[0:MR, p, h, :], start=True, stop=True, skip_group_check=True)
                mm.then_inc(s["max_mm"], 1)

            def scores_t(j, p, h):
                if h == 0:
                    pe.wait_ge(s["m_in"], j * 16 + 16)
                need(pe, s["exp_done"], NH * j + h - 1)
                for t in range(KT):
                    mm = pe.matmul(ps_a[:, h % 2, t, :], kst[:, p, h, t * P:(t + 1) * P], qst[:, p, h, :],
                                   start=True, stop=True, skip_group_check=True)
                mm.then_inc(s["att_mm"], 1)

            def weigh(j, p, h):
                pe.wait_ge(s["exp_done"], NH * j + h + 1)
                if h == 0:
                    pe.wait_ge(s["v_out"], j + 1)
                    need(pe, s["oraw_lo"], j)
                if h == HH:
                    need(pe, s["oraw_hi"], j)
                for t in range(KT):
                    mm = pe.matmul(ps_o[VW * (h % 4):VW * (h % 4 + 1), h // 4, :], vals[:, p, t, h, :],
                                   pt[:, h % 2, t, :],
                                   start=(t == 0), stop=(t == KT - 1), skip_group_check=True)
                mm.then_inc(s["pv_mm"], 1)

            def sums_by_query(j, t):
                if t == 0:
                    pe.wait_ge(s["oraw_hi"], j + 1)
                    need(pe, s["place_done"], j)
                else:
                    pe.wait_ge(s["on_done"], 2 * j + 1)
                for g in range(4):
                    mm = pe.transpose(ps_e[:, g * P:(g + 1) * P], oraw[:, g, t * P:(t + 1) * P], eye[:])
                mm.then_inc(s["ot_mm"], 1)

            def project_out(j, t):
                if t == 0:
                    pe.wait_ge(s["ont_out"], j + 1)
                for k in range(KD):
                    mm = pe.matmul(ps_e[:, t * D:(t + 1) * D], ont[:, k, t * P:(t + 1) * P], w["o"][:, k, :],
                                   start=(k == 0), stop=(k == KD - 1), skip_group_check=True)
                if t == KT - 1:
                    mm.then_inc(s["oproj_mm"], 1)

            def router(j):
                pe.wait_ge(s["x2t_out"], j + 1)
                for t in range(KT):
                    for k in range(KD):
                        mm = pe.matmul(ps_e[:, t * E:(t + 1) * E], x2t[:, k, t * P:(t + 1) * P], w["r"][:, k, :],
                                       start=(k == 0), stop=(k == KD - 1), skip_group_check=True)
                mm.then_inc(s["logit_mm"], 1)

            def count(j):
                pe.wait_ge(s["hot_ready"], j + 1)
                need(pe, s["carry_ready"], j)
                for t in range(KT):
                    here = ps_e[:, t * E:(t + 1) * E]
                    pe.matmul(here, tri[:], hot[:, t, :], start=True, stop=False, skip_group_check=True)
                    if t:
                        pe.matmul(here, ones_b[:], hot[:, 0, :], start=False, stop=False, skip_group_check=True)
                    mm = pe.matmul(here, ones_b[:], carry[:], start=False, stop=True, skip_group_check=True)
                mm.then_inc(s["cum_mm"], 1)

            def step(n, p):
                q = 1 - p
                for h in range(NH):
                    if on(n, 1):
                        scores(n - 1, q, h)
                    if h == 0 and on(n, 2):
                        maxima_rows(n - 2, p)
                    j, head, lag = behind(n, h, AL)
                    if on(n, lag):
                        scores_t(j, p if lag == 2 else q, head)
                    if h == 12 and on(n, -1):
                        spread_s(n + 1)
                    if h in (14, 15) and on(n, -1):
                        mixer_out(n + 1, h - 14)
                    if h in (1, 2) and on(n, 0):
                        keys(n, p, h - 1)
                    if h == 5 and on(n, 0):
                        pe.wait_ge(s["k_out"], n + 1)
                        pe.wait_ge(s["x1_done"], n + 1)
                        turn(ps_d, x1, s["x1t_mm"])
                    if h == 7 and on(n, 0):
                        queries(n, 0)
                        queries(n, 1)
                    if h in (9, 10) and on(n, 1):
                        values(n - 1, q, h - 9, n if on(n, 0) else None)
                    if h == 5 and on(n, 4):
                        count(n - 4)
                    if h in (7, 9) and on(n, 3):
                        sums_by_query(n - 3, (h - 7) // 2)
                    if h == 11 and on(n, 3):
                        pe.wait_ge(s["on_done"], 2 * (n - 3) + 2)
                        turn(ps_e, onrm, s["ont_mm"])
                    if h in (12, 13) and on(n, 3):
                        project_out(n - 3, h - 12)
                    if h == 1 and on(n, 4):
                        pe.wait_ge(s["x2_done"], n - 3)
                        turn(ps_e, pay[:, p], s["x2t_mm"])
                    if h == 2 and on(n, 4):
                        router(n - 4)
                    j, head, lag = behind(n, h, WL)
                    if on(n, lag):
                        weigh(j, p if lag == 2 else q, head)

            run(pe, step)

        @block.scalar
        def _(act):
            act.wait_ge(c["loaded"], 16 * len(c["loads"]))

            def add_bias(bias, out):
                for m in range(KD):
                    op = nc.scalar.activation(kq[:, m, :], ps_d[:, m * S:(m + 1) * S], ACT.Identity,
                                              bias=bias[:, m:m + 1])
                op.then_inc(out, 1)

            def split_hi(j, out, hi, stored, before):
                act.wait_ge(out, j + 1)
                need(act, stored, before)
                nc.scalar.copy(half[:, 0], kq[:]).then_inc(hi, 1)

            def sums_out(j, half_of, done):
                act.wait_ge(s["pv_mm"], NH * j + HH * (half_of + 1))
                need(act, s["ot_mm"], 2 * j)
                two = slice(2 * half_of, 2 * half_of + 2)
                nc.scalar.copy(oraw[:, two].rearrange("p g t -> p (g t)"), ps_o[:, two].rearrange("p g t -> p (g t)")
                               ).then_inc(done, 1)

            def step(n, p):
                q = 1 - p
                for h in range(NH):
                    if h == 1 and on(n, 2):
                        act.wait_ge(s["mt_mm"], n - 1)
                        need(act, s["m_in"], 16 * (n - 2))
                        nc.scalar.copy(mrow[:], ps_m[0:NH, p, 0, :]).then_inc(s["m_out"], 1)
                    if h == 4 and on(n, 0):
                        split_hi(n, s["k_out"], s["k_hi"], s["q_stored"], 32 * n)
                    if h == 9 and on(n, 0):
                        split_hi(n, s["q_out"], s["q_hi"], s["k_stored"], 32 * n + 32)
                    if h == 5 and on(n, 4):
                        j = n - 4
                        act.wait_ge(s["ntop_out"], j + 1)
                        need(act, s["pay_ready"], j)
                        for t in range(KT):
                            op = nc.scalar.activation(el[:, t, :], lg[:, t, :], ACT.Exp, bias=ntop[:, t:t + 1],
                                                      accum_out=den[:, t:t + 1])
                        op.then_inc(s["den_done"], 1)
                    if h == 3 and on(n, 0):
                        act.wait_ge(s["k_mm"], n + 1)
                        need(act, s["q_split"], n)
                        add_bias(c["b_k"], s["k_out"])
                    if h == 6 and on(n, 0):
                        act.wait_ge(s["x1t_mm"], n + 1)
                        nc.scalar.copy(x1t[:].rearrange("p k t -> p (k t)"), ps_d[:]).then_inc(s["x1t_out"], 1)
                    if h == WL and on(n, 3):
                        sums_out(n - 3, 1, s["oraw_hi"])
                    if h == 8 and on(n, 0):
                        act.wait_ge(s["q_mm"], n + 1)
                        act.wait_ge(s["k_split"], n + 1)
                        if isinstance(n, int) and n == 0:
                            act.wait_ge(s["setup_dve"], 7)
                        add_bias(bq, s["q_out"])
                    if h == 12 and on(n, 3):
                        act.wait_ge(s["ont_mm"], n - 2)
                        nc.scalar.copy(ont[:].rearrange("p k t -> p (k t)"), ps_e[:]).then_inc(s["ont_out"], 1)
                    if h == 11 and on(n, 1):
                        act.wait_ge(s["v_mm"], n)
                        need(act, s["pv_mm"], NH * (n - 2))
                        nc.scalar.copy(vals[:, q, :, :, 0:HD], ps_d[:].rearrange("p (t h d) -> p t h d", t=KT, h=NH)
                                       ).then_inc(s["v_out"], 1)
                    if h == WL + HH and on(n, 2):
                        sums_out(n - 2, 0, s["oraw_lo"])
                    if h == 2 and on(n, 4):
                        act.wait_ge(s["x2t_mm"], n - 3)
                        nc.scalar.copy(x2t[:].rearrange("p k t -> p (k t)"), ps_e[:]).then_inc(s["x2t_out"], 1)
                    j, head, lag = behind(n, h, AL)
                    if on(n, lag):
                        act.wait_ge(s["att_mm"], NH * j + head + 1)
                        need(act, s["pv_mm"], NH * j + head - 1)
                        nc.scalar.activation(pt[:, head % 2].rearrange("p t q -> p (t q)"),
                                             ps_a[:, head % 2].rearrange("p t q -> p (t q)"), ACT.Exp
                                             ).then_inc(s["exp_done"], 1)

            run(act, step)

        @block.vector
        def _(dve):
            nc.vector.memset(vals[:, :, :, :, HD:VW], 1.0).then_inc(s["setup_dve"], 1)
            nc.vector.memset(carry[:], 0.0).then_inc(s["setup_dve"], 1)
            nc.vector.memset(qst[64:P, :, :, :].bitcast(F32), 0.0).then_inc(s["setup_dve"], 1)
            dve.wait_ge(c["loaded"], 16 * len(c["loads"]))
            nc.vector.tensor_scalar(w["q"][:], w["q"][:], SCALE, None, ALU.mult).then_inc(s["setup_dve"], 1)
            nc.vector.tensor_scalar(bq[:], c["b_q"][:], SCALE, None, ALU.mult).then_inc(s["setup_dve"], 1)
            nc.vector.tensor_copy(tri[:], c["tri"][:]).then_inc(s["setup_dve"], 1)
            nc.vector.tensor_copy(ones_b[:], ones[:]).then_inc(s["setup_dve"], 1)
            dve.wait_ge(s["setup_pe"], 1)
            nc.vector.tensor_tensor(c["b_o"][:], c["b_o"][:], ps_d[:, 0:D], ALU.add).then_inc(s["vo_row"], 1)
            dve.wait_ge(s["setup_dve"], 7)
            dve.wait_ge(s["setup_pool"], 2)
            dve.wait_ge(s["vo_row"], 1)

            def stats(st, src, stats_done):
                for t in range(KT):
                    op = nc.vector.bn_stats(st[:, t, :], src[:, t, 0:D])
                op.then_inc(stats_done, 1)

            def mean_var(chain, st, mv, stats_done, batch):
                dve.wait_ge(s["vo_row"], 1)
                dve.wait_ge(stats_done, batch + 1)
                for t in range(KT):
                    op = nc.vector.bn_aggr(mv[:, t, :], st[:, t, :])
                chain.done(op)

            def step(n, p):
                q = 1 - p
                j, i = n - 3, n - 4
                dc = Steps(dve, s["d_step"], 1, n)
                oc = Steps(dve, s["o_step"], 3, j)
                rc = Steps(dve, s["r_step"], 4, i)
                for h in range(NH):
                    if on(n, 1):
                        dve.wait_ge(s["max_mm"], NH * (n - 1) + h + 1)
                        nc.vector.tensor_reduce(nmax[:, q, :, h], ps_m[:, (h + (h > 0) + q) % 2], AX.X, ALU.max,
                                                negate=True).then_inc(s["max_done"], 1)
                    if h == 0 and on(n, 0):
                        dve.wait_ge(s["wout_mm"], n + 1)
                        dve.wait_ge(s["x_added"], n + 1)
                        nc.vector.tensor_tensor(r1[:].rearrange("p t d -> p (t d)"), ps_d[:],
                                                c["x2b"][:].rearrange("p t d -> p (t d)"), ALU.add
                                                ).then_inc(s["r1_done"], 1)
                    if h == 0 and on(n, 4):
                        dve.wait_ge(s["rstd2"], i + 1)
                        need(dve, sent[p], use(i, 32, p) - 32)
                        need(dve, s["out_ready"], i - 1)
                        for t in range(KT):
                            op = nc.vector.tensor_scalar(pay[:, p, t, 0:D], c["r2"][:, t, :], mv2[:, t, 0:1],
                                                         ve2[:, t:t + 1], ALU.subtract, ALU.mult)
                        op.then_inc(s["x2_done"], 1)
                        nc.vector.tensor_copy(pay[:, p, :, D], c["tokens"][:, bass.ds(i * KT, KT)])
                    if h == 0 and on(n, 0):
                        dve.wait_ge(s["r1_done"], n + 1)
                        stats(st1, r1, s["stats1"])
                    if h == 1 and on(n, 0):
                        mean_var(dc, st1, mv1, s["stats1"], n)
                        nc.vector.tensor_scalar(ve1[:], mv1[:, :, 1], EPS, None, ALU.add).then_inc(s["var1_ready"], 1)
                    if h == 2 and on(n, 4):
                        dve.wait_ge(s["x2_done"], i + 1)
                        need(dve, s["out_ready"], i)
                        stats(st3, pay[:, p], s["stats3"])
                    if h == 3 and on(n, 0):
                        dve.wait_ge(s["rstd1"], n + 1)
                        need(dve, s["x1_kept"], n)
                        for t in range(KT):
                            op = nc.vector.tensor_scalar(x1[:, t, :], r1[:, t, :], mv1[:, t, 0:1], ve1[:, t:t + 1],
                                                         ALU.subtract, ALU.mult)
                        op.then_inc(s["x1_done"], 1)
                    if h == 3 and on(n, 4):
                        mean_var(rc, st3, mv3, s["stats3"], i)
                        nc.vector.tensor_scalar(ve3[:], mv3[:, :, 1], EPS / 4, None, ALU.add
                                                ).then_inc(s["var3_ready"], 1)
                    if h == 3 and on(n, 4):
                        dve.wait_ge(s["logit_mm"], i + 1)
                        nc.vector.tensor_copy(lg[:].rearrange("p t e -> p (t e)"), ps_e[:, 0:KT * E]).then_inc(s["lg_out"], 1)
                        dve.wait_ge(s["vo_row"], 1)
                        dve.wait_ge(s["lg_out"], i + 1)
                        for t in range(KT):
                            op = nc.vector.max(top[:, t, :], lg[:, t, :])
                        op.then_inc(s["top_out"], 1)
                    if h == 4 and on(n, 4):
                        dve.wait_ge(s["top_out"], i + 1)
                        nc.vector.tensor_scalar(ntop[:], top[:, :, 0], -1.0, None, ALU.mult).then_inc(s["ntop_out"], 1)
                        for t in range(KT):
                            op = nc.vector.max_index(where[:, t, :], top[:, t, :], lg[:, t, :])
                        rc.done(op)
                        rc.done(nc.vector.tensor_copy(expert[:], where[:, :, 0]))
                        for t in range(KT):
                            op = nc.vector.tensor_scalar(hot[:, t, :], c["kinds"][:], expert[:, t:t + 1], None, ALU.is_equal)
                        op.then_inc(s["hot_ready"], 1)
                        rc.done(nc.vector.tensor_scalar(slot0[:], expert[:], float(CAP), -1.0, ALU.mult, ALU.add))
                    if h == 6 and on(n, 4):
                        dve.wait_ge(s["cum_mm"], n - 3)
                        nc.vector.tensor_tensor(sel[:].rearrange("p t e -> p (t e)"), ps_e[:, 0:KT * E],
                                                hot[:].rearrange("p t e -> p (t e)"), ALU.mult).then_inc(s["sel_out"], 1)
                        nc.vector.tensor_tensor(carry[:], carry[:], hot[:, 0, :], ALU.add).then_inc(s["place_done"], 1)
                    if h == 7 and on(n, 4):
                        dve.wait_ge(s["sel_out"], n - 3)
                        nc.vector.tensor_reduce(place[:], sel[:], AX.X, ALU.add).then_inc(s["place_out"], 1)
                        dve.wait_ge(s["place_done"], n - 3)
                        nc.vector.tensor_tensor(carry[:], carry[:], hot[:, 1, :], ALU.add).then_inc(s["carry_ready"], 1)
                    if h == 8 and on(n, 4):
                        dve.wait_ge(s["place_out"], n - 3)
                        nc.vector.tensor_scalar(over[:], place[:], float(CAP), FAR, ALU.is_gt, ALU.mult)
                        nc.vector.tensor_tensor(slot[:], slot0[:], place[:], ALU.add).then_inc(s["over_out"], 1)
                        dve.wait_ge(s["den_done"], n - 3)
                        nc.vector.reciprocal(pay[:, p, :, D + 1], den[:]).then_inc(s["pay_ready"], 1)
                    if h == 9 and on(n, 4):
                        dve.wait_ge(s["over_out"], n - 3)
                        nc.vector.tensor_tensor(dest[:, p, :], slot[:], over[:], ALU.add).then_inc(s["dest_ready"], 1)
                    if h in (8, 10) and on(n, 3):
                        t = (h - 8) // 2
                        dve.wait_ge(s["ot_mm"], 2 * j + t + 1)
                        if t == 0:
                            need(dve, s["ont_mm"], j)
                        o4 = ps_e[:].rearrange("p (h w) -> p h w", w=VW)
                        oc.done(nc.vector.reciprocal(rec[:], o4[:, :, HD]))
                        nc.vector.tensor_tensor(onrm[:, t].rearrange("p (h d) -> p h d", d=HD), o4[:, :, 0:HD],
                                                rec[:, :, None].to_broadcast([P, NH, HD]), ALU.mult
                                                ).then_inc(s["on_done"], 1)
                    if h == 14 and on(n, 3):
                        dve.wait_ge(s["oproj_mm"], j + 1)
                        dve.wait_ge(s["x1_kept"], j + 1)
                        nc.vector.tensor_tensor(c["r2"][:], ps_e[:].rearrange("p (t d) -> p t d", t=KT),
                                                gated[:, 0:KT, bass.ds(j * S, S)], ALU.add).then_inc(s["r2_done"], 1)
                        dve.wait_ge(s["r2_done"], j + 1)
                        stats(st2, c["r2"], s["stats2"])
                    if h == 15 and on(n, 3):
                        mean_var(oc, st2, mv2, s["stats2"], j)
                        nc.vector.tensor_scalar(ve2[:], mv2[:, :, 1], EPS, None, ALU.add).then_inc(s["var2_ready"], 1)
                    if h == 11 and on(n, -1):
                        need(dve, s["sbc_mm"], n + 1)
                        nc.vector.tensor_tensor(diag[:], s_all[:, :, bass.ds(n + 1, 1)].to_broadcast([P, 4, 64]),
                                                mask[:, None, :].to_broadcast([P, 4, 64]), ALU.mult
                                                ).then_inc(s["diag_done"], 1)
                    if h == 13 and on(n, -1):
                        dve.wait_ge(s["sbc_mm"], n + 2)
                        for m in range(MH):
                            op = nc.vector.scalar_tensor_tensor(y[:, m, :], ps_d[:, 0:S], c["d_col"][:, m:m + 1],
                                                                gated[:, m, bass.ds((n + 1) * S, S)], ALU.add, ALU.mult)
                        op.then_inc(s["y_done"], 1)

            run(dve, step)
            dve.wait_ge(s["carry_ready"], B)


def experts(nc, T, PS, sem, c, dram):
    eye = c["eye"]
    TS = CAP // P
    FT = F // P
    HC = CAP // 2
    HI, LO = 0, 1
    PARTS = ((HI, HI), (HI, LO), (LO, HI))

    gated = c["gated"]
    w1_raw, w2_raw = c["w1_raw"], c["w2_raw"]
    res = gated[:, 0, 0:TS * D].rearrange("p (t d) -> p t d", t=TS)
    new = gated[:, 1, 0:2 * TS * D].rearrange("p (b t d) -> p b t d", b=2, t=TS)
    rows = gated[:, 3, 0:2 * TS * ROW].rearrange("p (b t r) -> p b t r", b=2, t=TS)
    w1 = [T("w1_hi", [P, 2, KD, F], F32R), T("w1_lo", [P, 2, KD, F], F32R)]
    w2 = [T("w2_hi", [P, 2, FT, D], F32R), T("w2_lo", [P, 2, FT, D], F32R)]
    xt = T("xt3", [P, 2, 2, KD, CAP], F32R)
    hid = T("hid", [P, 2, FT, CAP], F32R)
    st, mv, ve = T("st4", [P, TS, 6], F32), T("mv4", [P, TS, 2], F32), T("ve4", [P, TS], F32)
    power = T("power4", [P, TS], F32)
    token = T("token", [P, 2, TS], I32)

    ps_t = PS("ps_t", [P, 2, 512], F32)
    ps_h = PS("ps_h", [P, 2, 2, 512], F32)
    ps_y = PS("ps_y", [P, 2, 512], F32)

    names = """rows_in0 rows_in1 turn_mm turn_hi turn_lo hid_mm hid_hi hid_lo w1_hi w1_lo w2_hi w2_lo out_mm res_done
        var_ready rstd new_done sent0 sent1 step3 token_done setup3 stats_done""".split()
    s = {n: sem("e_" + n) for n in names}
    rows_in, sent = ([s[n + str(i)] for i in range(2)] for n in ("rows_in", "sent"))
    w1_in, w2_in = c["w1_in"], c["w2_in"]
    TURNS = (TS + 1) // 2

    def use(e, per, parity):
        if isinstance(e, int):
            return (e // 2 + 1) * per
        return e * (per // 2) + (per if parity == 0 else per // 2)

    def run(eng, step):
        step(0, 0)
        step(1, 1)
        with eng.Fori(1, E // 2 - 1) as i:
            step(i * 2, 0)
            step(i * 2 + 1, 1)
        step(E - 2, 0)
        step(E - 1, 1, last=True)

    def flat(x):
        return x.rearrange("p a b -> p (a b)")

    with nc.Block() as block:

        @block.sync
        def _(sp):
            def step(e, p, last=False):
                first = isinstance(e, int) and e == 0
                if not first:
                    sp.wait_ge(s["setup3"], 1)
                    sp.wait_ge(s["w1_lo"], e)
                    sp.dma_start(w1_raw, dram["w1"][bass.ds(e * D, D), :].rearrange("(k p) f -> p k f", p=P)
                                 ).then_inc(w1_in, 16)
                    sp.wait_ge(s["setup3"], 1)
                    sp.wait_ge(s["w2_lo"], e)
                    sp.dma_start(w2_raw, dram["w2"][bass.ds(e * F, F), :].rearrange("(k p) d -> p k d", p=P)
                                 ).then_inc(w2_in, 16)
                    sp.wait_ge(s["setup3"], 1)
                need(sp, s["res_done"], (e - 1) * TS)
                need(sp, s["token_done"], e - 1)
                sp.dma_start(rows[:, p], dram["rows"][bass.ds(e * CAP, CAP), :].rearrange("(t p) r -> p t r", p=P)
                             ).then_inc(rows_in[p], 16)

            run(sp, step)

        @block.tensor
        def _(pe):
            def turn_rows(e, p):
                pe.wait_ge(rows_in[p], use(e, 16, p))
                for i in range(TURNS):
                    need(pe, s["turn_lo"], e * TURNS + i - 1)
                    for t in range(2 * i, min(2 * i + 2, TS)):
                        for k in range(KD):
                            mm = pe.transpose(ps_t[:, (p * TURNS + i) % 2, (t % 2) * D + k * P:(t % 2) * D + (k + 1) * P],
                                              rows[:, p, t, k * P:(k + 1) * P], eye[:])
                    mm.then_inc(s["turn_mm"], 1)

            def hidden(e, p):
                pe.wait_ge(s["w1_lo"], e + 1)
                pe.wait_ge(s["turn_lo"], (e + 1) * TURNS)
                for f in range(FT):
                    need(pe, s["hid_lo"], e * FT + f - 1)
                    for c2 in range(2):
                        for n, (a, b) in enumerate(PARTS):
                            for k in range(KD):
                                mm = pe.matmul(ps_h[:, f % 2, c2, 0:HC], w1[a][:, p, k, f * P:(f + 1) * P],
                                               xt[:, b, p, k, c2 * HC:(c2 + 1) * HC], start=(n == 0 and k == 0),
                                               stop=(n == 2 and k == KD - 1))
                    mm.then_inc(s["hid_mm"], 1)

            def down(e, p):
                pe.wait_ge(s["w2_lo"], e + 1)
                pe.wait_ge(s["hid_lo"], (e + 1) * FT)
                for t in range(TS):
                    need(pe, s["res_done"], e * TS + t - 1)
                    for n, (a, b) in enumerate(PARTS):
                        for f in range(FT):
                            mm = pe.matmul(ps_y[:, (p + t) % 2, 0:D], hid[:, a, f, t * P:(t + 1) * P], w2[b][:, p, f, :],
                                           start=(n == 0 and f == 0), stop=(n == 2 and f == FT - 1))
                    mm.then_inc(s["out_mm"], 1)

            turn_rows(0, 0)

            def step(e, p, last=False):
                hidden(e, p)
                if not last:
                    turn_rows(e + 1, 1 - p)
                down(e, p)

            run(pe, step)

        def turned(e, p, i):
            n = min(2, TS - 2 * i)
            src = ps_t[:, (p * TURNS + i) % 2, 0:n * D].rearrange("p (t k c) -> p t k c", t=n, k=KD)
            return src, [xt[:, part, p, :, 2 * i * P:(2 * i + n) * P].rearrange("p k (t c) -> p t k c", t=n)
                         for part in range(2)]

        @block.scalar
        def _(act):
            def x_hi(e, p):
                for i in range(TURNS):
                    act.wait_ge(s["turn_mm"], e * TURNS + i + 1)
                    need(act, s["hid_mm"], (e - 1) * FT)
                    src, dst = turned(e, p, i)
                    nc.scalar.copy(dst[HI], src).then_inc(s["turn_hi"], 1)

            def w1_hi(e, p):
                act.wait_ge(w1_in, 16 * e + 16)
                need(act, s["hid_mm"], (e - 1) * FT)
                nc.scalar.copy(flat(w1[HI][:, p]), flat(w1_raw)).then_inc(s["w1_hi"], 1)

            def w2_hi(e, p):
                act.wait_ge(w2_in, 16 * e + 16)
                need(act, s["out_mm"], (e - 1) * TS)
                nc.scalar.copy(flat(w2[HI][:, p]), flat(w2_raw)).then_inc(s["w2_hi"], 1)

            w1_hi(0, 0)
            x_hi(0, 0)
            w2_hi(0, 0)

            def step(e, p, last=False):
                for f in range(FT):
                    act.wait_ge(s["hid_mm"], e * FT + f + 1)
                    need(act, s["out_mm"], e * TS)
                    nc.scalar.activation(hid[:, HI, f, :].rearrange("p (c n) -> p c n", c=2), ps_h[:, f % 2, :, 0:HC],
                                         ACT.Relu).then_inc(s["hid_hi"], 1)
                if not last:
                    x_hi(e + 1, 1 - p)
                    w1_hi(e + 1, 1 - p)
                    w2_hi(e + 1, 1 - p)

            run(act, step)

        @block.vector
        def _(dve):
            def x_lo(e, p):
                for i in range(TURNS):
                    dve.wait_ge(s["turn_hi"], e * TURNS + i + 1)
                    src, dst = turned(e, p, i)
                    nc.vector.tensor_tensor(dst[LO], src, dst[HI].bitcast(F32), ALU.subtract).then_inc(s["turn_lo"], 1)

            def w1_lo(e, p):
                dve.wait_ge(s["w1_hi"], e + 1)
                nc.vector.tensor_tensor(flat(w1[LO][:, p]), flat(w1_raw), flat(w1[HI][:, p]).bitcast(F32),
                                        ALU.subtract).then_inc(s["w1_lo"], 1)

            def mean_var(e, p):
                chain = Steps(dve, s["step3"], 1, e)
                dve.wait_ge(s["res_done"], 1)
                dve.wait_ge(s["stats_done"], e + 1)
                for t in range(TS):
                    op = nc.vector.bn_aggr(mv[:, t, :], st[:, t, :])
                chain.done(op)
                need(dve, sent[p], use(e, 16 * TS, p) - 16 * TS)
                nc.vector.tensor_copy(token[:, p, :], rows[:, p, :, D]).then_inc(s["token_done"], 1)
                nc.vector.tensor_scalar(ve[:], mv[:, :, 1], EPS, None, ALU.add).then_inc(s["var_ready"], 1)

            def norm(e, p, t):
                if t == 0:
                    dve.wait_ge(s["rstd"], e + 1)
                op = nc.vector.tensor_scalar(new[:, p, t, :], res[:, t, :], mv[:, t, 0:1], ve[:, t:t + 1],
                                             ALU.subtract, ALU.mult)
                if t == TS - 1:
                    op.then_inc(s["new_done"], 1)

            w1_lo(0, 0)
            x_lo(0, 0)

            def step(e, p, last=False):
                before = not isinstance(e, int) or e > 0
                for f in range(FT):
                    dve.wait_ge(s["hid_hi"], e * FT + f + 1)
                    nc.vector.scalar_tensor_tensor(
                        hid[:, LO, f, :].rearrange("p (c n) -> p c n", c=2), ps_h[:, f % 2, :, 0:HC], 0.0,
                        hid[:, HI, f, :].rearrange("p (c n) -> p c n", c=2).bitcast(F32), ALU.max, ALU.subtract
                    ).then_inc(s["hid_lo"], 1)
                    if f == 0 and before:
                        mean_var(e - 1, 1 - p)
                    if 1 < f < 2 + TS and before:
                        norm(e - 1, 1 - p, f - 2)
                if not last:
                    x_lo(e + 1, 1 - p)
                for t in range(TS):
                    dve.wait_ge(s["out_mm"], e * TS + t + 1)
                    nc.vector.scalar_tensor_tensor(res[:, t, :], ps_y[:, (p + t) % 2, 0:D], rows[:, p, t, D + 1:D + 2],
                                                   rows[:, p, t, 0:D], ALU.mult, ALU.add).then_inc(s["res_done"], 1)
                    dve.wait_ge(s["res_done"], e * TS + t + 1)
                    op = nc.vector.bn_stats(st[:, t, :], res[:, t, :])
                    if t == TS - 1:
                        op.then_inc(s["stats_done"], 1)
                    if t == 0 and not last:
                        w1_lo(e + 1, 1 - p)

            run(dve, step)
            mean_var(E - 1, 1)
            for t in range(TS):
                norm(E - 1, 1, t)

        @block.gpsimd
        def _(pool):
            nc.gpsimd.memset(power[:], -0.5).then_inc(s["setup3"], 1)
            pool.wait_ge(s["setup3"], 1)

            def w2_lo(e, p):
                pool.wait_ge(s["w2_hi"], e + 1)
                nc.gpsimd.tensor_tensor(flat(w2[LO][:, p]), flat(w2_raw), flat(w2[HI][:, p]).bitcast(F32),
                                        ALU.subtract).then_inc(s["w2_lo"], 1)

            w2_lo(0, 0)

            def send(e, p):
                pool.wait_ge(s["var_ready"], e + 1)
                nc.gpsimd.tensor_tensor(ve[:], ve[:], power[:], ALU.pow).then_inc(s["rstd"], 1)
                pool.wait_ge(s["var_ready"], 1)
                pool.wait_ge(s["new_done"], e + 1)
                pool.wait_ge(s["token_done"], e + 1)
                for t in range(TS):
                    nc.gpsimd.indirect_dma_start(
                        out=dram["out"], out_offset=bass.IndirectOffsetOnAxis(ap=token[:, p, t:t + 1], axis=0),
                        in_=new[:, p, t, :], in_offset=None, bounds_check=NT - 1, oob_is_err=False,
                    ).then_inc(sent[p], 16)

            def step(e, p, last=False):
                if not isinstance(e, int) or e > 0:
                    send(e - 1, 1 - p)
                if not last:
                    w2_lo(e + 1, 1 - p)

            run(pool, step)
            send(E - 1, 1)
            pool.wait_ge(sent[0], E // 2 * TS * 16)
            pool.wait_ge(sent[1], E // 2 * TS * 16)


def decoder(nc, dram):
    with ExitStack() as whole:
        def keep(name, shape, dt):
            return whole.enter_context(nc.sbuf_tensor(name, shape, dt))

        def sem(name):
            return whole.enter_context(nc.semaphore(name))

        dram["rows"] = nc.dram_tensor("rows_dram", (E * CAP, ROW), F32, kind="Internal").ap()
        c = {"eye": keep("eye", [P, P], F32), "w": {}}
        c["loads"] = [(c["eye"][:], dram["eye"])]
        c["gated"] = keep("gated", [P, MH, NT], F32)
        c["w1_raw"] = c["gated"][:, 2, 0:NT // 2].rearrange("p (k f) -> p k f", k=KD)
        c["w2_raw"] = c["gated"][:, 2, NT // 2:NT].rearrange("p (k d) -> p k d", d=D)
        c["w1_in"], c["w2_in"] = sem("w1_in"), sem("w2_in")
        with ExitStack() as first_two:
            def hold(name, shape, dt=F32):
                return first_two.enter_context(nc.sbuf_tensor(name, shape, dt))

            def load(name, shape, pattern=None, **kw):
                tile = hold(name + "_sb", shape)
                source = dram[name] if pattern is None else dram[name].rearrange(pattern, **kw)
                c["loads"].append((tile[:], source))
                return tile

            c["s"] = hold("s_all", [P, 4, B])
            c["blank"] = hold("blank", [P, ROW])
            c["hscr"] = nc.dram_tensor("halves_dram", (2, 2, KD, 2 * HD, P // HD, S), F32, kind="Internal").ap()
            for n in "qkvo":
                c["w"][n] = load("w_" + n, [P, KD, D], "(k p) n -> p k n", p=P)
            c["w"]["out"] = load("w_out", [P, MH, D], "(k p) n -> p k n", p=P)
            c["w"]["r"] = load("w_r", [P, KD, E], "(k p) n -> p k n", p=P)
            c["bv_rep"] = load("bv_rep", [P, KD, P], "(k p) n -> p k n", p=P)
            for n, width in (("ones", P), ("mask", 64), ("tri", P), ("kinds", E), ("tokens", NT // P),
                             ("b_out", D), ("b_o", D), ("d_col", MH), ("b_k", KD), ("b_q", KD)):
                c[n] = load(n, [P, width])
            for n in ("loaded", "blank_ready", "rows_blank"):
                c[n] = sem(n)
            for part, before in ((mixer_in, {}), (attend, {"x2b": [P, S // P, D], "r2": [P, S // P, D],
                                                          "twice": [P, 2, S // P, D]})):
                with ExitStack() as own:
                    def tile(name, shape, dt):
                        return own.enter_context(nc.sbuf_tensor(name, shape, dt))

                    def bank(name, shape, dt):
                        return own.enter_context(nc.psum_tensor(name, shape, dt))

                    def flag(name):
                        return own.enter_context(nc.semaphore(name))

                    for name, shape in before.items():
                        c[name] = tile(name, shape, F32)
                    part(nc, tile, bank, flag, c, dram)
        with ExitStack() as own:
            def tile(name, shape, dt):
                return own.enter_context(nc.sbuf_tensor(name, shape, dt))

            def bank(name, shape, dt):
                return own.enter_context(nc.psum_tensor(name, shape, dt))

            def flag(name):
                return own.enter_context(nc.semaphore(name))

            experts(nc, tile, bank, flag, c, dram)


def laid_out(inputs):
    import numpy as np

    def a(name):
        return np.ascontiguousarray(inputs[name])

    def column(v):
        return v.reshape(-1, P).T

    def by_dim(v):
        return v.reshape(v.shape[:-1] + (KD, P // HD, HD)).swapaxes(-1, -2).reshape(v.shape)

    mix, att, ffn = "L0_attn_", "L0_xattn_", "L0_ffn_"
    arrays = {
        "x": a("x").reshape(NT, D), "x_t": a("x").reshape(NT, D).T, "ctx_t": a("ctx_1024").reshape(NT, D).T,
        "w_in": a(mix + "W_in").T, "b_in": column(a(mix + "b_in")),
        "conv_w": a(mix + "conv_w").reshape(MH, P, K).transpose(1, 0, 2), "conv_b": column(a(mix + "conv_b")),
        "w_ssm": np.tile(a(mix + "W_ssm").T, (1, 4)), "b_ssm": np.tile(a(mix + "b_ssm"), 4)[:, None],
        "a_rep": np.tile(a(mix + "A"), (1, 4)), "a_tr": a(mix + "A").T,
        "c_rep": np.tile(a(mix + "Cv"), 4)[:, None], "b_rep": np.tile(a(mix + "Bv"), 4)[:, None],
        "d_col": column(a(mix + "Dv")), "w_out": a(mix + "W_out").T,
        "b_out": np.broadcast_to(a(mix + "b_out"), (P, D)), "b_o": np.broadcast_to(a(att + "bo"), (P, D)),
        "bv_rep": np.broadcast_to(a(att + "bv")[:, None], (D, P)),
        "b_q": column(by_dim(a(att + "bq"))), "b_k": column(by_dim(a(att + "bk"))),
        "w_r": a(ffn + "Wr"), "w1": a(ffn + "W1").reshape(E * D, F), "w2": a(ffn + "W2").reshape(E * F, D),
    }
    for n in "vo":
        arrays["w_" + n] = a(att + "W" + n).T
    for n in "qk":
        arrays["w_" + n] = by_dim(a(att + "W" + n).T)
    one = np.float32
    arrays["eye_rep"] = np.tile(np.eye(NS, dtype=one), (4, 1))
    arrays["eye"] = np.eye(P, dtype=one)
    arrays["ones"] = np.ones((P, P), one)
    arrays["tri"] = np.triu(np.ones((P, P), one))
    arrays["kinds"] = np.tile(np.arange(E, dtype=one), (P, 1))
    arrays["tokens"] = np.arange(NT, dtype=one).reshape(NT // P, P).T
    mask = np.zeros((4, NS, 4, L), one)
    for c4 in range(4):
        mask[c4, :L, c4, :] = np.eye(L, dtype=one)
    arrays["mask"] = mask.reshape(P, 4 * L)
    return {n: np.ascontiguousarray(v) for n, v in arrays.items()}


def kernel(**inputs):
    import numpy as _np
    import concourse.bacc as _bacc
    from concourse import mybir as _mybir
    from concourse.bass_utils import run_bass_kernel_spmd as _run

    nc = _bacc.Bacc("TRN2", target_bir_lowering=False, num_devices=1)
    arrays, dram = {}, {}
    for name, v in laid_out(inputs).items():
        arrays["in_" + name] = v
        dram[name] = nc.dram_tensor("in_" + name, v.shape, _mybir.dt.from_np(v.dtype), kind="ExternalInput").ap()
    dram["out"] = nc.dram_tensor("out_rows", (NT, D), _mybir.dt.from_np(_np.dtype("float32")), kind="ExternalOutput").ap()
    decoder(nc, dram)
    r = _run(nc, [arrays], core_ids=[0])
    return r.results[0]["out_rows"].reshape(B, S, D)
```
